# Optimizing a Trainium2 kernel written in Bass

```python
import numpy as np
import jax
import jax.numpy as jnp

def _softmax(x, axis=-1):
    return jax.nn.softmax(x, axis=axis)

def _gelu(x):
    return jax.nn.gelu(x, approximate=True)

def _silu(x):
    return jax.nn.silu(x)

def _sigmoid(x):
    return jax.nn.sigmoid(x)

def _layernorm(x, axis=-1, eps=1e-05):
    m = jnp.mean(x, axis=axis, keepdims=True)
    v = jnp.var(x, axis=axis, keepdims=True)
    return (x - m) / jnp.sqrt(v + eps)

def _scatter_add(tgt, idx, src, axis=0):
    return tgt.at[idx].add(src)

def _segment_sum(src, seg, n):
    return jax.ops.segment_sum(src, seg, n)
kernel_name = 'mk_early_fusion_embed_d1_tok_img768_r4_cdc8c9'

def setup_inputs(seed: int=0):
    np.random.seed(seed)
    _w = jnp.asarray

    def _rec_inputs():
        import jax
        import jax.numpy as jnp
        _rk = jax.random.key(seed)
        x = -0.000348323 + 0.999952 * jax.random.normal(jax.random.fold_in(_rk, 1), (64, 3, 96, 96), jnp.float32)
        x_txt = jax.random.randint(jax.random.fold_in(_rk, 51), (64, 32), 0, 12564, jnp.int32)
        return (x, x_txt)
    x, x_txt = _rec_inputs()

    def _L0_tok_setup():
        import jax, jax.numpy as jnp
        import numpy as np
        PATCH = 16
        EMBED = 192
        IMG = 96
        CH = 3
        NP_ = (IMG // PATCH) ** 2
        key = jax.random.key(seed)
        k1, k2, k3 = jax.random.split(key, 3)
        x = jax.random.normal(k1, (32, CH, IMG, IMG), dtype=jnp.float32)
        in_feat = PATCH * PATCH * CH
        lim = 1.0 / np.sqrt(in_feat)
        W = jax.random.uniform(k2, (EMBED, in_feat), dtype=jnp.float32, minval=-lim, maxval=lim)
        b = jax.random.uniform(k3, (EMBED,), dtype=jnp.float32, minval=-lim, maxval=lim)
        pos = jnp.zeros((1, NP_, EMBED), dtype=jnp.float32)
        return {'x': x, 'W': W, 'b': b, 'pos': pos}
    _L0_tok_all = _L0_tok_setup()
    _L0_tok_in = {k: v for k, v in _L0_tok_all.items() if k in ('W', 'b', 'pos')}
    del _L0_tok_all

    def _L0_txt_setup():
        import jax, jax.numpy as jnp
        import numpy as np
        VOCAB = 50257
        FRONT = 768
        EMBED = 192
        key = jax.random.key(seed)
        k1, k2, k3, k4, k5, k6 = jax.random.split(key, 6)
        idxs = jax.random.randint(k1, (4, 1024), 0, VOCAB, dtype=jnp.int64 if jax.config.jax_enable_x64 else jnp.int32)
        tok_embed = jax.random.normal(k2, (VOCAB, FRONT), dtype=jnp.float32)
        lim1 = 1.0 / np.sqrt(FRONT)
        W1 = jax.random.uniform(k3, (EMBED, FRONT), minval=-lim1, maxval=lim1, dtype=jnp.float32)
        b1 = jax.random.uniform(k4, (EMBED,), minval=-lim1, maxval=lim1, dtype=jnp.float32)
        lim2 = 1.0 / np.sqrt(EMBED)
        W2 = jax.random.uniform(k5, (EMBED, EMBED), minval=-lim2, maxval=lim2, dtype=jnp.float32)
        b2 = jax.random.uniform(k6, (EMBED,), minval=-lim2, maxval=lim2, dtype=jnp.float32)
        return {'idxs': idxs, 'tok_embed': tok_embed, 'W1': W1, 'b1': b1, 'W2': W2, 'b2': b2}
    _L0_txt_all = _L0_txt_setup()
    _L0_txt_in = {k: v for k, v in _L0_txt_all.items() if k in ('tok_embed', 'W1', 'b1', 'W2', 'b2')}
    del _L0_txt_all

    def _L0_attn_setup():
        import jax, jax.numpy as jnp
        import numpy as np
        NUM_HEADS = 12
        BITS_W = 8
        BITS_A = 8
        BITS_S = 4
        EPS = 1.1920928955078125e-07

        def fq_weight(w):
            qmin, qmax = (-2 ** (BITS_W - 1), 2 ** (BITS_W - 1) - 1)
            mn = jnp.minimum(w.min(axis=1, keepdims=True), 0.0)
            mx = jnp.maximum(w.max(axis=1, keepdims=True), 0.0)
            scale = jnp.maximum((mx - mn) / float(qmax - qmin), EPS)
            zp = qmin - jnp.round(mn / scale)
            wq = jnp.clip(jnp.round(w / scale) + zp, qmin, qmax)
            return (wq - zp) * scale

        def fq_act(x):
            qmin, qmax = (-2 ** (BITS_A - 1), 2 ** (BITS_A - 1) - 1)
            mn = jnp.minimum(x.min(), 0.0)
            mx = jnp.maximum(x.max(), 0.0)
            scale = jnp.maximum((mx - mn) / float(qmax - qmin), EPS)
            zp = qmin - jnp.round(mn / scale)
            xq = jnp.clip(jnp.round(x / scale) + zp, qmin, qmax)
            return ((xq - zp) * scale, scale)

        def int_log_softmax(x, scale):
            x_int = x / scale
            x_int = x_int - x_int.max(axis=-1, keepdims=True)
            x0, n = (-0.6931, 30)
            x0_int = jnp.floor(x0 / scale)
            x_int = jnp.maximum(x_int, n * x0_int)
            q = jnp.floor(x_int / x0_int)
            r = x_int - x0_int * q
            c0 = 0.35815147
            b_int = jnp.floor(0.96963238 / c0 / scale)
            c_int = jnp.floor(1.0 / c0 / (scale * scale))
            z = r * (r + b_int) + c_int
            exp_int = jnp.clip(jnp.floor(z * jnp.exp2(n - q)), 0.0, None)
            exp_sum = exp_int.sum(axis=-1, keepdims=True)
            sm = jnp.round(exp_sum / exp_int)
            big = jnp.floor(jnp.log2(sm))
            big = jnp.where(sm - jnp.exp2(big) >= jnp.exp2(big - 1.0), big + 1.0, big)
            mask = big >= float(2 ** BITS_S)
            qlog = jnp.clip(big, 0.0, float(2 ** BITS_S - 1))
            return jnp.where(mask, 0.0, jnp.exp2(-qlog))
        key = jax.random.key(seed)
        ks = jax.random.split(key, 5)
        B, N, C = (16, 577, 192)
        return {'x': jax.random.normal(ks[0], (B, N, C), jnp.float32), 'w_qkv': jax.random.normal(ks[1], (3 * C, C), jnp.float32) * 0.02, 'b_qkv': jax.random.normal(ks[2], (3 * C,), jnp.float32) * 0.02, 'w_proj': jax.random.normal(ks[3], (C, C), jnp.float32) * 0.02, 'b_proj': jax.random.normal(ks[4], (C,), jnp.float32) * 0.02}
    _L0_attn_all = _L0_attn_setup()
    _L0_attn_in = {k: v for k, v in _L0_attn_all.items() if k in ('w_qkv', 'b_qkv', 'w_proj', 'b_proj')}
    del _L0_attn_all

    def _L0_ffn_setup():
        import jax, jax.numpy as jnp
        import numpy as np
        B, T, C = (4, 512, 192)
        E, K = (8, 2)

        def _mlp(x, wfc, wproj):
            h = jnp.square(jax.nn.relu(x @ wfc))
            return h @ wproj
        key = jax.random.key(seed)
        ks = jax.random.split(key, 6)
        s = 0.02
        return {'x': jax.random.normal(ks[0], (B, T, C), jnp.float32), 'w_fc_sh': jax.random.normal(ks[1], (C, C), jnp.float32) * s, 'w_proj_sh': jax.random.normal(ks[2], (C, C), jnp.float32) * s, 'w1': jax.random.normal(ks[3], (E, C, C), jnp.float32) * s, 'w2': jax.random.normal(ks[4], (E, C, C), jnp.float32) * s, 'router_w': jax.random.normal(ks[5], (E, C), jnp.float32) * s, 'balance_bias': jnp.zeros((E,), jnp.float32)}
    _L0_ffn_all = _L0_ffn_setup()
    _L0_ffn_in = {k: v for k, v in _L0_ffn_all.items() if k in ('w_fc_sh', 'w_proj_sh', 'w1', 'w2', 'router_w', 'balance_bias')}
    del _L0_ffn_all
    return {'x': x, 'x_txt': x_txt, 'L0_tok_W': _L0_tok_in['W'], 'L0_tok_b': _L0_tok_in['b'], 'L0_tok_pos': _L0_tok_in['pos'], 'L0_txt_tok_embed': _L0_txt_in['tok_embed'], 'L0_txt_W1': _L0_txt_in['W1'], 'L0_txt_b1': _L0_txt_in['b1'], 'L0_txt_W2': _L0_txt_in['W2'], 'L0_txt_b2': _L0_txt_in['b2'], 'L0_attn_w_qkv': _L0_attn_in['w_qkv'], 'L0_attn_b_qkv': _L0_attn_in['b_qkv'], 'L0_attn_w_proj': _L0_attn_in['w_proj'], 'L0_attn_b_proj': _L0_attn_in['b_proj'], 'L0_ffn_w_fc_sh': _L0_ffn_in['w_fc_sh'], 'L0_ffn_w_proj_sh': _L0_ffn_in['w_proj_sh'], 'L0_ffn_w1': _L0_ffn_in['w1'], 'L0_ffn_w2': _L0_ffn_in['w2'], 'L0_ffn_router_w': _L0_ffn_in['router_w'], 'L0_ffn_balance_bias': _L0_ffn_in['balance_bias']}

def reference(x, x_txt, L0_tok_W, L0_tok_b, L0_tok_pos, L0_txt_tok_embed, L0_txt_W1, L0_txt_b1, L0_txt_W2, L0_txt_b2, L0_attn_w_qkv, L0_attn_b_qkv, L0_attn_w_proj, L0_attn_b_proj, L0_ffn_w_fc_sh, L0_ffn_w_proj_sh, L0_ffn_w1, L0_ffn_w2, L0_ffn_router_w, L0_ffn_balance_bias):
    import jax
    import jax.numpy as jnp

    def _L0_tok_ref(x, W, b, pos):
        import jax, jax.numpy as jnp
        import numpy as np
        PATCH = 16
        EMBED = 192
        IMG = 96
        CH = 3
        NP_ = (IMG // PATCH) ** 2
        B, C, H, Wd = x.shape
        hp, wp = (H // PATCH, Wd // PATCH)
        patches = x.reshape(B, C, hp, PATCH, wp, PATCH)
        patches = patches.transpose(0, 2, 4, 1, 3, 5).reshape(B, hp * wp, C * PATCH * PATCH)
        out = jnp.einsum('bnf,ef->bne', patches, W) + b + pos
        return out

    def _L0_txt_ref(idxs, tok_embed, W1, b1, W2, b2):
        import jax, jax.numpy as jnp
        import numpy as np
        VOCAB = 50257
        FRONT = 768
        EMBED = 192
        x = tok_embed[idxs]
        x = jnp.einsum('bsf,ef->bse', x, W1) + b1
        x = jax.nn.gelu(x, approximate=False)
        x = jnp.einsum('bse,oe->bso', x, W2) + b2
        return x

    def _L0_attn_ref(x, w_qkv, b_qkv, w_proj, b_proj):
        import jax, jax.numpy as jnp
        import numpy as np
        NUM_HEADS = 12
        BITS_W = 8
        BITS_A = 8
        BITS_S = 4
        EPS = 1.1920928955078125e-07

        def fq_weight(w):
            qmin, qmax = (-2 ** (BITS_W - 1), 2 ** (BITS_W - 1) - 1)
            mn = jnp.minimum(w.min(axis=1, keepdims=True), 0.0)
            mx = jnp.maximum(w.max(axis=1, keepdims=True), 0.0)
            scale = jnp.maximum((mx - mn) / float(qmax - qmin), EPS)
            zp = qmin - jnp.round(mn / scale)
            wq = jnp.clip(jnp.round(w / scale) + zp, qmin, qmax)
            return (wq - zp) * scale

        def fq_act(x):
            qmin, qmax = (-2 ** (BITS_A - 1), 2 ** (BITS_A - 1) - 1)
            mn = jnp.minimum(x.min(), 0.0)
            mx = jnp.maximum(x.max(), 0.0)
            scale = jnp.maximum((mx - mn) / float(qmax - qmin), EPS)
            zp = qmin - jnp.round(mn / scale)
            xq = jnp.clip(jnp.round(x / scale) + zp, qmin, qmax)
            return ((xq - zp) * scale, scale)

        def int_log_softmax(x, scale):
            x_int = x / scale
            x_int = x_int - x_int.max(axis=-1, keepdims=True)
            x0, n = (-0.6931, 30)
            x0_int = jnp.floor(x0 / scale)
            x_int = jnp.maximum(x_int, n * x0_int)
            q = jnp.floor(x_int / x0_int)
            r = x_int - x0_int * q
            c0 = 0.35815147
            b_int = jnp.floor(0.96963238 / c0 / scale)
            c_int = jnp.floor(1.0 / c0 / (scale * scale))
            z = r * (r + b_int) + c_int
            exp_int = jnp.clip(jnp.floor(z * jnp.exp2(n - q)), 0.0, None)
            exp_sum = exp_int.sum(axis=-1, keepdims=True)
            sm = jnp.round(exp_sum / exp_int)
            big = jnp.floor(jnp.log2(sm))
            big = jnp.where(sm - jnp.exp2(big) >= jnp.exp2(big - 1.0), big + 1.0, big)
            mask = big >= float(2 ** BITS_S)
            qlog = jnp.clip(big, 0.0, float(2 ** BITS_S - 1))
            return jnp.where(mask, 0.0, jnp.exp2(-qlog))
        B, N, C = x.shape
        H = NUM_HEADS
        hd = C // H
        attn_scale = hd ** (-0.5)
        y = x @ fq_weight(w_qkv).T + b_qkv
        y, _ = fq_act(y)
        qkv = y.reshape(B, N, 3, H, hd).transpose(2, 0, 3, 1, 4)
        q, k, v = (qkv[0], qkv[1], qkv[2])
        attn = jnp.einsum('bhnd,bhmd->bhnm', q, k) * attn_scale
        attn, s_attn = fq_act(attn)
        attn = int_log_softmax(attn, s_attn)
        o = jnp.einsum('bhnm,bhmd->bhnd', attn, v)
        o = o.transpose(0, 2, 1, 3).reshape(B, N, C)
        o, _ = fq_act(o)
        o = o @ fq_weight(w_proj).T + b_proj
        o, _ = fq_act(o)
        return o

    def _L0_ffn_ref(x, w_fc_sh, w_proj_sh, w1, w2, router_w, balance_bias):
        import jax, jax.numpy as jnp
        import numpy as np
        B, T, C = (4, 512, 192)
        E, K = (8, 2)

        def _mlp(x, wfc, wproj):
            h = jnp.square(jax.nn.relu(x @ wfc))
            return h @ wproj
        Bx, Tx, Cx = x.shape
        shared = _mlp(x, w_fc_sh, w_proj_sh)
        xf = x.reshape(-1, Cx)
        logits = xf.astype(jnp.float32) @ router_w.T
        scores = jax.nn.sigmoid(logits)
        _, idx = jax.lax.top_k(scores + balance_bias, K)
        tw = jnp.take_along_axis(scores, idx, axis=-1)
        tw = tw / (tw.sum(-1, keepdims=True) + 1e-20)
        combine = (jax.nn.one_hot(idx, E, dtype=tw.dtype) * tw[..., None]).sum(1)
        h = jnp.square(jax.nn.relu(jnp.einsum('nc,ech->neh', xf, w1)))
        y = jnp.einsum('neh,ehc->nec', h, w2)
        routed = jnp.einsum('nec,ne->nc', y, combine)
        return shared + routed.reshape(Bx, Tx, Cx)
    h = _L0_tok_ref(x, L0_tok_W, L0_tok_b, L0_tok_pos)
    h = jnp.concatenate([h, _L0_txt_ref(x_txt, L0_txt_tok_embed, L0_txt_W1, L0_txt_b1, L0_txt_W2, L0_txt_b2)], axis=1)
    h = h + _L0_attn_ref(_layernorm(h, axis=-1), L0_attn_w_qkv, L0_attn_b_qkv, L0_attn_w_proj, L0_attn_b_proj)
    h = h + _L0_ffn_ref(_layernorm(h, axis=-1), L0_ffn_w_fc_sh, L0_ffn_w_proj_sh, L0_ffn_w1, L0_ffn_w2, L0_ffn_router_w, L0_ffn_balance_bias)
    return h

_drawn_inputs = setup_inputs


def setup_inputs(seed=0):
    import zlib

    import numpy as np

    out = dict(_drawn_inputs(seed))
    spreads = {'L0_tok_pos': (0.0, 0.1), 'L0_ffn_balance_bias': (0.0, 0.1)}
    factors = {'L0_txt_b1': 4.728, 'L0_attn_b_qkv': 4.367}
    for name, (base, spread) in spreads.items():
        noise = np.random.default_rng([zlib.crc32(name.encode()), seed]).standard_normal(out[name].shape)
        drawn = base * np.exp(spread * noise) if base else spread * noise
        out[name] = jnp.asarray(drawn.astype(out[name].dtype))
    for name, factor in factors.items():
        out[name] = (out[name] * factor).astype(out[name].dtype)
    return out
```

```python
from contextlib import ExitStack

import concourse.bass as bass
from concourse import mybir

F32 = mybir.dt.float32
F16 = mybir.dt.float16
BF16 = mybir.dt.bfloat16
I16 = mybir.dt.int16
I32 = mybir.dt.int32
ALU = mybir.AluOpType
ACT = mybir.ActivationFunctionType
X = mybir.AxisListType.X
XY = mybir.AxisListType.XY
RMAX = bass.bass_isa.ReduceOp.max

P = 128
B = 64
C = 192
C1 = C - P
GRID = 6
PATCH = 16
NI = GRID * GRID
NT = 32
N = NI + NT
T = B * N
TT = T // P
H = 12
HD = C // H
MW = 6356
PAIRS = H // 2
NQ = 64
NL = N - NQ
FRONT = 768
KC = FRONT // P
SLOTS = PAIRS + 1
QKW = 3 * NQ + N
E = 8
U = (E + 1) * C
UC = (U + P - 1) // P
EPS_LN = 1e-5
EPS_Q = 1.1920928955078125e-07
MAGIC = 12582912.0
H16 = 1024.0
C0 = 0.35815147


def pipeline(eng, stages, groups):
    last = max(lag for _, lag in stages)
    lead = last + 2 + (groups - last) % 2

    def step(s):
        for fn, lag in stages:
            if 0 <= s - lag < groups:
                fn(s - lag, (s - lag) % 2, (s - lag) // 2)

    for s in range(lead):
        step(s)
    with eng.Fori(0, (groups - lead) // 2) as i:
        for p in (0, 1):
            for fn, lag in stages:
                g = lead + p - lag
                fn(i * 2 + g, g % 2, i + g // 2)
    for s in range(groups, groups + last):
        step(s)


def program(nc, x, x_txt, tok_W, tok_b, tok_pos, embed, W1, b1, W2, b2, w_qkv, b_qkv, w_proj, b_proj,
            w_fc_sh, w_proj_sh, w1, w2, router_w, balance_bias, ident_c, headmask_c, select_c, lower_c, out):
    ctx = ExitStack()
    with ctx:
        def sb(name, shape, dt=F32):
            return ctx.enter_context(nc.sbuf_tensor(name, shape, dt))

        sems = {}

        def sem(name):
            if name not in sems:
                sems[name] = ctx.enter_context(nc.semaphore(name))
            return sems[name]

        def wait(eng, name, value):
            if isinstance(value, int) and value <= 0:
                return
            eng.wait_ge(sem(name), value)

        counts = {}

        def chain(eng, name, ins):
            counts[name] = counts.get(name, 0) + 1
            ins.then_inc(sem(name), 1)
            eng.wait_ge(sem(name), counts[name])

        barriers = {}

        def barrier(eng, name):
            n = barriers.get(name, 0) + 1
            barriers[name] = n
            eng.drain().then_inc(sem("all_engines_done"), 1)
            eng.wait_ge(sem("all_engines_done"), 5 * n)

        h_dram = nc.dram_tensor("h_rows", [T, C], F32, kind="Internal").ap()

        R0 = sb("R0", [P, 4 * T])
        R1 = sb("R1", [P, B * C])
        R2 = sb("R2", [P, 16640])
        M = sb("M", [P, MW])
        ps = ctx.enter_context(nc.psum_tensor("ps", [P, 8, 512], F32))
        used = [0]

        def misc(words, dt=F32, rows=P):
            a = used[0]
            used[0] += words
            assert used[0] <= MW, used[0]
            v = M[0:rows, a:a + words]
            return v if dt == F32 else v.bitcast(dt)

        ident = sb("ident", [P, P])
        ident_b = sb("ident_b", [P, P], BF16)
        headmask = sb("headmask", [P, 2, 16])
        parmask = sb("parmask", [P, 2])
        sc = sb("sc", [P, 64])
        biases = sb("biases", [P, 16])
        ones = sb("ones", [P, P])

        ximg = R0[0:96, 0:2 * 4608].rearrange("p (a c f) -> p a c f", a=2, c=3)
        emb = R0[:, 9216:9216 + 4 * FRONT].rearrange("p (a f) -> p a f", a=4)
        patT = R0[:, 12288:12288 + 2 * 768].rearrange("p (a f) -> p a f", a=2)
        hstage = R1[0:96, 0:2 * 1152].rearrange("p (a w c) -> p a w c", a=2, w=GRID)
        tstage = R1[:, 2304:2304 + 2 * C].rearrange("p (a c) -> p a c", a=2)
        zT = R1[0:96, 2688:2688 + 4 * P].rearrange("p (a m t) -> p a m t", a=2, m=2)
        posb = R1[0:96, 3200:3200 + GRID * C].rearrange("p (w c) -> p w c", w=GRID)
        brow = R1[:, 4352:4352 + 3 * C].rearrange("p (k c) -> p k c", k=3)
        idx = R1[:, 4928:4944].bitcast(I32)
        w_rows = R1[0:96, 5000:5000 + 2 * 2 * FRONT].rearrange("p (a j f) -> p a j f", a=2, j=2)
        w2_rows = R1[0:96, 8072:8072 + 2 * C].rearrange("p (j f) -> p j f", j=2)
        tokT = R2[:, 0:KC * C].rearrange("p (k c) -> p k c", k=KC)
        w1T = R2[:, 1152:1152 + KC * C].rearrange("p (k c) -> p k c", k=KC)
        xp = R2[0:96, 6000:6000 + 2 * 4608].rearrange("p (a c f) -> p a c f", a=2, c=3)
        w2T = R2[0:96, 2304:2304 + 2 * C].rearrange("p (m c) -> p m c", m=2)

        QROWS = [(0, P), (P, C1), (C, P), (C + P, C1), (2 * C, 96), (2 * C + 96, 96), (3 * C, 96), (3 * C + 96, 96)]
        wq_rows = R2[:, 2700:2700 + 8 * C].rearrange("p (j c) -> p j c", j=8)
        wqT0 = misc(3 * C)
        wqT1 = misc(3 * C, rows=C1)
        wpb0 = misc(C // 2, BF16)
        wpb1 = misc(C // 2, BF16, rows=C1)
        wscale = misc(8)
        wtmp = R2[:, 4300:4300 + 8 * C].rearrange("p (j c) -> p j c", j=8)
        prow = misc(C)
        bprow = misc(C)
        bvrow = misc(C)

        yq = [R0[:, 0:T], R0[0:C1, T:2 * T]]
        yk = [R0[:, 2 * T:3 * T], R0[0:C1, 3 * T:4 * T]]
        yv = R1[0:N, :].rearrange("p (b c) -> p b c", b=B)
        hb = R2[0:N, 0:B * C].rearrange("p (b c) -> p b c", b=B)
        xn = R2[0:N, B * C:B * C + 2 * 4 * C].rearrange("p (a b c) -> p a b c", a=2, b=4)
        xT0 = R2[:, 13824:13824 + 2 * 272].rearrange("p (a t) -> p a t", a=2)
        xT1 = R2[0:C1, 14368:14368 + 2 * 272].rearrange("p (a t) -> p a t", a=2)
        bst = R2[0:N, 14912:14912 + 6 * 2].rearrange("p (a s) -> p a s", a=2)
        mv = R2[0:N, 14924:14924 + 2 * B].rearrange("p (b s) -> p b s", s=2)
        rs = R2[0:N, 15052:15052 + 3 * B].rearrange("p (k b) -> p k b", k=3)

        QK0 = R2[:, 0:B * QKW // 2].bitcast(BF16).rearrange("p (b w) -> p b w", b=B)
        QK1 = R2[0:C1, B * QKW // 2:B * QKW].bitcast(BF16).rearrange("p (b w) -> p b w", b=B)
        VQ = R0[0:N, 0:B * C // 2].bitcast(BF16).rearrange("p (b c) -> p b c", b=B)
        qt = misc(2 * 8 * N).rearrange("p (a t) -> p a t", a=2)

        CW = 2 * SLOTS * N
        st0 = misc(2 * QKW, BF16).rearrange("p (a b w) -> p a b w", a=2, b=2)
        st1 = misc(2 * QKW, BF16, rows=C1).rearrange("p (a b w) -> p a b w", a=2, b=2)
        stv = misc(2 * 2 * C, BF16, rows=N).rearrange("p (a b h c) -> p a b h c", a=2, b=2, h=2)
        rowmax = misc(32 * 2 * SLOTS).rearrange("p (g s) -> p g s", g=32)
        gmin = misc(64)
        rmq = misc(32 * SLOTS, F16).rearrange("p (g s) -> p g s", g=32)
        oT = [R1[:, 0:T], R1[0:C1, T:2 * T]]
        w0 = [B * C // 2]

        def r0(words, dt=F32):
            a = w0[0]
            w0[0] += words
            assert w0[0] <= 4 * T
            v = R0[:, a:a + words]
            return v if dt == F32 else v.bitcast(dt)

        w1_ = [2 * T]

        def r1(words, dt=F32):
            a = w1_[0]
            w1_[0] += words
            assert w1_[0] <= B * C
            v = R1[:, a:a + words]
            return v if dt == F32 else v.bitcast(dt)

        def slots(v):
            return v.rearrange("p (s k) -> p s k", k=N)

        Dq = [slots(r0(CW // 2, F16)) for _ in range(2)]
        Qq = [slots(r0(CW // 2, F16)) for _ in range(2)]
        PW = [slots(r0(CW // 2, I16)) for _ in range(2)]
        sq = [slots(r0(CW)) for _ in range(2)]
        wv = [slots(r1(CW)) for _ in range(2)]
        L = [slots(r0(CW)) for _ in range(2)]
        yb = [slots(r1(CW // 2, F16)) for _ in range(2)]
        Pb = [slots(r0(CW // 2, BF16)) for _ in range(2)]
        PT = [r0(SLOTS * P, BF16)[0:N].rearrange("p (b s q) -> p b s q", b=2, s=SLOTS) for _ in range(2)]
        S = misc(3 * 4 * SLOTS).rearrange("p (a k s) -> p a k s", a=2, k=3)
        top = [slots(r0(CW // 2, BF16)) for _ in range(2)]

        def score_slot(b, j):
            if j == PAIRS:
                return 2 + b, 2, 8 + 3 * b + 2
            r = j % 4
            if r < 2:
                k = 2 * b + j // 4
                return r, k, 4 * r + k
            return r, b, 8 + 3 * (r - 2) + b

        PARTS = [(0, 4, 0), (2, 3, 8)]

        def score_part(base, part):
            bank, k, _ = PARTS[part]
            return ps[:, base + bank:base + bank + 2, 0:k * N].rearrange("p a (s k) -> p a s k", k=N)

        pPT = ps[0:N, 4:6, 0:SLOTS * P // 2].bitcast(BF16).rearrange("p b (s q) -> p b s q", s=SLOTS)
        pO = [ps[:, 6, 0:4 * N].rearrange("p (b c t) -> p b c t", b=2, c=2),
              ps[:, 7, 0:4 * N].rearrange("p (b c t) -> p b c t", b=2, c=2)]

        oq = [R0[:, 0:T // 2].bitcast(BF16), R0[0:C1, T // 2:T].bitcast(BF16)]
        y2 = R0[:, T:T + TT * C].rearrange("p (i c) -> p i c", i=TT)
        hf = R0[:, T + TT * C:T + 2 * TT * C].rearrange("p (i c) -> p i c", i=TT)
        xn2 = R1[:, 0:TT * C].rearrange("p (i c) -> p i c", i=TT)
        CT = R1[0:32, 6528:6528 + T // 2].bitcast(BF16)
        hr = R1[:, 8704:8704 + 512].rearrange("p (a t) -> p a t", a=2)
        hc = R1[:, 9216:9216 + 512].rearrange("p (a t) -> p a t", a=2)
        hh = R1[:, 9728:9728 + 512].rearrange("p (a t) -> p a t", a=2)
        ost = R1[:, 10240:10240 + 2 * 2 * C].rearrange("p (a i c) -> p a i c", a=2, i=2)
        sel_b = R1[0:32, 11008:11008 + UC * P // 2].bitcast(BF16)
        X0 = R2[:, 0:T]
        X1 = R2[0:C1, T:2 * T]
        w1a = R2[:, 8704:8704 + U]
        w1b = R2[0:C1, 8704 + U:8704 + 2 * U]
        w2a = R2[:, 12160:12160 + UC * C].rearrange("p (m c) -> p m c", m=UC)
        mv2 = R2[:, 14848:14848 + 2 * TT].rearrange("p (i s) -> p i s", s=2)
        rs2 = R2[:, 14920:14920 + 3 * TT].rearrange("p (k i) -> p k i", k=3)
        bst2 = R2[:, 15024:15036].rearrange("p (a s) -> p a s", a=2)
        rwT = R2[:, 15040:15056].rearrange("p (k e) -> p k e", k=2)
        rw_rows = R2[0:E, 15060:15060 + C]
        bbrow = R2[:, 15260:15268]
        scr = [R2[:, 15280 + 272 * k:15280 + 272 * (k + 1)].rearrange("p (i e) -> p i e", e=E) for k in range(4)]
        cmp_a = R0[:, T:T + TT * E * E].rearrange("p (i e f) -> p i e f", e=E, f=E)
        cmp_b = R0[:, T + TT * E * E:T + 2 * TT * E * E].rearrange("p (i e f) -> p i e f", e=E, f=E)
        lower = R0[:, T + 2 * TT * E * E:T + 2 * TT * E * E + E * E]
        sel_w = R0[0:32, T + 2 * TT * E * E + 64:T + 2 * TT * E * E + 64 + UC * P]
        xs0 = R0[:, 0:512].rearrange("p (a t) -> p a t", a=2)
        xs1 = R0[0:C1, 512:1024].rearrange("p (a t) -> p a t", a=2)
        cts = R0[0:32, 1024:1280].bitcast(BF16).rearrange("p (a t) -> p a t", a=2)
        C3 = misc(TT * 16, BF16).rearrange("p (i e) -> p i e", i=TT)
        csum = misc(2 * TT).rearrange("p (k i) -> p k i", k=2)

        turns = []

        def turn(pieces, rows, cols, dst):
            turns.append((pieces, rows, cols, dst))

        for a, dst in ((0, tokT), (1, w1T)):
            for k in range(KC):
                turn([(w_rows[:, a, j, k * P:(k + 1) * P], 96, j * 96) for j in range(2)], P, C, dst[:, k, :])
        for m in range(2):
            turn([(w2_rows[:, j, m * 96:(m + 1) * 96], 96, j * 96) for j in range(2)], 96, C, w2T[:, m, :])
        for j, (o, m) in enumerate(QROWS):
            d0, d1, c = (wqT0, wqT1, o) if j < 6 else (wpb0, wpb1, o - 3 * C)
            turn([(wq_rows[0:m, j, 0:P], m, 0)], P, m, d0[:, c:c + m])
            turn([(wq_rows[0:m, j, P:C], m, 0)], C1, m, d1[:, c:c + m])
        for j in (6, 7):
            turn([(None, j, 0)], P, 96, prow[:, (j - 6) * 96:(j - 5) * 96])
        wready = []

        jobs3 = []

        def job(src, scale, shape, dst, rows):
            t = qt[0:rows, len(jobs3) % 2, 0:shape[0] * shape[1]].rearrange("p (b c) -> p b c", b=shape[0])
            jobs3.append((src, scale, t, dst, rows))

        block = ctx.enter_context(nc.Block())

        (Q_MX, Q_NMN, Q_R, Q_INV, Q_CAPM, Q_EV, Q_OD, Q_S, A_MX, A_NMN, A_S, A_INV, A_KK, A_NKK, A_CAP, A_IS,
         A_A, A_IA, A_BH, A_K0, A_CL, A_CB, A_NA, A_SB, O_MX, O_NMN, O_S, O_INV, O_CAPM, O_SC, Y_MX, Y_NMN, Y_S,
         Y_INV, Y_CAPM, T0, T1, T2, G0, G1, A_M16, A_B, A_C, A_K1, A_PB) = range(45)

        for ysrc, kk, QK, rows in ((yq[0], yk[0], QK0, P), (yq[1], yk[1], QK1, C1)):
            qv = ysrc.rearrange("p (b n) -> p b n", n=N)
            kv = kk.rearrange("p (b n) -> p b n", n=N)
            for c in range(8):
                bs = slice(8 * c, 8 * c + 8)
                job(qv[:, bs, 0:NQ], Q_EV, (8, NQ), QK[:, bs, 0:NQ], rows)
                job(qv[:, bs, 0:NQ], Q_OD, (8, NQ), QK[:, bs, NQ:2 * NQ], rows)
                job(kv[:, bs, :], Q_INV, (8, N), QK[:, bs, 3 * NQ:QKW], rows)
            job(qv[:, :, NQ:N], Q_INV, (B, NL), None, rows)
        for b in range(0, B, 2):
            job(yv[:, b:b + 2, :], Q_INV, (2, C), VQ[:, b:b + 2, :], N)

        def s1(k, rows=P):
            return sc[0:rows, k:k + 1]

        @block.sync
        def _(sp):
            sp.dma_start(ident[:, :], ident_c).then_inc(sem("consts"), 16)
            sp.dma_start(headmask[:, :, :], headmask_c[:, 0:32].rearrange("p (k h) -> p k h", k=2)).then_inc(sem("consts"), 16)
            sp.dma_start(parmask[:, :], headmask_c[:, 32:34]).then_inc(sem("consts"), 16)
            sp.dma_start(w_rows[:, 0], tok_W.rearrange("(j p) f -> p j f", p=96)).then_inc(sem("w_rows"), 16)
            sp.dma_start(w_rows[:, 1], W1.rearrange("(j p) f -> p j f", p=96)).then_inc(sem("w_rows"), 16)
            sp.dma_start(w2_rows[:, :, :], W2.rearrange("(j p) f -> p j f", p=96)).then_inc(sem("w_rows"), 16)
            for j, (o, m) in enumerate(QROWS):
                src = w_qkv[o:o + m, :] if o < 3 * C else w_proj[o - 3 * C:o - 3 * C + m, :]
                sp.dma_start(wq_rows[0:m, j, :], src).then_inc(sem("wq_rows"), 16)
            for b in range(16):
                sp.dma_start(posb[GRID * b:GRID * (b + 1), :, :],
                             tok_pos.rearrange("o (h w) c -> (o h) w c", w=GRID)).then_inc(sem("bias_rows"), 16)
            sp.dma_start(brow[:, 0, :], tok_b.partition_broadcast(P)).then_inc(sem("bias_rows"), 16)
            sp.dma_start(brow[:, 1, :], b2.partition_broadcast(P)).then_inc(sem("bias_rows"), 16)
            sp.dma_start(bprow, b_proj.partition_broadcast(P)).then_inc(sem("bias_rows"), 16)
            sp.dma_start(bvrow, b_qkv[2 * C:3 * C].partition_broadcast(P)).then_inc(sem("bias_rows"), 16)
            sp.dma_start(biases[0:96, 0:2], b1.rearrange("(j p) -> p j", p=96), allow_slow_non_contiguous=True).then_inc(sem("bias_rows"), 16)
            for j in range(4):
                o, m = QROWS[j]
                sp.dma_start(biases[0:m, 2 + j:3 + j], b_qkv[o:o + m].rearrange("(p a) -> p a", a=1),
                             allow_slow_non_contiguous=True).then_inc(sem("bias_rows"), 16)
            xv = x.rearrange("b c (h r) w -> c b h (r w)", h=GRID)

            for q in range(4):
                if q >= 2:
                    sp.wait_ge(sem("by_patch_a"), q - 1)
                    sp.wait_ge(sem("by_patch_b"), q - 1)
                for c in range(3):
                    sp.dma_start(ximg[:, q % 2, c, :], xv[c, 16 * q:16 * q + 16]).then_inc(sem(f"ximg{q % 2}"), 16)
            hv = h_dram.rearrange("(b n) c -> b n c", n=N)
            for q in range(4):
                sp.wait_ge(sem("img_h"), GRID * (q + 1))
                sp.dma_start(hv[16 * q:16 * q + 16, 0:NI, :].rearrange("b (h w) c -> b h (w c)", w=GRID),
                             hstage[:, q % 2].rearrange("p w c -> p (w c)")).then_inc(sem(f"h_stored{q % 2}"), 16)
            for t in range(16):
                sp.wait_ge(sem("txt_h"), t + 1)
                sp.dma_start(hv[4 * t:4 * t + 4, NI:N, :], tstage[:, t % 2, :]).then_inc(sem(f"t_stored{t % 2}"), 16)
            for a in range(2):
                sp.wait_ge(sem(f"h_stored{a}"), 32)
                sp.wait_ge(sem(f"t_stored{a}"), 128)
            barrier(sp, "sp")
            for q in range(4):
                sp.dma_start(hb[:, 16 * q:16 * q + 16, :],
                             hv[16 * q:16 * q + 16].rearrange("b n c -> n b c")).then_inc(sem(f"hb{q}"), 16)
            barrier(sp, "sp")
            barrier(sp, "sp")

            def load_qk(phase):
                def fn(g, par, half):
                    wait(sp, "scored", 32 * phase + g - 1)
                    b = bass.ds(g * 2, 2)
                    sp.dma_start(st0[:, par], QK0[:, b, :]).then_inc(sem(f"st_qk{par}"), 16)
                    sp.dma_start(st1[:, par], QK1[:, b, :]).then_inc(sem(f"st_qk{par}"), 16)
                return fn

            pipeline(sp, [(load_qk(0), 0)], 32)
            barrier(sp, "sp")
            pipeline(sp, [(load_qk(1), 0)], 32)
            barrier(sp, "sp")
            sp.dma_start(hf, h_dram.rearrange("(i p) c -> p i c", p=P)).then_inc(sem("hf"), 16)
            for e in range(E + 1):
                src = w1[e] if e < E else w_fc_sh
                sp.dma_start(w1a[:, e * C:(e + 1) * C], src[0:P, :]).then_inc(sem("ffn_w"), 16)
                sp.dma_start(w1b[:, e * C:(e + 1) * C], src[P:C, :]).then_inc(sem("ffn_w"), 16)
            sp.dma_start(w2a[:, 0:UC - 2, :], w2.rearrange("e h c -> (e h) c").rearrange("(m p) c -> p m c", p=P)).then_inc(sem("ffn_w"), 16)
            sp.dma_start(w2a[:, UC - 2, :], w_proj_sh[0:P, :]).then_inc(sem("ffn_w"), 16)
            sp.dma_start(w2a[0:C1, UC - 1, :], w_proj_sh[P:C, :]).then_inc(sem("ffn_w"), 16)
            sp.dma_start(rw_rows, router_w).then_inc(sem("ffn_w"), 16)
            sp.dma_start(bbrow, balance_bias.partition_broadcast(P)).then_inc(sem("ffn_w"), 16)
            barrier(sp, "sp")
            sp.dma_start(lower, lower_c.partition_broadcast(P)).then_inc(sem("ffn_c"), 16)
            sp.dma_start(sel_w, select_c).then_inc(sem("ffn_c"), 16)
            barrier(sp, "sp")
            ov = out.rearrange("b n c -> (b n) c").rearrange("(i p) c -> p i c", p=P)

            def store(g, par, half):
                sp.wait_ge(sem("out_ready"), g + 1)
                sp.dma_start(ov[:, bass.ds(g * 2, 2), :], ost[:, par]).then_inc(sem(f"stored{par}"), 16)

            def load_x(g, par, half):
                wait(sp, "h_used", (g - 1) * UC)
                t = bass.ds(g * 256, 256)
                sp.dma_start(xs0[:, par], X0[:, t]).then_inc(sem(f"xs{par}"), 16)
                sp.dma_start(xs1[:, par], X1[:, t]).then_inc(sem(f"xs{par}"), 16)
                sp.dma_start(cts[:, par], CT[:, t]).then_inc(sem(f"xs{par}"), 16)

            pipeline(sp, [(load_x, 0), (store, 2)], TT // 2)
            sp.wait_ge(sem("stored0"), 16 * 9)
            sp.wait_ge(sem("stored1"), 16 * 8)

        @block.gpsimd
        def _(pool):
            pool.dma_start(idx, x_txt.rearrange("b s -> (b s)").rearrange("(t p) -> p t", p=P),
                           allow_slow_non_contiguous=True).then_inc(sem("idx"), 16)
            pool.wait_ge(sem("idx"), 16)
            for t in range(16):
                if t >= 4:
                    pool.wait_ge(sem("pat_psum"), 24 + t - 3)
                pool.indirect_dma_start(emb[:, t % 4, :], None, embed,
                                        bass.IndirectOffsetOnAxis(ap=idx[:, t:t + 1], axis=0)).then_inc(sem(f"emb{t % 4}"), 16)
            barrier(pool, "pool")

            def reduce_pair(k, name):
                pool.wait_ge(sem(name), 1)
                pool.partition_all_reduce(sc[:, G0:G0 + 2], sc[:, k:k + 2], P, RMAX).then_inc(sem("reduced"), 1)

            reduce_pair(Q_MX, "q_minmax")
            barrier(pool, "pool")
            barrier(pool, "pool")
            reduce_pair(A_MX, "a_minmax")
            barrier(pool, "pool")

            def quotient_bits(g, par, half):
                pool.wait_ge(sem("total"), g + 1)
                pool.tensor_tensor(L[par].bitcast(I32), L[par].bitcast(I32), wv[par].bitcast(I32), ALU.subtract).then_inc(sem("log2"), 1)
                wait(pool, "probs", g - 1)
                pool.tensor_tensor(top[par], wv[par], S[:, par, 2, :].unsqueeze(2).to_broadcast([P, 2 * SLOTS, N]),
                                   ALU.subtract).then_inc(sem("excess"), 1)

            def spread_v(g, par, half):
                wait(pool, "o_summed", g - 1)
                for a in range(2):
                    last = pool.tensor_copy(stv[:, par, :, a].rearrange("p b (j h d) -> p b j h d", h=2, d=HD)[:, :, :, a, :],
                                            VQ[:, bass.ds(g * 2, 2), :].rearrange("p b (j h d) -> p b j h d", h=2, d=HD)[:, :, :, a, :])
                last.then_inc(sem("v_spread"), 1)

            pool.memset(stv, 0.0).then_inc(sem("v_cleared"), 1)
            pool.wait_ge(sem("v_cleared"), 1)
            pipeline(pool, [(quotient_bits, 0), (spread_v, 2)], 32)
            barrier(pool, "pool")
            reduce_pair(O_MX, "o_minmax")
            pool.wait_ge(sem("y2_minmax"), 1)
            pool.partition_all_reduce(sc[:, G0:G0 + 2], sc[:, Y_MX:Y_MX + 2], P, RMAX).then_inc(sem("reduced"), 1)
            barrier(pool, "pool")
            barrier(pool, "pool")

            def square(g):
                for m in range(UC):
                    rows = P if m < UC - 1 else C1
                    n = g * UC + m
                    a = m % 2
                    pool.wait_ge(sem("weighted"), n + 1)
                    wait(pool, "h_used", n - 1)
                    pool.tensor_tensor(hh[0:rows, a, :], hr[0:rows, a, :], hc[0:rows, a, :], ALU.mult).then_inc(sem("hidden"), 1)

            square(0)
            with pool.Fori(1, TT // 2) as g:
                square(g)

        @block.scalar
        def _(act):
            def copy(out_, in_):
                return act.activation(out_, in_, ACT.Copy)

            def ident_(out_, in_, scale=1.0, bias=0.0):
                return act.activation(out_, in_, ACT.Identity, scale=scale, bias=bias)

            act.wait_ge(sem("consts"), 48)
            copy(ident_b[:, :], ident[:, :]).then_inc(sem("ident_b"), 1)
            act.wait_ge(sem("bias_rows"), 16 * 25)
            def by_patch(q, c):
                act.wait_ge(sem(f"ximg{q % 2}"), 48 * (q // 2 + 1))
                wait(act, "pat_psum", (q - 1) * GRID)
                return copy(xp[:, q % 2, c].rearrange("p (w r v) -> p w r v", w=GRID, v=PATCH),
                            ximg[:, q % 2, c].rearrange("p (r w v) -> p w r v", w=GRID, v=PATCH))

            by_patch(0, 0).then_inc(sem("by_patch_a"), 1)
            for q in range(4):
                if q < 3:
                    by_patch(q + 1, 0).then_inc(sem("by_patch_a"), 1)
                for wp in range(GRID):
                    n = q * GRID + wp
                    act.wait_ge(sem("pat_psum"), n + 1)
                    wait(act, "h_out", n - 1)
                    copy(patT[:, n % 2, 0:288], ps[:, 0, 0:288]).then_inc(sem("patT_a"), 1)
            for t in range(16):
                n = 24 + t
                act.wait_ge(sem("pat_psum"), n + 1)
                wait(act, "h_out", n - 1)
                copy(patT[:, n % 2, 0:384], ps[:, 0, 0:384]).then_inc(sem("patT_a"), 1)
                act.wait_ge(sem("z_psum"), t + 1)
                wait(act, "h_out", 24 + t - 1 if t >= 2 else 0)
                for m in range(2):
                    last = act.activation(zT[:, t % 2, m, :], ps[0:96, 4, m * P:(m + 1) * P], ACT.Gelu, bias=biases[0:96, m:m + 1])
                last.then_inc(sem("zT"), 1)
            barrier(act, "act")
            act.wait_ge(sem("ln_var"), 1)
            act.activation(rs[:, 1, :], rs[:, 0, :], ACT.Sqrt).then_inc(sem("ln_sqrt"), 1)

            def evac_x(g, par, half):
                act.wait_ge(sem("x_psum"), g + 1)
                wait(act, "v_psum", (g - 1) * 2)
                copy(xT0[:, par, :], ps[:, 0, 0:272])
                copy(xT1[:, par, :], ps[0:C1, 1, 0:272]).then_inc(sem("xT"), 1)

            def evac_q(g, par, half):
                act.wait_ge(sem("qk_psum"), g + 1)
                cols = bass.ds(g * 272, 272)
                ident_(yq[0][:, cols], ps[:, 2, 0:272], bias=biases[:, 2:3])
                ident_(yq[1][:, cols], ps[0:C1, 3, 0:272], bias=biases[0:C1, 3:4]).then_inc(sem("q_stored"), 1)

            pipeline(act, [(evac_x, 0), (evac_q, 0)], 16)
            barrier(act, "act")
            for n, (src, scale, dst, _, rows) in enumerate(jobs3):
                act.wait_ge(sem("q_scalars"), 1)
                wait(act, "q_rounded", n - 1)
                ident_(dst, src, scale=sc[0:rows, scale:scale + 1], bias=s1(T2, rows)).then_inc(sem("q_added"), 1)
            barrier(act, "act")
            barrier(act, "act")
            ident_(rmq[:, :, :], rowmax[:, :, :], scale=s1(A_KK), bias=s1(A_M16)).then_inc(sem("rmq"), 1)

            def squares(g, par, half):
                act.wait_ge(sem("rem"), g + 1)
                act.activation(sq[par], sq[par], ACT.Square, bias=s1(A_BH)).then_inc(sem("sq"), 1)

            def signs(g, par, half):
                act.wait_ge(sem("excess"), g + 1)
                act.activation(top[par], top[par], ACT.Sign).then_inc(sem("top"), 1)

            def powers(g, par, half):
                act.wait_ge(sem("quot"), g + 1)
                wait(act, "w", g - 1)
                ident_(PW[par], Qq[par], scale=-128.0, bias=s1(A_PB)).then_inc(sem("power"), 1)

            def exponent(g, par, half):
                act.wait_ge(sem("log2"), g + 1)
                wait(act, "pbits", g - 1)
                ident_(yb[par], L[par].bitcast(I32), scale=2.0 ** -23, bias=s1(A_CB)).then_inc(sem("exponent"), 1)

            def evac_pt(g, par, half):
                act.wait_ge(sem("pt_psum"), g + 1)
                wait(act, "o_summed", g - 1)
                copy(PT[par], pPT).then_inc(sem("PT"), 1)

            def evac_o(g, par, half):
                act.wait_ge(sem("o_summed"), g + 1)
                b = bass.ds(g * 2, 2)
                copy(oT[0].rearrange("p (b n) -> p b n", n=N)[:, b, :], pO[par][:, :, 0, :])
                copy(oT[1].rearrange("p (b n) -> p b n", n=N)[:, b, :], pO[par][0:C1, :, 1, :]).then_inc(sem("o_out"), 1)

            pipeline(act, [(powers, 0), (squares, 0), (evac_pt, 3), (exponent, 1), (signs, 1), (evac_o, 4)], 32)
            barrier(act, "act")
            act.wait_ge(sem("o_scalars"), 1)
            ident_(oT[0], oT[0], scale=s1(O_SC), bias=s1(T2)).then_inc(sem("o_added"), 1)
            ident_(oT[1], oT[1], scale=s1(O_SC, C1), bias=s1(T2, C1)).then_inc(sem("o_added"), 1)
            act.wait_ge(sem("ln2_var"), 1)
            act.activation(rs2[:, 1, :], rs2[:, 0, :], ACT.Sqrt).then_inc(sem("ln2_sqrt"), 1)
            barrier(act, "act")
            act.wait_ge(sem("rw_psum"), 1)
            copy(rwT[:, 0, :], ps[:, 5, 0:E])
            copy(rwT[0:C1, 1, :], ps[0:C1, 5, E:2 * E]).then_inc(sem("rwT"), 1)
            for i in range(TT):
                act.wait_ge(sem("x2_psum"), i + 1)
                a = i % 2
                copy(X0[:, i * P:(i + 1) * P], ps[:, a, 0:P])
                copy(X1[:, i * P:(i + 1) * P], ps[0:C1, a, P:2 * P]).then_inc(sem("X"), 1)
            act.wait_ge(sem("logits"), 1)
            act.activation(scr[0], ps[:, 2, 0:TT * E].rearrange("p (i e) -> p i e", e=E), ACT.Sigmoid).then_inc(sem("sigmoid"), 1)
            act.wait_ge(sem("ffn_c"), 32)
            copy(sel_b, sel_w).then_inc(sem("sel_b"), 1)
            for q in range(5):
                act.wait_ge(sem("ct_psum"), q + 1)
                n = min(8, TT - 8 * q) * P
                copy(CT[:, 1024 * q:1024 * q + n], ps[0:32, 3 + q % 2, 0:n // 2].bitcast(BF16)).then_inc(sem("CT"), 1)
            barrier(act, "act")

            def relu(g):
                for m in range(UC):
                    rows = P if m < UC - 1 else C1
                    n = g * UC + m
                    act.wait_ge(sem("h_psum"), n + 1)
                    wait(act, "hidden", n - 1)
                    act.activation(hr[0:rows, m % 2, :], ps[0:rows, m % 2, 0:256], ACT.Relu).then_inc(sem("relu"), 1)

            relu(0)
            with act.Fori(1, TT // 2) as g:
                relu(g)

        @block.vector
        def _(dve):
            def ch(ins):
                chain(dve, "vector_step", ins)

            ts = dve.tensor_scalar
            tt = dve.tensor_tensor
            dve.wait_ge(sem("bias_rows"), 16 * 25)
            for wp in range(GRID):
                last = tt(posb[:, wp, :], posb[:, wp, :], brow[0:96, 0, :], ALU.add)
            ch(last)
            dve.wait_ge(sem("wq_rows"), 16 * 8)
            mxw, mnw, nzw, inw = (wtmp[:, k, 0:8] for k in range(4))
            ch(dve.memset(wtmp[:, 0:6, :], 0.0))
            ch(dve.memset(wscale, 1.0))
            for j, (o, m) in enumerate(QROWS):
                dve.tensor_reduce(mxw[0:m, j:j + 1], wq_rows[0:m, j, :], X, ALU.max)
                last = dve.tensor_reduce(mnw[0:m, j:j + 1], wq_rows[0:m, j, :], X, ALU.min)
            ch(last)
            ch(ts(mxw, mxw, 0.0, None, ALU.max))
            ch(ts(mnw, mnw, 0.0, None, ALU.min))
            ch(tt(wscale, mxw, mnw, ALU.subtract))
            ch(ts(wscale, wscale, 1.0 / 255.0, EPS_Q, ALU.mult, ALU.max))
            ch(dve.reciprocal(inw, wscale))
            ch(tt(nzw, mnw, inw, ALU.mult))
            ch(ts(nzw, nzw, MAGIC, MAGIC, ALU.add, ALU.subtract))
            ch(ts(nzw, nzw, 255.0, MAGIC, ALU.add, ALU.add))
            for j, (o, m) in enumerate(QROWS):
                w = wq_rows[0:m, j, :]
                ch(ts(w, w, inw[0:m, j:j + 1], MAGIC, ALU.mult, ALU.add))
                ch(ts(w, w, nzw[0:m, j:j + 1], MAGIC, ALU.min, ALU.subtract))
                if j < 6:
                    ch(ts(w, w, wscale[0:m, j:j + 1], None, ALU.mult))
            for j in (6, 7):
                ch(ts(wtmp[0:96, j, 0:96], ident[0:96, 0:96], wscale[0:96, j:j + 1], None, ALU.mult))
            ch(dve.memset(ones[:, :], 1.0))
            wready.append(counts["vector_step"])
            for n, (_, rows, cols, dst) in enumerate(turns):
                dve.wait_ge(sem("w_psum"), n + 1)
                dve.tensor_copy(dst, ps[0:rows, n % 2, 0:cols]).then_inc(sem("w_turned"), 1)
            def by_patch(q):
                dve.wait_ge(sem(f"ximg{q % 2}"), 48 * (q // 2 + 1))
                wait(dve, "pat_psum", (q - 1) * GRID)
                for c in (1, 2):
                    last = dve.tensor_copy(xp[:, q % 2, c].rearrange("p (w r v) -> p w r v", w=GRID, v=PATCH),
                                           ximg[:, q % 2, c].rearrange("p (r w v) -> p w r v", w=GRID, v=PATCH))
                last.then_inc(sem("by_patch_b"), 1)

            by_patch(0)
            for q in range(4):
                if q < 3:
                    by_patch(q + 1)
                for wp in range(GRID):
                    n = q * GRID + wp
                    dve.wait_ge(sem("pat_psum"), n + 1)
                    wait(dve, "h_out", n - 1)
                    dve.tensor_copy(patT[:, n % 2, 288:576], ps[:, 1, 0:288]).then_inc(sem("patT_b"), 1)
                    dve.wait_ge(sem("h_out"), n + 1)
                    if q >= 2 and wp == 0:
                        dve.wait_ge(sem(f"h_stored{q % 2}"), 16 * (q // 2))
                    tt(hstage[:, q % 2, wp, :], ps[0:96, 2 + n % 2, 0:C], posb[:, wp, :], ALU.add).then_inc(sem("img_h"), 1)
            for t in range(16):
                n = 24 + t
                dve.wait_ge(sem("pat_psum"), n + 1)
                wait(dve, "h_out", n - 1)
                dve.tensor_copy(patT[:, n % 2, 384:768], ps[:, 1, 0:384]).then_inc(sem("patT_b"), 1)
                dve.wait_ge(sem("h_out"), n + 1)
                if t >= 2:
                    dve.wait_ge(sem(f"t_stored{t % 2}"), 16 * (t // 2))
                tt(tstage[:, t % 2, :], ps[:, 2 + n % 2, 0:C], brow[:, 1, :], ALU.add).then_inc(sem("txt_h"), 1)
            barrier(dve, "dve")

            for b in range(B):
                if b % 16 == 0:
                    dve.wait_ge(sem(f"hb{b // 16}"), 16)
                ch(dve.bn_stats(bst[:, b % 2, :], hb[:, b, :]))
                ch(dve.bn_aggr(mv[:, b, :], bst[:, b % 2, :]))

            def inverse_deviation(var, r, name):
                ch(ts(r[:, 0, :], var, EPS_LN, None, ALU.add))
                ch(ts(r[:, 2, :], r[:, 0, :], 1.0, None, ALU.mult))
                dve.drain().then_inc(sem(f"{name}_var"), 1)
                dve.wait_ge(sem(f"{name}_sqrt"), 1)
                ch(dve.reciprocal(r[:, 2, :], r[:, 1, :]))
                ch(tt(r[:, 2, :], r[:, 2, :], r[:, 0, :], ALU.mult))
                ch(tt(r[:, 1, :], r[:, 1, :], r[:, 2, :], ALU.add))
                ch(ts(r[:, 1, :], r[:, 1, :], 0.5, None, ALU.mult))
                ch(dve.reciprocal(r[:, 2, :], r[:, 1, :]))

            inverse_deviation(mv[:, :, 1], rs, "ln")

            def normalise(g, par, half):
                wait(dve, "x_psum", g - 1)
                for k in range(4):
                    b = g * 4 + k
                    last = ts(xn[:, par, k:k + 1, :], hb[:, bass.ds(b, 1), :], mv[:, bass.ds(b, 1), 0], rs[:, 2, bass.ds(b, 1)],
                              ALU.subtract, ALU.mult)
                last.then_inc(sem("xn"), 1)

            def evac_kv(g, par, half):
                dve.wait_ge(sem("qk_psum"), g + 1)
                cols = bass.ds(g * 272, 272)
                ts(yk[0][:, cols], ps[:, 4, 0:272], biases[:, 4:5], None, ALU.add)
                ts(yk[1][:, cols], ps[0:C1, 5, 0:272], biases[0:C1, 5:6], None, ALU.add).then_inc(sem("k_stored"), 1)
                for k in range(2):
                    dve.wait_ge(sem("v_psum"), g * 2 + k + 1)
                    tt(yv[:, bass.ds(g * 4 + 2 * k, 2), :], ps[0:N, 6 + k, 0:2 * C].rearrange("p (b c) -> p b c", b=2),
                       bvrow[0:N, :].unsqueeze(1).to_broadcast([N, 2, C]), ALU.add).then_inc(sem("v_stored"), 1)

            pipeline(dve, [(normalise, 0), (evac_kv, 1)], 16)
            dve.wait_ge(sem("q_stored"), 16)
            dve.wait_ge(sem("k_stored"), 16)
            dve.wait_ge(sem("v_stored"), 32)

            def minmax(parts, k):
                ch(dve.memset(sc[:, T0:T1 + 1], 0.0))
                ch(dve.memset(sc[:, k:k + 2], 0.0))
                for rows, part, axis in parts:
                    ch(dve.tensor_reduce(sc[0:rows, T0:T0 + 1], part, axis, ALU.max))
                    ch(dve.tensor_reduce(sc[0:rows, T1:T1 + 1], part, axis, ALU.min, negate=True))
                    ch(tt(sc[0:rows, k:k + 2], sc[0:rows, k:k + 2], sc[0:rows, T0:T0 + 2], ALU.max))

            def scale_of(mx, nmn, s, inv, capm):
                ch(tt(s1(T0), s1(mx), s1(nmn), ALU.add))
                ch(ts(s1(s), s1(T0), 1.0 / 255.0, EPS_Q, ALU.mult, ALU.max))
                ch(dve.reciprocal(s1(inv), s1(s)))
                ch(tt(s1(T0), s1(nmn), s1(inv), ALU.mult))
                ch(ts(s1(T0), s1(T0), MAGIC, MAGIC, ALU.add, ALU.subtract))
                ch(ts(s1(capm), s1(T0), -1.0, 255.0, ALU.mult, ALU.add))

            minmax([(P, yq[0], X), (C1, yq[1], X), (P, yk[0], X), (C1, yk[1], X), (N, yv, XY)], Q_MX)
            dve.drain().then_inc(sem("q_minmax"), 1)
            dve.wait_ge(sem("reduced"), 1)
            ch(dve.tensor_copy(sc[:, Q_MX:Q_MX + 2], sc[:, G0:G0 + 2]))
            scale_of(Q_MX, Q_NMN, Q_S, Q_INV, Q_CAPM)
            ch(ts(s1(Q_CAPM), s1(Q_CAPM), MAGIC, None, ALU.add))
            ch(tt(s1(Q_EV), s1(Q_INV), parmask[:, 0:1], ALU.mult))
            ch(tt(s1(Q_OD), s1(Q_INV), parmask[:, 1:2], ALU.mult))
            ch(dve.memset(s1(T2), MAGIC))
            barrier(dve, "dve")
            dve.drain().then_inc(sem("q_scalars"), 1)
            for n, (src, scale, t, dst, rows) in enumerate(jobs3):
                dve.wait_ge(sem("q_added"), n + 1)
                if dst is not None:
                    ts(dst, t, s1(Q_CAPM, rows), MAGIC, ALU.min, ALU.subtract).then_inc(sem("q_rounded"), 1)
                else:
                    ch(ts(t, t, s1(Q_CAPM, rows), MAGIC, ALU.min, ALU.subtract))
                    k = 0 if rows == P else 1
                    QK = (QK0, QK1)[k]
                    tt(QK[:, :, 2 * NQ:3 * NQ].rearrange("p b (h i) -> p b h i", i=NL),
                       t.unsqueeze(2).to_broadcast([rows, B, 16, NL]),
                       headmask[0:rows, k, :].unsqueeze(1).unsqueeze(3).to_broadcast([rows, B, 16, NL]),
                       ALU.mult).then_inc(sem("q_rounded"), 1)
            barrier(dve, "dve")

            def extremes(g, par, half):
                dve.wait_ge(sem("scored"), g + 1)
                for part, (_, k, s0) in enumerate(PARTS):
                    sv = score_part(4 * par, part)
                    dve.tensor_reduce(rowmax[:, bass.ds(g, 1), s0:s0 + 2 * k].rearrange("p o (a s) -> p (o a) s", a=2), sv, X, ALU.max)
                    last = dve.tensor_reduce(gmin[:, bass.ds(g * 2 + part, 1)], sv, mybir.AxisListType.XYZ, ALU.min)
                last.then_inc(sem("extremes"), 1)

            pipeline(dve, [(extremes, 0)], 32)
            dve.wait_ge(sem("extremes"), 32)
            ch(dve.tensor_reduce(s1(A_MX), rowmax, XY, ALU.max))
            ch(ts(s1(A_MX), s1(A_MX), 0.0, None, ALU.max))
            ch(dve.tensor_reduce(s1(A_NMN), gmin, X, ALU.min, negate=True))
            ch(ts(s1(A_NMN), s1(A_NMN), 0.0, None, ALU.max))
            dve.drain().then_inc(sem("a_minmax"), 1)
            dve.wait_ge(sem("reduced"), 2)
            ch(tt(s1(A_K1), s1(Q_S), s1(Q_S), ALU.mult))
            ch(ts(s1(A_K1), s1(A_K1), HD ** -0.5, None, ALU.mult))
            ch(ts(sc[:, A_MX:A_MX + 2], sc[:, G0:G0 + 2], s1(A_K1), None, ALU.mult))
            scale_of(A_MX, A_NMN, A_S, A_INV, A_CAP)
            ch(ts(s1(A_CAP), s1(A_CAP), H16 + 512.0, None, ALU.add))
            ch(dve.memset(s1(A_M16), H16 + 512.0))
            ch(tt(s1(A_KK), s1(A_K1), s1(A_INV), ALU.mult))
            ch(ts(s1(A_NKK), s1(A_KK), -1.0, None, ALU.mult))
            ch(dve.reciprocal(s1(A_IS), s1(A_S)))

            def floor_(k, tmp):
                ch(ts(s1(tmp), s1(k), MAGIC, MAGIC, ALU.add, ALU.subtract))
                ch(tt(s1(T1), s1(tmp), s1(k), ALU.is_gt))
                ch(tt(s1(tmp), s1(tmp), s1(T1), ALU.subtract))
                ch(ts(s1(T1), s1(k), 4194304.0, None, ALU.is_gt))
                ch(tt(s1(T0), s1(k), s1(tmp), ALU.subtract))
                ch(tt(s1(T0), s1(T0), s1(T1), ALU.mult))
                ch(tt(s1(k), s1(tmp), s1(T0), ALU.add))

            ch(ts(s1(A_A), s1(A_IS), 0.6931, 1e6, ALU.mult, ALU.min))
            ch(ts(s1(A_B), s1(A_A), MAGIC, MAGIC, ALU.add, ALU.subtract))
            ch(tt(s1(T1), s1(A_A), s1(A_B), ALU.is_gt))
            ch(tt(s1(A_A), s1(A_B), s1(T1), ALU.add))
            ch(ts(s1(A_A), s1(A_A), 256.0, None, ALU.min))
            ch(dve.reciprocal(s1(A_IA), s1(A_A)))
            ch(ts(s1(A_NA), s1(A_A), -1.0, None, ALU.mult))
            ch(ts(s1(A_B), s1(A_IS), 0.96963238 / C0, None, ALU.mult))
            floor_(A_B, T2)
            ch(tt(s1(A_C), s1(A_IS), s1(A_IS), ALU.mult))
            ch(ts(s1(A_C), s1(A_C), 1.0 / C0, None, ALU.mult))
            floor_(A_C, T2)
            ch(ts(s1(A_BH), s1(A_A), H16, -H16, ALU.mult, ALU.add))
            ch(ts(s1(T0), s1(A_B), 0.5, None, ALU.mult))
            ch(tt(s1(A_BH), s1(A_BH), s1(T0), ALU.subtract))
            ch(tt(s1(T0), s1(T0), s1(T0), ALU.mult))
            ch(tt(s1(A_K0), s1(A_C), s1(T0), ALU.subtract))
            ch(ts(s1(A_CL), s1(A_A), 30.0, H16, ALU.mult, ALU.add))
            ch(ts(s1(A_SB), s1(A_IA), -H16, H16 - 0.5 + 2.0 ** -10, ALU.mult, ALU.add))
            ch(dve.memset(s1(A_CB), H16 + 1.5 + 2.0 ** -12))
            ch(dve.memset(s1(A_PB), 128.0 * (127.0 + 1.0 + H16) + 64.0))
            barrier(dve, "dve")
            dve.wait_ge(sem("rmq"), 1)
            ch(ts(rmq, rmq, s1(A_CAP), None, ALU.min))
            ch(ts(rmq, rmq, -512.0, None, ALU.add))

            def front(g, par, half):
                dve.wait_ge(sem("scored"), 32 + g + 1)
                D, Q = Dq[par], Qq[par]
                for part, (_, k, s0) in enumerate(PARTS):
                    m = rmq[:, bass.ds(g, 1), s0:s0 + 2 * k].rearrange("p o (a s) -> p (o a) s", a=2)
                    for a in range(2):
                        last = dve.scalar_tensor_tensor(D[:, s0 + k * a:s0 + k * (a + 1), :], score_part(0, part)[:, a],
                                                        s1(A_NKK), m[:, a, :].unsqueeze(2).to_broadcast([P, k, N]),
                                                        ALU.mult, ALU.add)
                last.then_inc(sem("dist"), 1)
                dve.wait_ge(sem("dist"), g + 1)
                ts(D, D, H16, s1(A_CL), ALU.max, ALU.min).then_inc(sem("clamped"), 1)
                dve.wait_ge(sem("clamped"), g + 1)
                ts(Q, D, s1(A_IA), s1(A_SB), ALU.mult, ALU.add).then_inc(sem("quot"), 1)
                dve.wait_ge(sem("quot"), g + 1)
                dve.scalar_tensor_tensor(sq[par], Q, s1(A_NA), D, ALU.mult, ALU.add).then_inc(sem("rem"), 1)

            def mid(g, par, half):
                dve.wait_ge(sem("sq"), g + 1)
                dve.wait_ge(sem("power"), g + 1)
                wait(dve, "top", g - 1)
                W = wv[par]
                dve.scalar_tensor_tensor(W, sq[par], s1(A_K0), PW[par].rearrange("p s k -> p (s k)").bitcast(BF16).rearrange("p (s k) -> p s k", k=N),
                                         ALU.add, ALU.mult).then_inc(sem("w"), 1)
                dve.wait_ge(sem("w"), g + 1)
                dve.tensor_reduce(S[:, par, 0, :], W, X, ALU.add).then_inc(sem("wsum"), 1)
                dve.wait_ge(sem("wsum"), g + 1)
                ts(S[:, par, 1, :], S[:, par, 0, :], 1.0 / 3.0, None, ALU.mult).then_inc(sem("third"), 1)
                ts(S[:, par, 2, :], S[:, par, 0, :], 2.0 / 3.0, None, ALU.mult)
                dve.wait_ge(sem("third"), g + 1)
                wait(dve, "exponent", g - 1)
                dve.scalar_tensor_tensor(L[par], W, 1.0 / 6.0, S[:, par, 1, :].unsqueeze(2).to_broadcast([P, 2 * SLOTS, N]),
                                         ALU.mult, ALU.add).then_inc(sem("total"), 1)

            def tail(g, par, half):
                dve.wait_ge(sem("exponent"), g + 1)
                wait(dve, "pt_psum", g - 1)
                pi = Pb[par].rearrange("p s k -> p (s k)").bitcast(I16)
                ts(pi, yb[par].rearrange("p s k -> p (s k)"), -128.0, 128.0 * (H16 + 127.0), ALU.mult, ALU.add).then_inc(sem("pbits"), 1)
                dve.wait_ge(sem("pbits"), g + 1)
                ts(Pb[par], Pb[par], 384.0, 384.0, ALU.add, ALU.subtract).then_inc(sem("masked"), 1)
                dve.wait_ge(sem("masked"), g + 1)
                dve.wait_ge(sem("top"), g + 1)
                tt(Pb[par], Pb[par], top[par], ALU.max).then_inc(sem("probs"), 1)

            pipeline(dve, [(front, 0), (mid, 1), (tail, 2)], 32)
            barrier(dve, "dve")
            minmax([(P, oT[0], X), (C1, oT[1], X)], O_MX)
            dve.drain().then_inc(sem("o_minmax"), 1)
            dve.wait_ge(sem("reduced"), 3)
            ch(ts(sc[:, O_MX:O_MX + 2], sc[:, G0:G0 + 2], s1(Q_S), None, ALU.mult))
            scale_of(O_MX, O_NMN, O_S, O_INV, O_CAPM)
            ch(ts(s1(O_CAPM), s1(O_CAPM), MAGIC, None, ALU.add))
            ch(tt(s1(O_SC), s1(Q_S), s1(O_INV), ALU.mult))
            ch(dve.memset(s1(T2), MAGIC))
            ch(ts(prow, prow, s1(O_S), None, ALU.mult))
            dve.drain().then_inc(sem("o_scalars"), 1)
            dve.wait_ge(sem("o_added"), 2)
            ts(oq[0], oT[0], s1(O_CAPM), MAGIC, ALU.min, ALU.subtract)
            ts(oq[1], oT[1], s1(O_CAPM, C1), MAGIC, ALU.min, ALU.subtract).then_inc(sem("oq"), 1)
            for i in range(TT):
                dve.wait_ge(sem("y2_psum"), i + 1)
                tt(y2[:, i, :], ps[:, i % 2, 0:C], prow, ALU.mult).then_inc(sem("y2_a"), 1)
            dve.wait_ge(sem("y2_a"), TT)
            ch(tt(y2, y2, bprow.unsqueeze(1).to_broadcast([P, TT, C]), ALU.add))
            minmax([(P, y2, XY)], Y_MX)
            dve.drain().then_inc(sem("y2_minmax"), 1)
            dve.wait_ge(sem("reduced"), 4)
            ch(dve.tensor_copy(sc[:, Y_MX:Y_MX + 2], sc[:, G0:G0 + 2]))
            scale_of(Y_MX, Y_NMN, Y_S, Y_INV, Y_CAPM)
            ch(ts(s1(Y_CAPM), s1(Y_CAPM), MAGIC, None, ALU.add))
            ch(ts(y2, y2, s1(Y_INV), MAGIC, ALU.mult, ALU.add))
            ch(ts(y2, y2, s1(Y_CAPM), MAGIC, ALU.min, ALU.subtract))
            dve.wait_ge(sem("hf"), 16)
            ch(dve.scalar_tensor_tensor(hf, y2, s1(Y_S), hf, ALU.mult, ALU.add))
            for i in range(TT):
                ch(dve.bn_stats(bst2[:, i % 2, :], hf[:, i, :]))
                ch(dve.bn_aggr(mv2[:, i, :], bst2[:, i % 2, :]))
            inverse_deviation(mv2[:, :, 1], rs2, "ln2")
            for i in range(TT):
                last = ts(xn2[:, i, :], hf[:, i, :], mv2[:, i, 0:1], rs2[:, 2, i:i + 1], ALU.subtract, ALU.mult)
            ch(last)
            barrier(dve, "dve")
            dve.wait_ge(sem("sigmoid"), 1)
            dve.wait_ge(sem("ffn_w"), 16 * 23)
            dve.wait_ge(sem("ffn_c"), 32)
            scores, biased, rank, comb = scr
            ch(tt(biased, scores, bbrow.unsqueeze(1).to_broadcast([P, TT, E]), ALU.add))
            mine = biased.unsqueeze(3).to_broadcast([P, TT, E, E])
            other = biased.unsqueeze(2).to_broadcast([P, TT, E, E])
            ch(tt(cmp_a, other, mine, ALU.is_equal))
            ch(tt(cmp_a.rearrange("p i e f -> p i (e f)"), cmp_a.rearrange("p i e f -> p i (e f)"),
                  lower.unsqueeze(1).to_broadcast([P, TT, E * E]), ALU.mult))
            ch(tt(cmp_b, other, mine, ALU.is_gt))
            ch(tt(cmp_a, cmp_a, cmp_b, ALU.add))
            ch(dve.tensor_reduce(rank, cmp_a, X, ALU.add))
            ch(dve.scalar_tensor_tensor(comb, rank, 1.5, scores, ALU.is_lt, ALU.mult))
            ch(dve.tensor_reduce(csum[:, 0, :], comb, X, ALU.add))
            ch(ts(csum[:, 0, :], csum[:, 0, :], 1e-20, None, ALU.add))
            ch(dve.reciprocal(csum[:, 1, :], csum[:, 0, :]))
            ch(tt(comb, comb, csum[:, 1, :].unsqueeze(2).to_broadcast([P, TT, E]), ALU.mult))
            ch(dve.memset(C3, 0.0))
            for k in range(3):
                ch(dve.tensor_copy(C3[:, :, E * k:E * (k + 1)], comb))
                ch(tt(comb, comb, C3[:, :, E * k:E * (k + 1)], ALU.subtract))
            ch(dve.memset(C3[:, :, 24:25], 1.0))
            dve.drain().then_inc(sem("C3"), 1)
            barrier(dve, "dve")

            def weigh(g):
                for m in range(UC):
                    rows = P if m < UC - 1 else C1
                    n = g * UC + m
                    dve.wait_ge(sem("relu"), n + 1)
                    dve.wait_ge(sem("c_psum"), n + 1)
                    wait(dve, "hidden", n - 1)
                    tt(hc[0:rows, m % 2, :], hr[0:rows, m % 2, :], ps[0:rows, 2 + m % 2, 0:256], ALU.mult).then_inc(sem("weighted"), 1)

            def add_h(g, par, half):
                dve.wait_ge(sem("h_used"), (g + 1) * UC)
                wait(dve, f"stored{par}", half * 16)
                tt(ost[:, par], ps[:, 4 + 2 * par:6 + 2 * par, 0:C], hf[:, bass.ds(g * 2, 2), :], ALU.add).then_inc(sem("out_ready"), 1)

            weigh(0)
            weigh(1)
            add_h(0, 0, 0)
            weigh(2)
            add_h(1, 1, 0)
            with dve.Fori(0, (TT // 2 - 3) // 2) as i:
                for p in (0, 1):
                    weigh(i * 2 + 3 + p)
                    add_h(i * 2 + 2 + p, p, i + 1)
            add_h(TT // 2 - 1, 0, 8)

        @block.tensor
        def _(pe):
            def mm(o, a, b, start=True, stop=True):
                return pe.matmul(o, a, b, start=start, stop=stop, skip_group_check=True)

            pe.wait_ge(sem("consts"), 48)
            pe.wait_ge(sem("w_rows"), 48)
            pe.wait_ge(sem("vector_step"), wready[0])
            for n, (pieces, rows, cols, dst) in enumerate(turns):
                wait(pe, "w_turned", n - 1)
                for src, m, at in pieces:
                    if src is None:
                        last = mm(ps[:, n % 2, 0:96], ones[0:96, :], wtmp[0:96, m, 0:96])
                    else:
                        last = pe.transpose(ps[0:rows, n % 2, at:at + m], src, ident[0:m, 0:m])
                last.then_inc(sem("w_psum"), 1)
            pe.wait_ge(sem("w_turned"), len(turns))

            for q in range(4):
                pe.wait_ge(sem("by_patch_a"), q + 1)
                pe.wait_ge(sem("by_patch_b"), q + 1)
                for wp in range(GRID):
                    n = q * GRID + wp
                    wait(pe, "patT_a", n)
                    wait(pe, "patT_b", n)
                    for k in range(KC):
                        c, half = k // 2, k % 2
                        src = xp[:, q % 2, c, (2 * wp + half) * P:(2 * wp + half + 1) * P]
                        last = pe.transpose(ps[:, k // 3, (k % 3) * 96:(k % 3) * 96 + 96], src, ident[0:96, 0:96])
                    last.then_inc(sem("pat_psum"), 1)
                    pe.wait_ge(sem("patT_a"), n + 1)
                    pe.wait_ge(sem("patT_b"), n + 1)
                    wait(pe, "img_h", n - 1)
                    for k in range(KC):
                        last = mm(ps[0:96, 2 + n % 2, 0:C], patT[:, n % 2, k * 96:(k + 1) * 96], tokT[:, k, :], k == 0, k == KC - 1)
                    last.then_inc(sem("h_out"), 1)
            pe.wait_ge(sem("img_h"), 24)
            for t in range(16):
                n = 24 + t
                pe.wait_ge(sem(f"emb{t % 4}"), 16 * (t // 4 + 1))
                for k in range(KC):
                    last = pe.transpose(ps[:, k // 3, (k % 3) * P:(k % 3) * P + P], emb[:, t % 4, k * P:(k + 1) * P], ident[:, :])
                last.then_inc(sem("pat_psum"), 1)
                pe.wait_ge(sem("patT_a"), n + 1)
                pe.wait_ge(sem("patT_b"), n + 1)
                wait(pe, "zT", t)
                for m in range(2):
                    for k in range(KC):
                        last = mm(ps[0:96, 4, m * P:(m + 1) * P], w1T[:, k, m * 96:(m + 1) * 96], patT[:, n % 2, k * P:(k + 1) * P], k == 0, k == KC - 1)
                last.then_inc(sem("z_psum"), 1)
                pe.wait_ge(sem("zT"), t + 1)
                wait(pe, "txt_h", t - 1)
                for m in range(2):
                    last = mm(ps[:, 2 + n % 2, 0:C], zT[:, t % 2, m, :], w2T[:, m, :], m == 0, m == 1)
                last.then_inc(sem("h_out"), 1)
            barrier(pe, "pe")

            def turn_x(g, par, half):
                pe.wait_ge(sem("xn"), g + 1)
                wait(pe, "xT", g)
                for k in range(4):
                    pe.transpose(ps[:, 0, k * N:(k + 1) * N], xn[:, par, k, 0:P], ident[0:N, 0:N])
                    last = pe.transpose(ps[0:C1, 1, k * N:(k + 1) * N], xn[:, par, k, P:C], ident[0:N, 0:N])
                last.then_inc(sem("x_psum"), 1)

            def qkv(g, par, half):
                pe.wait_ge(sem("xT"), g + 1)
                wait(pe, "q_stored", g)
                wait(pe, "k_stored", g)
                for j in range(4):
                    o, m = QROWS[j]
                    mm(ps[0:m, 2 + j, 0:272], wqT0[:, o:o + m], xT0[:, par, :], True, False)
                    last = mm(ps[0:m, 2 + j, 0:272], wqT1[:, o:o + m], xT1[:, par, :], False, True)
                last.then_inc(sem("qk_psum"), 1)
                for k in range(2):
                    wait(pe, "v_stored", g * 2 + k - 1)
                    for b in range(2):
                        t = slice((2 * k + b) * N, (2 * k + b + 1) * N)
                        o = ps[0:N, 6 + k, b * C:(b + 1) * C]
                        mm(o, xT0[:, par, t], wqT0[:, 2 * C:3 * C], True, False)
                        last = mm(o, xT1[:, par, t], wqT1[:, 2 * C:3 * C], False, True)
                    last.then_inc(sem("v_psum"), 1)

            pipeline(pe, [(turn_x, 0), (qkv, 0)], 16)
            barrier(pe, "pe")
            barrier(pe, "pe")

            def scores(phase, freed):
                def fn(g, par, half):
                    pe.wait_ge(sem(f"st_qk{par}"), (half + 1 + 16 * phase) * 32)
                    wait(pe, freed, g if phase else g - 1)
                    base = 0 if phase else 4 * par
                    for b in range(2):
                        for j in range(PAIRS):
                            st = st0 if j < 4 else st1
                            rows = slice(32 * (j % 4), 32 * (j % 4) + 32)
                            bank, k, _ = score_slot(b, j)
                            for a in range(2):
                                mm(ps[NQ * a:NQ * (a + 1), base + bank, k * N:(k + 1) * N],
                                   st[rows, par, b, NQ * a:NQ * (a + 1)], st[rows, par, b, 3 * NQ:QKW])
                    for b in range(2):
                        bank, k, _ = score_slot(b, PAIRS)
                        for a in range(2):
                            o = ps[NQ * a:NQ * (a + 1), base + bank, k * N:(k + 1) * N]
                            mm(o, st0[:, par, b, 2 * NQ:3 * NQ], st0[:, par, b, 3 * NQ:QKW], True, False)
                            last = mm(o, st1[:, par, b, 2 * NQ:3 * NQ], st1[:, par, b, 3 * NQ:QKW], False, True)
                    last.then_inc(sem("scored"), 1)
                return fn

            pipeline(pe, [(scores(0, "extremes"), 0)], 32)
            barrier(pe, "pe")

            def turn_p(g, par, half):
                pe.wait_ge(sem("probs"), g + 1)
                wait(pe, "PT", g)
                for s in range(2 * SLOTS):
                    last = pe.transpose(pPT[:, s // SLOTS, s % SLOTS, :], Pb[par][:, s, :], ident_b[:, :])
                last.then_inc(sem("pt_psum"), 1)

            def sum_v(g, par, half):
                pe.wait_ge(sem("PT"), g + 1)
                pe.wait_ge(sem("v_spread"), g + 1)
                wait(pe, "o_out", g - 1)
                pt = PT[par].rearrange("p b s q -> p (b s) q")
                for b in range(2):
                    left = pt[:, score_slot(b, PAIRS)[2], :]
                    for j in range(PAIRS):
                        rows = slice(32 * (j % 4), 32 * (j % 4) + 32)
                        main = pt[:, score_slot(b, j)[2], :]
                        o = pO[par][rows, b, j // 4, :]
                        for a in range(2):
                            mm(o[:, 0:NQ], stv[:, par, b, a, 32 * j:32 * j + 32], main[:, NQ * a:NQ * (a + 1)], a == 0, a == 1)
                        for a in range(2):
                            h = 2 * j + a
                            last = mm(o[:, NQ:N], stv[:, par, b, a, 32 * j:32 * j + 32], left[:, NL * h:NL * (h + 1)], a == 0, a == 1)
                last.then_inc(sem("o_summed"), 1)

            pipeline(pe, [(scores(1, "dist"), 0), (turn_p, 3), (sum_v, 4)], 32)
            barrier(pe, "pe")
            pe.wait_ge(sem("oq"), 1)
            for i in range(TT):
                wait(pe, "y2_a", i - 1)
                t = slice(i * P, (i + 1) * P)
                mm(ps[:, i % 2, 0:C], oq[0][:, t], wpb0, True, False)
                mm(ps[:, i % 2, 0:C], oq[1][:, t], wpb1, False, True).then_inc(sem("y2_psum"), 1)
            barrier(pe, "pe")
            pe.wait_ge(sem("ffn_w"), 16 * 23)
            pe.transpose(ps[:, 5, 0:E], rw_rows[:, 0:P], ident[0:E, 0:E])
            pe.transpose(ps[0:C1, 5, E:2 * E], rw_rows[:, P:C], ident[0:E, 0:E]).then_inc(sem("rw_psum"), 1)
            for i in range(TT):
                wait(pe, "X", i - 1)
                pe.transpose(ps[:, i % 2, 0:P], xn2[:, i, 0:P], ident[:, :])
                pe.transpose(ps[0:C1, i % 2, P:2 * P], xn2[:, i, P:C], ident[:, :]).then_inc(sem("x2_psum"), 1)
            pe.wait_ge(sem("X"), TT)
            pe.wait_ge(sem("rwT"), 1)
            for i in range(TT):
                t = slice(i * P, (i + 1) * P)
                mm(ps[:, 2, i * E:(i + 1) * E], X0[:, t], rwT[:, 0, :], True, False)
                last = mm(ps[:, 2, i * E:(i + 1) * E], X1[:, t], rwT[0:C1, 1, :], False, True)
            last.then_inc(sem("logits"), 1)
            pe.wait_ge(sem("C3"), 1)
            for q in range(5):
                wait(pe, "CT", q - 1)
                for k in range(min(8, TT - 8 * q)):
                    last = pe.transpose(ps[0:32, 3 + q % 2, k * 64:(k + 1) * 64].bitcast(BF16), C3[:, 8 * q + k, :], ident_b[:, :])
                last.then_inc(sem("ct_psum"), 1)
            barrier(pe, "pe")

            def experts(g, par, half):
                def up(m):
                    rows = P if m < UC - 1 else C1
                    n = g * UC + m
                    if m == 0:
                        pe.wait_ge(sem(f"xs{par}"), (half + 1) * 48)
                    wait(pe, "relu", n - 1)
                    u = slice(m * P, m * P + rows)
                    mm(ps[0:rows, m % 2, 0:256], w1a[:, u], xs0[:, par], True, False)
                    mm(ps[0:rows, m % 2, 0:256], w1b[:, u], xs1[:, par], False, True).then_inc(sem("h_psum"), 1)
                    wait(pe, "weighted", n - 1)
                    mm(ps[0:rows, 2 + m % 2, 0:256], sel_b[:, u], cts[:, par]).then_inc(sem("c_psum"), 1)

                def down(m):
                    rows = P if m < UC - 1 else C1
                    n = g * UC + m
                    pe.wait_ge(sem("hidden"), n + 1)
                    if m == 0:
                        wait(pe, "out_ready", g - 1)
                    for i in range(2):
                        last = mm(ps[:, 4 + 2 * par + i, 0:C], hh[0:rows, m % 2, i * P:(i + 1) * P], w2a[0:rows, m, :], m == 0, m == UC - 1)
                    last.then_inc(sem("h_used"), 1)

                for m in range(UC + 2):
                    if m < UC:
                        up(m)
                    if m >= 2:
                        down(m - 2)

            pipeline(pe, [(experts, 0)], TT // 2)


_INS = ['x', 'x_txt', 'L0_tok_W', 'L0_tok_b', 'L0_tok_pos', 'L0_txt_tok_embed', 'L0_txt_W1', 'L0_txt_b1', 'L0_txt_W2',
        'L0_txt_b2', 'L0_attn_w_qkv', 'L0_attn_b_qkv', 'L0_attn_w_proj', 'L0_attn_b_proj', 'L0_ffn_w_fc_sh',
        'L0_ffn_w_proj_sh', 'L0_ffn_w1', 'L0_ffn_w2', 'L0_ffn_router_w', 'L0_ffn_balance_bias']


def constants():
    import numpy as np

    p = np.arange(P)
    h = np.arange(16)
    masks = np.zeros((P, 34), np.float32)
    masks[:, 0:16] = (p[:, None] // HD == h) & (h < 8)
    masks[:, 16:32] = (p[:, None] // HD + 8 == h) & (h < H)
    masks[:, 32] = p // HD % 2 == 0
    masks[:, 33] = p // HD % 2 == 1
    u = np.arange(UC * P)
    rows = np.arange(32)
    expert = np.where(rows < 3 * E, rows % E, np.where(rows == 3 * E, E, -1))
    select = (u // C == expert[:, None]).astype(np.float32)
    e = np.arange(E)
    lower = (e[None, :] < e[:, None]).astype(np.float32).reshape(-1)
    return {"ident": np.eye(P, dtype=np.float32), "masks": masks, "select": select, "lower": lower}


def kernel(**inputs):
    import numpy as _np
    import concourse.bacc as _bacc
    from concourse import mybir as _mybir
    from concourse.bass_utils import run_bass_kernel_spmd as _run

    nc = _bacc.Bacc("TRN2", target_bir_lowering=False, num_devices=1)
    arrays, args = {}, []
    for name, a in [(n, inputs[n]) for n in _INS] + list(constants().items()):
        a = _np.ascontiguousarray(a)
        arrays[f"in_{name}_dram"] = a
        args.append(nc.dram_tensor(f"in_{name}_dram", a.shape, _mybir.dt.from_np(a.dtype), kind="ExternalInput").ap())
    args.append(nc.dram_tensor("out_0_dram", (B, N, C), _mybir.dt.float32, kind="ExternalOutput").ap())
    program(nc, *args)
    r = _run(nc, [arrays], core_ids=[0])
    return r.results[0]["out_0_dram"]
```

```python
from contextlib import ExitStack

import concourse.bass as bass
from concourse import mybir

F32 = mybir.dt.float32
F16 = mybir.dt.float16
BF16 = mybir.dt.bfloat16
I16 = mybir.dt.int16
I32 = mybir.dt.int32
ALU = mybir.AluOpType
ACT = mybir.ActivationFunctionType
X = mybir.AxisListType.X
XY = mybir.AxisListType.XY
RMAX = bass.bass_isa.ReduceOp.max

P = 128
B = 64
C = 192
C1 = C - P
GRID = 6
PATCH = 16
NI = GRID * GRID
NT = 32
N = NI + NT
T = B * N
TT = T // P
H = 12
HD = C // H
MW = 6356
PAIRS = H // 2
NQ = 64
NL = N - NQ
FRONT = 768
KC = FRONT // P
SLOTS = PAIRS + 1
QKW = 3 * NQ + N
E = 8
U = (E + 1) * C
UC = (U + P - 1) // P
HB = 7
W2M = UC - 1
X_UNIT = 1024.0
H_UNIT = 2.0 ** -25
EPS_LN = 1e-5
EPS_Q = 1.1920928955078125e-07
MAGIC = 12582912.0
H16 = 1024.0
C0 = 0.35815147


def pipeline(eng, stages, groups):
    last = max(lag for _, lag in stages)
    lead = last + 2 + (groups - last) % 2

    def step(s):
        for fn, lag in stages:
            if 0 <= s - lag < groups:
                fn(s - lag, (s - lag) % 2, (s - lag) // 2)

    for s in range(lead):
        step(s)
    with eng.Fori(0, (groups - lead) // 2) as i:
        for p in (0, 1):
            for fn, lag in stages:
                g = lead + p - lag
                fn(i * 2 + g, g % 2, i + g // 2)
    for s in range(groups, groups + last):
        step(s)


def program(nc, x, x_txt, tok_W, tok_b, tok_pos, embed, W1, b1, W2, b2, w_qkv, b_qkv, w_proj, b_proj,
            w_fc_sh, w_proj_sh, w1, w2, router_w, balance_bias, ident_c, headmask_c, select_c, lower_c, out):
    ctx = ExitStack()
    with ctx:
        def sb(name, shape, dt=F32):
            return ctx.enter_context(nc.sbuf_tensor(name, shape, dt))

        sems = {}

        def sem(name):
            if name not in sems:
                sems[name] = ctx.enter_context(nc.semaphore(name))
            return sems[name]

        def wait(eng, name, value):
            if isinstance(value, int) and value <= 0:
                return
            eng.wait_ge(sem(name), value)

        counts = {}

        def chain(eng, name, ins):
            counts[name] = counts.get(name, 0) + 1
            ins.then_inc(sem(name), 1)
            eng.wait_ge(sem(name), counts[name])

        barriers = {}

        def barrier(eng, name):
            n = barriers.get(name, 0) + 1
            barriers[name] = n
            eng.drain().then_inc(sem("all_engines_done"), 1)
            eng.wait_ge(sem("all_engines_done"), 5 * n)

        h_dram = nc.dram_tensor("h_rows", [T, C], F32, kind="Internal").ap()

        R0 = sb("R0", [P, 4 * T])
        R1 = sb("R1", [P, B * C])
        R2 = sb("R2", [P, 16640])
        M = sb("M", [P, MW])
        ps = ctx.enter_context(nc.psum_tensor("ps", [P, 8, 512], F32))
        used = [0]

        def misc(words, dt=F32, rows=P):
            a = used[0]
            used[0] += words
            assert used[0] <= MW, used[0]
            v = M[0:rows, a:a + words]
            return v if dt == F32 else v.bitcast(dt)

        ident = sb("ident", [P, P])
        ident_b = sb("ident_b", [P, P], BF16)
        headmask = sb("headmask", [P, 2, 16])
        parmask = sb("parmask", [P, 2])
        sc = sb("sc", [P, 64])
        biases = sb("biases", [P, 16])
        ones = sb("ones", [P, P])

        ximg = R0[0:96, 0:2 * 4608].rearrange("p (a c f) -> p a c f", a=2, c=3)
        emb = R0[:, 9216:9216 + 4 * FRONT].rearrange("p (a f) -> p a f", a=4)
        patT = R0[:, 12288:12288 + 2 * 768].rearrange("p (a f) -> p a f", a=2)
        hstage = R1[0:96, 0:2 * 1152].rearrange("p (a w c) -> p a w c", a=2, w=GRID)
        tstage = R1[:, 2304:2304 + 2 * C].rearrange("p (a c) -> p a c", a=2)
        zT = R1[0:96, 2688:2688 + 4 * P].rearrange("p (a m t) -> p a m t", a=2, m=2)
        posb = R1[0:96, 3200:3200 + GRID * C].rearrange("p (w c) -> p w c", w=GRID)
        brow = R1[:, 4352:4352 + 3 * C].rearrange("p (k c) -> p k c", k=3)
        idx = R1[:, 4928:4944].bitcast(I32)
        w_rows = R1[0:96, 5000:5000 + 2 * 2 * FRONT].rearrange("p (a j f) -> p a j f", a=2, j=2)
        w2_rows = R1[0:96, 8072:8072 + 2 * C].rearrange("p (j f) -> p j f", j=2)
        tokT = R2[:, 0:KC * C].rearrange("p (k c) -> p k c", k=KC)
        w1T = R2[:, 1152:1152 + KC * C].rearrange("p (k c) -> p k c", k=KC)
        xp = R2[0:96, 6300:6300 + 2 * 4608].rearrange("p (a c f) -> p a c f", a=2, c=3)
        w2T = R2[0:96, 2304:2304 + 2 * C].rearrange("p (m c) -> p m c", m=2)

        WROWS = [([(0, P, 0)], 0), ([(C, P, 0)], P), ([(P, C1, 0), (C + P, C1, C1)], 2 * P),
                 ([(2 * C, 96, 0)], 2 * C), ([(2 * C + 96, 96, 0)], 2 * C + 96),
                 ([(3 * C, 96, 0)], 0), ([(3 * C + 96, 96, 0)], 96)]
        WJ = [(parts[-1][1] + parts[-1][2], at) for parts, at in WROWS]
        wq_rows = R2[:, 2700:2700 + 7 * 2 * P].rearrange("p (j c) -> p j c", j=7)
        wqT0 = misc(3 * C // 2, F16)
        wqT1 = misc(3 * C // 2, F16)
        wpb0 = misc(C // 2, BF16)
        wpb1 = misc(C // 2, BF16, rows=C1)
        wscale = misc(8)
        wtmp = R2[:, 4500:4500 + 7 * C].rearrange("p (j c) -> p j c", j=7)
        vrow = misc(C)
        prow = misc(C)
        bprow = misc(C)
        bvrow = misc(C)

        yqk = R0[:, 0:3 * T].rearrange("p (k t) -> p k t", k=3)
        yv = R1[0:N, :].rearrange("p (b c) -> p b c", b=B)
        hb = R2[0:N, 0:B * C].rearrange("p (b c) -> p b c", b=B)
        xn = R2[0:N, B * C:B * C + 2 * 4 * 2 * P].rearrange("p (a b c) -> p a b c", a=2, b=4)
        xT = R2[:, 14336:14336 + 3 * 272].bitcast(F16).rearrange("p (a k t) -> p a k t", a=2, k=3)
        mv = R2[0:N, 15152:15152 + 2 * B].rearrange("p (b s) -> p b s", s=2)
        rs = R2[0:N, 15280:15280 + 3 * B].rearrange("p (k b) -> p k b", k=3)
        bst = R2[0:N, 15472:15472 + 6 * B].rearrange("p (b s) -> p b s", s=6)
        extr = misc(4 * 16).rearrange("p (m k g) -> p m k g", m=2, k=2)

        QK0 = R2[:, 0:B * QKW // 2].bitcast(BF16).rearrange("p (b w) -> p b w", b=B)
        QK1 = R2[:, B * QKW // 2:B * QKW].bitcast(BF16).rearrange("p (b w) -> p b w", b=B)
        VQ = R0[0:N, 0:B * C // 2].bitcast(BF16).rearrange("p (b c) -> p b c", b=B)
        QTW = 2 * NQ + NL + N
        qt = R0[:, 3 * T:3 * T + 4 * 8 * QTW // 2].bitcast(F16).rearrange("p (a k b w) -> p a k b w", a=2, k=2, b=8)
        vt = R0[0:N, 8704:8704 + 8 * C].bitcast(F16).rearrange("p (a b c) -> p a b c", a=2, b=8)

        CW = 2 * SLOTS * N
        st0 = misc(4 * QKW, BF16).rearrange("p (a b w) -> p a b w", a=2, b=4)
        st1 = misc(4 * QKW, BF16, rows=C1).rearrange("p (a b w) -> p a b w", a=2, b=4)
        stv = misc(2 * 2 * C, BF16, rows=N).rearrange("p (a b h c) -> p a b h c", a=2, b=2, h=2)
        rowmax = misc(32 * 2 * SLOTS).rearrange("p (g s) -> p g s", g=32)
        gmin = misc(64)
        rmq = misc(32 * SLOTS, F16).rearrange("p (g s) -> p g s", g=32)
        oT = [R1[:, 0:T], R1[0:C1, T:2 * T]]
        w0 = [B * C // 2]

        def r0(words, dt=F32):
            a = w0[0]
            w0[0] += words
            assert w0[0] <= 4 * T
            v = R0[:, a:a + words]
            return v if dt == F32 else v.bitcast(dt)

        w1_ = [2 * T]

        def r1(words, dt=F32):
            a = w1_[0]
            w1_[0] += words
            assert w1_[0] <= B * C
            v = R1[:, a:a + words]
            return v if dt == F32 else v.bitcast(dt)

        def slots(v):
            return v.rearrange("p (s k) -> p s k", k=N)

        Dq = [slots(r0(CW // 2, F16)) for _ in range(2)]
        Qq = [slots(r0(CW // 2, F16)) for _ in range(2)]
        PW = [slots(r0(CW // 2, I16)) for _ in range(2)]
        sq = [slots(r0(CW)) for _ in range(2)]
        wv = [slots(r1(CW)) for _ in range(2)]
        L = [slots(r0(CW)) for _ in range(2)]
        yb = [slots(r1(CW // 2, F16)) for _ in range(2)]
        Pb = [slots(r0(CW // 2, BF16)) for _ in range(2)]
        PT = [r0(SLOTS * P, BF16)[0:N].rearrange("p (b s q) -> p b s q", b=2, s=SLOTS) for _ in range(2)]
        S = misc(3 * 4 * SLOTS).rearrange("p (a k s) -> p a k s", a=2, k=3)
        top = [slots(r0(CW // 2, BF16)) for _ in range(2)]

        def score_slot(b, j):
            if j == PAIRS:
                return 2 + b, 2, 8 + 3 * b + 2
            r = j % 4
            if r < 2:
                k = 2 * b + j // 4
                return r, k, 4 * r + k
            return r, b, 8 + 3 * (r - 2) + b

        PARTS = [(0, 4, 0), (2, 3, 8)]

        def score_part(base, part):
            bank, k, _ = PARTS[part]
            return ps[:, base + bank:base + bank + 2, 0:k * N].rearrange("p a (s k) -> p a s k", k=N)

        pPT = ps[0:N, 4:6, 0:SLOTS * P // 2].bitcast(BF16).rearrange("p b (s q) -> p b s q", s=SLOTS)
        pO = [ps[:, 6, 0:4 * N].rearrange("p (b c t) -> p b c t", b=2, c=2),
              ps[:, 7, 0:4 * N].rearrange("p (b c t) -> p b c t", b=2, c=2)]

        oq = [R0[:, 0:T // 2].bitcast(BF16), R0[0:C1, T // 2:T].bitcast(BF16)]
        y2 = R0[:, T:T + TT * C].rearrange("p (i c) -> p i c", i=TT)
        hf = R0[:, T + TT * C:T + 2 * TT * C].rearrange("p (i c) -> p i c", i=TT)
        xn2 = R1[:, 0:TT * 2 * P].rearrange("p (i c) -> p i c", i=TT)
        CT = R1[0:32, 8704:8704 + T // 2].bitcast(BF16)
        hr = R1[:, 0:7 * 256].rearrange("p (a t) -> p a t", a=HB)
        hc = R1[:, 1792:1792 + 512].rearrange("p (a t) -> p a t", a=2)
        hs = R1[:, 2304:2304 + 512].rearrange("p (a t) -> p a t", a=2)
        hh = [R1[:, 2816 + 896 * k:2816 + 896 * (k + 1)].bitcast(F16).rearrange("p (a t) -> p a t", a=HB) for k in range(2)]
        ost = R1[:, 4608:4608 + 2 * 2 * C].rearrange("p (a i c) -> p a i c", a=2, i=2)
        sel_b = R1[0:32, 11008:11008 + UC * P // 2].bitcast(BF16)
        w1a = R2[:, 8704:8704 + 2 * U]
        w2a = R2[:, 12160:12160 + UC * C].rearrange("p (m c) -> p m c", m=UC)
        w1s = [R2[:, U * k:U * (k + 1)].bitcast(F16) for k in range(2)]
        w2s = [R2[:, 2 * U + 1344 * k:2 * U + 1344 * (k + 1)].bitcast(F16).rearrange("p (m c) -> p m c", m=UC) for k in range(2)]
        XS = R2[:, 6144:6144 + 3 * T // 2].bitcast(F16).rearrange("p (k t) -> p k t", k=3)
        xf = R2[:, 12672:12672 + 1024].rearrange("p (a k i t) -> p a k i t", a=2, k=2, i=2)
        mv2 = R2[:, 14848:14848 + 2 * TT].rearrange("p (i s) -> p i s", s=2)
        rs2 = R2[:, 14920:14920 + 3 * TT].rearrange("p (k i) -> p k i", k=3)
        bst2 = R2[:, 15024:15036].rearrange("p (a s) -> p a s", a=2)
        rwT = R2[:, 15040:15056].rearrange("p (k e) -> p k e", k=2)
        rw_rows = R2[0:E, 15060:15060 + C]
        bbrow = R2[:, 15260:15268]
        scr = [R2[:, 15280 + 272 * k:15280 + 272 * (k + 1)].rearrange("p (i e) -> p i e", e=E) for k in range(4)]
        cmp_a = R0[:, T:T + TT * E * E].rearrange("p (i e f) -> p i e f", e=E, f=E)
        cmp_b = R0[:, T + TT * E * E:T + 2 * TT * E * E].rearrange("p (i e f) -> p i e f", e=E, f=E)
        lower = R0[:, T + 2 * TT * E * E:T + 2 * TT * E * E + E * E]
        sel_w = R0[0:32, T + 2 * TT * E * E + 64:T + 2 * TT * E * E + 64 + UC * P]
        xs = R0[:, 0:768].bitcast(F16).rearrange("p (a k t) -> p a k t", a=2, k=3)
        cts = R0[0:32, 1024:1280].bitcast(BF16).rearrange("p (a t) -> p a t", a=2)
        C3 = misc(TT * 16, BF16).rearrange("p (i e) -> p i e", i=TT)
        csum = misc(2 * TT).rearrange("p (k i) -> p k i", k=2)

        turns = []

        def turn(pieces, rows, cols, dst):
            turns.append((pieces, rows, cols, dst))

        for a, dst in ((0, tokT), (1, w1T)):
            for k in range(KC):
                turn([(w_rows[:, a, j, k * P:(k + 1) * P], 96, j * 96) for j in range(2)], P, C, dst[:, k, :])
        for m in range(2):
            turn([(w2_rows[:, j, m * 96:(m + 1) * 96], 96, j * 96) for j in range(2)], 96, C, w2T[:, m, :])
        for j, (m, at) in enumerate(WJ):
            d0, d1, end = (wqT0, wqT1, 2 * P) if j < 5 else (wpb0, wpb1, C)
            turn([(wq_rows[0:m, j, 0:P], m, 0)], P, m, d0[:, at:at + m])
            turn([(wq_rows[0:m, j, P:end], m, 0)], end - P, m, d1[:, at:at + m])
        for j, row in ((3, vrow), (4, vrow), (5, prow), (6, prow)):
            turn([(None, j, 0)], P, 96, row[:, (1 - j % 2) * 96:(2 - j % 2) * 96])
        wready = []

        def chunk_rows(m):
            return P if m < W2M else C1

        def chunks(steps):
            most = max(lag for _, lag in steps)

            def group(g, par, half):
                for m in range(UC):
                    for fn, lag in steps:
                        if m >= lag:
                            fn(g, m - lag, par, g * UC + m - lag, half)
                        elif not (isinstance(g, int) and g == 0):
                            fn(g - 1, m - lag + UC, 1 - par, g * UC + m - lag, half - 1 + par)

            def run(eng):
                pipeline(eng, [(group, 0)], TT // 2)
                for m in range(most):
                    for fn, lag in steps:
                        if m < lag:
                            g = TT // 2
                            fn(g - 1, m - lag + UC, 1 - g % 2, g * UC + m - lag, (g - 1) // 2)

            return run

        block = ctx.enter_context(nc.Block())

        (Q_MX, Q_NMN, Q_R, Q_INV, Q_CAPM, Q_EV, Q_OD, Q_S, A_MX, A_NMN, A_S, A_INV, A_KK, A_NKK, A_CAP, A_IS,
         A_A, A_IA, A_BH, A_K0, A_CL, A_CB, A_NA, A_SB, O_MX, O_NMN, O_S, O_INV, O_CAPM, O_SC, Y_MX, Y_NMN, Y_S,
         Y_INV, Y_CAPM, T0, T1, T2, G0, G1, A_M16, A_B, A_C, A_K1, A_PB, W_M1, W_M2, W_E1, W_E2,
         W_S1, W_S2, W_U, G2, G3) = range(54)

        QKPARTS = [(yqk[:, 0].rearrange("p (b n) -> p b n", n=N), yqk[:, 1].rearrange("p (b n) -> p b n", n=N),
                    QK0, slice(0, P), slice(0, P)),
                   (yqk[:, 2].rearrange("p (b n) -> p b n", n=N), yqk[:, 2].rearrange("p (b n) -> p b n", n=N),
                    QK1, slice(0, C1), slice(C1, P))]

        def s1(k, rows=P):
            return sc[0:rows, k:k + 1]

        @block.sync
        def _(sp):
            sp.dma_start(ident[:, :], ident_c).then_inc(sem("consts"), 16)
            sp.dma_start(headmask[:, :, :], headmask_c[:, 0:32].rearrange("p (k h) -> p k h", k=2)).then_inc(sem("consts"), 16)
            sp.dma_start(parmask[:, :], headmask_c[:, 32:34]).then_inc(sem("consts"), 16)
            sp.dma_start(w_rows[:, 0], tok_W.rearrange("(j p) f -> p j f", p=96)).then_inc(sem("w_rows"), 16)
            sp.dma_start(w_rows[:, 1], W1.rearrange("(j p) f -> p j f", p=96)).then_inc(sem("w_rows"), 16)
            sp.dma_start(w2_rows[:, :, :], W2.rearrange("(j p) f -> p j f", p=96)).then_inc(sem("w_rows"), 16)
            for j, (parts, _) in enumerate(WROWS):
                for o, m, p0 in parts:
                    src = w_qkv[o:o + m, :] if o < 3 * C else w_proj[o - 3 * C:o - 3 * C + m, :]
                    sp.dma_start(wq_rows[p0:p0 + m, j, 0:C], src).then_inc(sem("wq_rows"), 16)
                    sp.dma_start(wq_rows[p0:p0 + m, j, C:2 * P], src[:, P:C]).then_inc(sem("wq_rows"), 16)
            for b in range(16):
                sp.dma_start(posb[GRID * b:GRID * (b + 1), :, :],
                             tok_pos.rearrange("o (h w) c -> (o h) w c", w=GRID)).then_inc(sem("bias_rows"), 16)
            sp.dma_start(brow[:, 0, :], tok_b.partition_broadcast(P)).then_inc(sem("bias_rows"), 16)
            sp.dma_start(brow[:, 1, :], b2.partition_broadcast(P)).then_inc(sem("bias_rows"), 16)
            sp.dma_start(bprow, b_proj.partition_broadcast(P)).then_inc(sem("bias_rows"), 16)
            sp.dma_start(bvrow, b_qkv[2 * C:3 * C].partition_broadcast(P)).then_inc(sem("bias_rows"), 16)
            sp.dma_start(biases[0:96, 0:2], b1.rearrange("(j p) -> p j", p=96), allow_slow_non_contiguous=True).then_inc(sem("bias_rows"), 16)
            for j in range(3):
                for o, m, p0 in WROWS[j][0]:
                    sp.dma_start(biases[p0:p0 + m, 2 + j:3 + j], b_qkv[o:o + m].rearrange("(p a) -> p a", a=1),
                                 allow_slow_non_contiguous=True).then_inc(sem("bias_rows"), 16)
            xv = x.rearrange("b c (h r) w -> c b h (r w)", h=GRID)

            for q in range(4):
                if q >= 2:
                    sp.wait_ge(sem("by_patch_a"), q - 1)
                    sp.wait_ge(sem("by_patch_b"), q - 1)
                for c in range(3):
                    sp.dma_start(ximg[:, q % 2, c, :], xv[c, 16 * q:16 * q + 16]).then_inc(sem(f"ximg{q % 2}"), 16)
            hv = h_dram.rearrange("(b n) c -> b n c", n=N)
            for q in range(4):
                sp.wait_ge(sem("img_h"), GRID * (q + 1))
                sp.dma_start(hv[16 * q:16 * q + 16, 0:NI, :].rearrange("b (h w) c -> b h (w c)", w=GRID),
                             hstage[:, q % 2].rearrange("p w c -> p (w c)")).then_inc(sem(f"h_stored{q % 2}"), 16)
            for t in range(16):
                sp.wait_ge(sem("txt_h"), t + 1)
                sp.dma_start(hv[4 * t:4 * t + 4, NI:N, :], tstage[:, t % 2, :]).then_inc(sem(f"t_stored{t % 2}"), 16)
            for a in range(2):
                sp.wait_ge(sem(f"h_stored{a}"), 32)
                sp.wait_ge(sem(f"t_stored{a}"), 128)
            barrier(sp, "sp")
            for q in range(4):
                sp.dma_start(hb[:, 16 * q:16 * q + 16, :],
                             hv[16 * q:16 * q + 16].rearrange("b n c -> n b c")).then_inc(sem(f"hb{q}"), 16)
            barrier(sp, "sp")
            def load_seqs(par, b, n):
                sp.dma_start(st0[:, par, 0:n], QK0[:, b, :]).then_inc(sem(f"st_qk{par}"), 16)
                sp.dma_start(st1[:, par, 0:n, 0:3 * NQ], QK1[0:C1, b, 0:3 * NQ]).then_inc(sem(f"st_qk{par}"), 16)
                sp.dma_start(st1[:, par, 0:n, 3 * NQ:QKW], QK1[C1:P, b, 3 * NQ:QKW]).then_inc(sem(f"st_qk{par}"), 16)

            def load_four(g, par, half):
                if par == 0:
                    sp.wait_ge(sem("qk_chunk"), half + 1)
                else:
                    wait(sp, "scored", (g - 1) * 2)
                load_seqs(par, bass.ds(g * 4, 4), 4)

            def load_two(g, par, half):
                wait(sp, "scored", 32 + g - 1)
                load_seqs(par, bass.ds(g * 2, 2), 2)

            pipeline(sp, [(load_four, 0)], 16)
            barrier(sp, "sp")
            pipeline(sp, [(load_two, 0)], 32)
            barrier(sp, "sp")
            sp.dma_start(hf, h_dram.rearrange("(i p) c -> p i c", p=P)).then_inc(sem("hf"), 16)
            for e in range(E + 1):
                src = w1[e] if e < E else w_fc_sh
                sp.dma_start(w1a[:, e * C:(e + 1) * C], src[0:P, :]).then_inc(sem("ffn_w"), 16)
                for k in range(2):
                    sp.dma_start(w1a[C1 * k:C1 * (k + 1), U + e * C:U + (e + 1) * C], src[P:C, :]).then_inc(sem("ffn_w"), 16)
            sp.dma_start(w2a[:, 0:UC - 2, :], w2.rearrange("e h c -> (e h) c").rearrange("(m p) c -> p m c", p=P)).then_inc(sem("ffn_w"), 16)
            sp.dma_start(w2a[:, UC - 2, :], w_proj_sh[0:P, :]).then_inc(sem("ffn_w"), 16)
            sp.dma_start(w2a[0:C1, UC - 1, :], w_proj_sh[P:C, :]).then_inc(sem("ffn_w"), 16)
            sp.dma_start(rw_rows, router_w).then_inc(sem("ffn_w"), 16)
            sp.dma_start(bbrow, balance_bias.partition_broadcast(P)).then_inc(sem("ffn_w"), 16)
            barrier(sp, "sp")
            sp.dma_start(lower, lower_c.partition_broadcast(P)).then_inc(sem("ffn_c"), 16)
            sp.dma_start(sel_w, select_c).then_inc(sem("ffn_c"), 16)
            barrier(sp, "sp")
            ov = out.rearrange("b n c -> (b n) c").rearrange("(i p) c -> p i c", p=P)

            def store(g, par, half):
                sp.wait_ge(sem("out_ready"), g + 1)
                sp.dma_start(ov[:, bass.ds(g * 2, 2), :], ost[:, par]).then_inc(sem(f"stored{par}"), 16)

            def load_x(g, par, half):
                wait(sp, "h_used", (g - 1) * UC)
                t = bass.ds(g * 256, 256)
                sp.dma_start(xs[:, par], XS[:, :, t]).then_inc(sem(f"xs{par}"), 16)
                sp.dma_start(cts[:, par], CT[:, t]).then_inc(sem(f"xs{par}"), 16)

            pipeline(sp, [(load_x, 0), (store, 2)], TT // 2)
            sp.wait_ge(sem("stored0"), 16 * 9)
            sp.wait_ge(sem("stored1"), 16 * 8)

        @block.gpsimd
        def _(pool):
            pool.dma_start(idx, x_txt.rearrange("b s -> (b s)").rearrange("(t p) -> p t", p=P),
                           allow_slow_non_contiguous=True).then_inc(sem("idx"), 16)
            pool.wait_ge(sem("idx"), 16)
            for t in range(16):
                if t >= 4:
                    pool.wait_ge(sem("pat_psum"), 24 + t - 3)
                pool.indirect_dma_start(emb[:, t % 4, :], None, embed,
                                        bass.IndirectOffsetOnAxis(ap=idx[:, t:t + 1], axis=0)).then_inc(sem(f"emb{t % 4}"), 16)
            barrier(pool, "pool")

            def reduce_pair(k, name):
                pool.wait_ge(sem(name), 1)
                pool.partition_all_reduce(sc[:, G0:G0 + 2], sc[:, k:k + 2], P, RMAX).then_inc(sem("reduced"), 1)

            def normalise(g, par, half):
                if isinstance(g, int) and g == 0:
                    pool.wait_ge(sem("ln_done"), 1)
                wait(pool, "x_psum", g - 1)
                b4 = bass.ds(g * 4, 4)
                v = xn[:, par, :, 0:C]
                pool.tensor_tensor(v, hb[:, b4, :], mv[:, b4, 0:1].to_broadcast([N, 4, C]), ALU.subtract).then_inc(sem("centred"), 1)
                pool.wait_ge(sem("centred"), g + 1)
                pool.tensor_tensor(v, v, rs[:, 2, b4].unsqueeze(2).to_broadcast([N, 4, C]), ALU.mult).then_inc(sem("xn"), 1)

            def v_bias(g, par, half):
                pool.wait_ge(sem("v_scaled"), g * 2 + 2)
                v = yv[:, bass.ds(g * 4, 4), :]
                pool.tensor_tensor(v, v, bvrow[0:N, :].unsqueeze(1).to_broadcast([N, 4, C]), ALU.add).then_inc(sem("v_stored"), 1)

            pipeline(pool, [(normalise, 0), (v_bias, 2)], 16)
            reduce_pair(Q_MX, "q_minmax")
            barrier(pool, "pool")

            def leftovers(c, par, half):
                pool.wait_ge(sem("q_rounded"), c + 1)
                for k, (_, _, QK, rows, _) in enumerate(QKPARTS):
                    if k == 1:
                        wait(pool, "scored", 4 * c - 2)
                    last = pool.tensor_tensor(QK[rows, bass.ds(c * 8, 8), 2 * NQ:3 * NQ].rearrange("p b (h i) -> p b h i", i=NL),
                                              qt[rows, par, k, :, 2 * NQ:2 * NQ + NL].unsqueeze(2).to_broadcast([rows.stop, 8, 16, NL]),
                                              headmask[rows, k, :].unsqueeze(1).unsqueeze(3).to_broadcast([rows.stop, 8, 16, NL]),
                                              ALU.mult)
                last.then_inc(sem("qk_chunk"), 1)

            pipeline(pool, [(leftovers, 0)], 8)
            reduce_pair(A_MX, "a_minmax")
            barrier(pool, "pool")

            def quotient_bits(g, par, half):
                pool.wait_ge(sem("total"), g + 1)
                pool.tensor_tensor(L[par].bitcast(I32), L[par].bitcast(I32), wv[par].bitcast(I32), ALU.subtract).then_inc(sem("log2"), 1)
                wait(pool, "probs", g - 1)
                pool.tensor_tensor(top[par], wv[par], S[:, par, 2, :].unsqueeze(2).to_broadcast([P, 2 * SLOTS, N]),
                                   ALU.subtract).then_inc(sem("excess"), 1)

            def spread_v(g, par, half):
                wait(pool, "o_summed", g - 1)
                for a in range(2):
                    last = pool.tensor_copy(stv[:, par, :, a].rearrange("p b (j h d) -> p b j h d", h=2, d=HD)[:, :, :, a, :],
                                            VQ[:, bass.ds(g * 2, 2), :].rearrange("p b (j h d) -> p b j h d", h=2, d=HD)[:, :, :, a, :])
                last.then_inc(sem("v_spread"), 1)

            pool.memset(stv, 0.0).then_inc(sem("v_cleared"), 1)
            pool.wait_ge(sem("v_cleared"), 1)
            pipeline(pool, [(quotient_bits, 0), (spread_v, 2)], 32)
            barrier(pool, "pool")
            reduce_pair(O_MX, "o_minmax")
            pool.wait_ge(sem("w_max"), 1)
            pool.partition_all_reduce(sc[:, G2:G3 + 1], sc[:, W_M1:W_M2 + 1], P, RMAX).then_inc(sem("w_reduced"), 1)
            def low_part(dst, ws, high, n):
                pool.wait_ge(sem("w_high"), n)
                pool.tensor_tensor(dst, ws, high, ALU.subtract).then_inc(sem("w_low"), 1)

            low_part(w1s[1], w1a, w1s[0], 1)
            low_part(w2s[1][:, 0:W2M, :], w2a[:, 0:W2M, :], w2s[0][:, 0:W2M, :], 2)
            low_part(w2s[1][0:C1, W2M, :], w2a[0:C1, W2M, :], w2s[0][0:C1, W2M, :], 3)
            pool.wait_ge(sem("y2_minmax"), 1)
            pool.partition_all_reduce(sc[:, G0:G0 + 2], sc[:, Y_MX:Y_MX + 2], P, RMAX).then_inc(sem("reduced"), 1)
            barrier(pool, "pool")
            barrier(pool, "pool")

            def square(g, m, par, n, half):
                rows = chunk_rows(m)
                pool.wait_ge(sem("weighted"), n + 1)
                wait(pool, "low", n - 1)
                pool.tensor_tensor(hs[0:rows, m % 2, :], hr[0:rows, m % HB, :], hc[0:rows, m % 2, :], ALU.mult).then_inc(sem("squared"), 1)

            chunks([(square, 0)])(pool)

        @block.scalar
        def _(act):
            def copy(out_, in_):
                return act.activation(out_, in_, ACT.Copy)

            def ident_(out_, in_, scale=1.0, bias=0.0):
                return act.activation(out_, in_, ACT.Identity, scale=scale, bias=bias)

            act.wait_ge(sem("consts"), 48)
            copy(ident_b[:, :], ident[:, :]).then_inc(sem("ident_b"), 1)
            act.wait_ge(sem("bias_rows"), 16 * 25)
            def by_patch(q, c):
                act.wait_ge(sem(f"ximg{q % 2}"), 48 * (q // 2 + 1))
                wait(act, "pat_psum", (q - 1) * GRID)
                return copy(xp[:, q % 2, c].rearrange("p (w r v) -> p w r v", w=GRID, v=PATCH),
                            ximg[:, q % 2, c].rearrange("p (r w v) -> p w r v", w=GRID, v=PATCH))

            by_patch(0, 0).then_inc(sem("by_patch_a"), 1)
            for q in range(4):
                if q < 3:
                    by_patch(q + 1, 0).then_inc(sem("by_patch_a"), 1)
                for wp in range(GRID):
                    n = q * GRID + wp
                    act.wait_ge(sem("pat_psum"), n + 1)
                    wait(act, "h_out", n - 1)
                    copy(patT[:, n % 2, 0:288], ps[:, 0, 0:288]).then_inc(sem("patT_a"), 1)
            for t in range(16):
                n = 24 + t
                act.wait_ge(sem("pat_psum"), n + 1)
                wait(act, "h_out", n - 1)
                copy(patT[:, n % 2, 0:384], ps[:, 0, 0:384]).then_inc(sem("patT_a"), 1)
                act.wait_ge(sem("z_psum"), t + 1)
                wait(act, "h_out", 24 + t - 1 if t >= 2 else 0)
                for m in range(2):
                    last = act.activation(zT[:, t % 2, m, :], ps[0:96, 4, m * P:(m + 1) * P], ACT.Gelu, bias=biases[0:96, m:m + 1])
                last.then_inc(sem("zT"), 1)
            barrier(act, "act")
            act.wait_ge(sem("ln_var"), 1)
            act.activation(rs[:, 1, :], rs[:, 0, :], ACT.Sqrt).then_inc(sem("ln_sqrt"), 1)

            def twice(g, par, half):
                act.wait_ge(sem("xn"), g + 1)
                copy(xn[:, par, :, C:2 * P], xn[:, par, :, P:C]).then_inc(sem("xn_twice"), 1)

            def x_high(g, par, half):
                act.wait_ge(sem("x_psum"), g + 1)
                wait(act, "v_psum", (g - 1) * 2)
                act.activation(xT[:, par, 0:3:2, :], ps[:, 0:2, 0:272], ACT.Copy, scale=X_UNIT).then_inc(sem("x_high"), 1)

            def evac_qk(g, par, half):
                act.wait_ge(sem("qk_psum"), g + 1)
                cols = bass.ds(g * 272, 272)
                for j in range(3):
                    last = ident_(yqk[:, j, cols], ps[:, 2 + j, 0:272], scale=wscale[:, j:j + 1], bias=biases[:, 2 + j:3 + j])
                last.then_inc(sem("qk_stored"), 1)

            pipeline(act, [(twice, 0), (x_high, 0), (evac_qk, 1)], 16)
            barrier(act, "act")
            def to_halves(c, par, half):
                wait(act, "qk_chunk", c - 1)
                b8 = bass.ds(c * 8, 8)
                for k, (q, kk, _, rows, krows) in enumerate(QKPARTS):
                    t = qt[:, par, k]
                    for dst, src, r, scale in ((t[rows, :, 0:NQ], q[rows, b8, 0:NQ], rows, Q_EV),
                                               (t[rows, :, NQ:2 * NQ], q[rows, b8, 0:NQ], rows, Q_OD),
                                               (t[rows, :, 2 * NQ:2 * NQ + NL], q[rows, b8, NQ:N], rows, Q_INV),
                                               (t[krows, :, 2 * NQ + NL:QTW], kk[krows, b8, :], krows, Q_INV)):
                        last = ident_(dst, src, scale=sc[r, scale:scale + 1], bias=sc[r, T2:T2 + 1])
                last.then_inc(sem("q_added"), 1)

            pipeline(act, [(to_halves, 0)], 8)
            act.wait_ge(sem("qk_chunk"), 8)
            for n in range(8):
                wait(act, "v_rounded", n - 1)
                ident_(vt[:, n % 2], yv[:, 8 * n:8 * n + 8, :], scale=s1(Q_INV, N), bias=s1(T2, N)).then_inc(sem("v_added"), 1)
            barrier(act, "act")
            ident_(rmq[:, :, :], rowmax[:, :, :], scale=s1(A_KK), bias=s1(A_M16)).then_inc(sem("rmq"), 1)

            def squares(g, par, half):
                act.wait_ge(sem("rem"), g + 1)
                act.activation(sq[par], sq[par], ACT.Square, bias=s1(A_BH)).then_inc(sem("sq"), 1)

            def signs(g, par, half):
                act.wait_ge(sem("excess"), g + 1)
                act.activation(top[par], top[par], ACT.Sign).then_inc(sem("top"), 1)

            def powers(g, par, half):
                act.wait_ge(sem("quot"), g + 1)
                wait(act, "w", g - 1)
                ident_(PW[par], Qq[par], scale=-128.0, bias=s1(A_PB)).then_inc(sem("power"), 1)

            def exponent(g, par, half):
                act.wait_ge(sem("log2"), g + 1)
                wait(act, "pbits", g - 1)
                ident_(yb[par], L[par].bitcast(I32), scale=2.0 ** -23, bias=s1(A_CB)).then_inc(sem("exponent"), 1)

            def evac_pt(g, par, half):
                act.wait_ge(sem("pt_psum"), g + 1)
                wait(act, "o_summed", g - 1)
                copy(PT[par], pPT).then_inc(sem("PT"), 1)

            def evac_o(g, par, half):
                act.wait_ge(sem("o_summed"), g + 1)
                b = bass.ds(g * 2, 2)
                copy(oT[0].rearrange("p (b n) -> p b n", n=N)[:, b, :], pO[par][:, :, 0, :])
                copy(oT[1].rearrange("p (b n) -> p b n", n=N)[:, b, :], pO[par][0:C1, :, 1, :]).then_inc(sem("o_out"), 1)

            pipeline(act, [(powers, 0), (squares, 0), (evac_pt, 3), (exponent, 1), (signs, 1), (evac_o, 4)], 32)
            barrier(act, "act")
            act.wait_ge(sem("o_scalars"), 1)
            ident_(oT[0], oT[0], scale=s1(O_SC), bias=s1(T2)).then_inc(sem("o_added"), 1)
            ident_(oT[1], oT[1], scale=s1(O_SC, C1), bias=s1(T2, C1)).then_inc(sem("o_added"), 1)
            act.wait_ge(sem("w_unit"), 1)
            act.wait_ge(sem("ffn_w"), 16 * 32)
            for ws, high, s_ in ((w1a, w1s[0], W_S1), (w2a[:, 0:W2M, :], w2s[0][:, 0:W2M, :], W_S2),
                                 (w2a[0:C1, W2M, :], w2s[0][0:C1, W2M, :], W_S2)):
                chain(act, "scalar_step", ident_(ws, ws, scale=s1(s_, ws.shape[0])))
                copy(high, ws).then_inc(sem("w_high"), 1)
            act.wait_ge(sem("ln2_var"), 1)
            act.activation(rs2[:, 1, :], rs2[:, 0, :], ACT.Sqrt).then_inc(sem("ln2_sqrt"), 1)
            act.wait_ge(sem("xn2"), 1)
            copy(xn2[:, :, C:2 * P], xn2[:, :, P:C])
            barrier(act, "act")
            act.wait_ge(sem("rw_psum"), 1)
            copy(rwT[:, 0, :], ps[:, 5, 0:E])
            copy(rwT[0:C1, 1, :], ps[0:C1, 5, E:2 * E]).then_inc(sem("rwT"), 1)
            for i in range(TT // 2):
                act.wait_ge(sem("x2_psum"), i + 1)
                wait(act, "routed", i - 1)
                src = ps[:, i % 2, :].rearrange("p (k i t) -> p k i t", k=2, i=2)
                copy(xf[:, i % 2], src).then_inc(sem("xf"), 1)
                act.activation(XS[:, 0:3:2, 2 * P * i:2 * P * (i + 1)].rearrange("p k (i t) -> p k i t", i=2), src,
                               ACT.Copy, scale=X_UNIT).then_inc(sem("X_high"), 1)
            act.wait_ge(sem("routed"), TT // 2)
            act.activation(scr[0], ps[:, 2, 0:TT * E].rearrange("p (i e) -> p i e", e=E), ACT.Sigmoid).then_inc(sem("sigmoid"), 1)
            act.wait_ge(sem("ffn_c"), 32)
            copy(sel_b, sel_w).then_inc(sem("sel_b"), 1)
            for q in range(5):
                act.wait_ge(sem("ct_psum"), q + 1)
                n = min(8, TT - 8 * q) * P
                copy(CT[:, 1024 * q:1024 * q + n], ps[0:32, 3 + q % 2, 0:n // 2].bitcast(BF16)).then_inc(sem("CT"), 1)
            barrier(act, "act")

            def relu(g, m, par, n, half):
                rows = chunk_rows(m)
                act.wait_ge(sem("h_psum"), n + 1)
                wait(act, "squared", n - HB + 1)
                act.activation(hr[0:rows, m % HB, :], ps[0:rows, m % 2, 0:256], ACT.Relu, scale=H_UNIT).then_inc(sem("relu"), 1)

            def high(g, m, par, n, half):
                rows = chunk_rows(m)
                act.wait_ge(sem("squared"), n + 1)
                wait(act, "h_used", n - HB + 1)
                copy(hh[0][0:rows, m % HB, :], hs[0:rows, m % 2, :]).then_inc(sem("high"), 1)

            chunks([(high, 2), (relu, 0)])(act)

        @block.vector
        def _(dve):
            def ch(ins):
                chain(dve, "vector_step", ins)

            ts = dve.tensor_scalar
            tt = dve.tensor_tensor
            dve.wait_ge(sem("bias_rows"), 16 * 25)
            for wp in range(GRID):
                last = tt(posb[:, wp, :], posb[:, wp, :], brow[0:96, 0, :], ALU.add)
            ch(last)
            dve.wait_ge(sem("wq_rows"), 16 * 16)
            mxw, mnw, nzw, inw = (wtmp[:, k, 0:8] for k in range(4))
            ch(dve.memset(wtmp[:, 0:6, :], 0.0))
            ch(dve.memset(wscale, 1.0))
            for j, (m, _) in enumerate(WJ):
                dve.tensor_reduce(mxw[0:m, j:j + 1], wq_rows[0:m, j, :], X, ALU.max)
                last = dve.tensor_reduce(mnw[0:m, j:j + 1], wq_rows[0:m, j, :], X, ALU.min)
            ch(last)
            ch(ts(mxw, mxw, 0.0, None, ALU.max))
            ch(ts(mnw, mnw, 0.0, None, ALU.min))
            ch(tt(wscale, mxw, mnw, ALU.subtract))
            ch(ts(wscale, wscale, 1.0 / 255.0, EPS_Q, ALU.mult, ALU.max))
            ch(dve.reciprocal(inw, wscale))
            ch(tt(nzw, mnw, inw, ALU.mult))
            ch(ts(nzw, nzw, MAGIC, MAGIC, ALU.add, ALU.subtract))
            ch(ts(nzw, nzw, 255.0, MAGIC, ALU.add, ALU.add))
            for j, (m, _) in enumerate(WJ):
                w = wq_rows[0:m, j, :]
                ch(ts(w, w, inw[0:m, j:j + 1], MAGIC, ALU.mult, ALU.add))
                ch(ts(w, w, nzw[0:m, j:j + 1], MAGIC, ALU.min, ALU.subtract))
            ch(ts(wscale[:, 0:5], wscale[:, 0:5], 1.0 / X_UNIT, None, ALU.mult))
            for j in (3, 4, 5, 6):
                ch(ts(wtmp[0:96, j, 0:96], ident[0:96, 0:96], wscale[0:96, j:j + 1], None, ALU.mult))
            ch(dve.memset(ones[:, :], 1.0))
            wready.append(counts["vector_step"])
            for n, (_, rows, cols, dst) in enumerate(turns):
                dve.wait_ge(sem("w_psum"), n + 1)
                dve.tensor_copy(dst, ps[0:rows, n % 2, 0:cols]).then_inc(sem("w_turned"), 1)
            def by_patch(q):
                dve.wait_ge(sem(f"ximg{q % 2}"), 48 * (q // 2 + 1))
                wait(dve, "pat_psum", (q - 1) * GRID)
                for c in (1, 2):
                    last = dve.tensor_copy(xp[:, q % 2, c].rearrange("p (w r v) -> p w r v", w=GRID, v=PATCH),
                                           ximg[:, q % 2, c].rearrange("p (r w v) -> p w r v", w=GRID, v=PATCH))
                last.then_inc(sem("by_patch_b"), 1)

            by_patch(0)
            for q in range(4):
                if q < 3:
                    by_patch(q + 1)
                for wp in range(GRID):
                    n = q * GRID + wp
                    dve.wait_ge(sem("pat_psum"), n + 1)
                    wait(dve, "h_out", n - 1)
                    dve.tensor_copy(patT[:, n % 2, 288:576], ps[:, 1, 0:288]).then_inc(sem("patT_b"), 1)
                    dve.wait_ge(sem("h_out"), n + 1)
                    if q >= 2 and wp == 0:
                        dve.wait_ge(sem(f"h_stored{q % 2}"), 16 * (q // 2))
                    tt(hstage[:, q % 2, wp, :], ps[0:96, 2 + n % 2, 0:C], posb[:, wp, :], ALU.add).then_inc(sem("img_h"), 1)
            for t in range(16):
                n = 24 + t
                dve.wait_ge(sem("pat_psum"), n + 1)
                wait(dve, "h_out", n - 1)
                dve.tensor_copy(patT[:, n % 2, 384:768], ps[:, 1, 0:384]).then_inc(sem("patT_b"), 1)
                dve.wait_ge(sem("h_out"), n + 1)
                if t >= 2:
                    dve.wait_ge(sem(f"t_stored{t % 2}"), 16 * (t // 2))
                tt(tstage[:, t % 2, :], ps[:, 2 + n % 2, 0:C], brow[:, 1, :], ALU.add).then_inc(sem("txt_h"), 1)
            barrier(dve, "dve")

            for b in range(B):
                if b % 16 == 0:
                    dve.wait_ge(sem(f"hb{b // 16}"), 16)
                last = dve.bn_stats(bst[:, b, :], hb[:, b, :])
            ch(last)
            for b in range(B):
                last = dve.bn_aggr(mv[:, b, :], bst[:, b, :])
            ch(last)

            def inverse_deviation(var, r, name):
                ch(ts(r[:, 0, :], var, EPS_LN, None, ALU.add))
                ch(ts(r[:, 2, :], r[:, 0, :], 1.0, None, ALU.mult))
                dve.drain().then_inc(sem(f"{name}_var"), 1)
                dve.wait_ge(sem(f"{name}_sqrt"), 1)
                ch(dve.reciprocal(r[:, 2, :], r[:, 1, :]))
                ch(tt(r[:, 2, :], r[:, 2, :], r[:, 0, :], ALU.mult))
                ch(tt(r[:, 1, :], r[:, 1, :], r[:, 2, :], ALU.add))
                ch(ts(r[:, 1, :], r[:, 1, :], 0.5, None, ALU.mult))
                ch(dve.reciprocal(r[:, 2, :], r[:, 1, :]))

            inverse_deviation(mv[:, :, 1], rs, "ln")

            dve.drain().then_inc(sem("ln_done"), 1)
            ch(dve.memset(extr, 0.0))

            def x_low(g, par, half):
                dve.wait_ge(sem("x_high"), g + 1)
                dve.scalar_tensor_tensor(xT[:, par, 1, :], ps[:, 0, 0:272], X_UNIT, xT[:, par, 0, :], ALU.mult, ALU.subtract)
                dve.scalar_tensor_tensor(xT[C1:P, par, 2, :], ps[C1:P, 1, 0:272], X_UNIT, xT[C1:P, par, 2, :],
                                         ALU.mult, ALU.subtract).then_inc(sem("xT"), 1)

            def scale_v(g, par, half):
                for k in range(2):
                    dve.wait_ge(sem("v_psum"), g * 2 + k + 1)
                    tt(yv[:, bass.ds(g * 4 + 2 * k, 2), :], ps[0:N, 5 + k, 0:2 * C].rearrange("p (b c) -> p b c", b=2),
                       vrow[0:N, :].unsqueeze(1).to_broadcast([N, 2, C]), ALU.mult).then_inc(sem("v_scaled"), 1)

            def extremes_qkv(g, par, half):
                dve.wait_ge(sem("qk_stored"), g + 1)
                dve.wait_ge(sem("v_stored"), g + 1)
                qk, v = yqk[:, :, bass.ds(g * 272, 272)], yv[:, bass.ds(g * 4, 4), :]
                at = bass.ds(g, 1)
                dve.tensor_reduce(extr[:, 0, 0, at], qk, XY, ALU.max)
                dve.tensor_reduce(extr[:, 1, 0, at], qk, XY, ALU.min)
                dve.tensor_reduce(extr[0:N, 0, 1, at], v, XY, ALU.max)
                dve.tensor_reduce(extr[0:N, 1, 1, at], v, XY, ALU.min).then_inc(sem("qkv_extremes"), 1)

            pipeline(dve, [(x_low, 0), (scale_v, 1), (extremes_qkv, 3)], 16)
            dve.wait_ge(sem("qkv_extremes"), 16)

            def minmax(parts, k):
                ch(dve.memset(sc[:, T0:T1 + 1], 0.0))
                ch(dve.memset(sc[:, k:k + 2], 0.0))
                for rows, part, axis in parts:
                    ch(dve.tensor_reduce(sc[0:rows, T0:T0 + 1], part, axis, ALU.max))
                    ch(dve.tensor_reduce(sc[0:rows, T1:T1 + 1], part, axis, ALU.min, negate=True))
                    ch(tt(sc[0:rows, k:k + 2], sc[0:rows, k:k + 2], sc[0:rows, T0:T0 + 2], ALU.max))

            def scale_of(mx, nmn, s, inv, capm):
                ch(tt(s1(T0), s1(mx), s1(nmn), ALU.add))
                ch(ts(s1(s), s1(T0), 1.0 / 255.0, EPS_Q, ALU.mult, ALU.max))
                ch(dve.reciprocal(s1(inv), s1(s)))
                ch(tt(s1(T0), s1(nmn), s1(inv), ALU.mult))
                ch(ts(s1(T0), s1(T0), MAGIC, MAGIC, ALU.add, ALU.subtract))
                ch(ts(s1(capm), s1(T0), -1.0, 255.0, ALU.mult, ALU.add))

            dve.tensor_reduce(s1(Q_MX), extr[:, 0], XY, ALU.max)
            ch(dve.tensor_reduce(s1(Q_NMN), extr[:, 1], XY, ALU.min, negate=True))
            dve.drain().then_inc(sem("q_minmax"), 1)
            dve.wait_ge(sem("reduced"), 1)
            ch(dve.tensor_copy(sc[:, Q_MX:Q_MX + 2], sc[:, G0:G0 + 2]))
            scale_of(Q_MX, Q_NMN, Q_S, Q_INV, Q_CAPM)
            ch(ts(s1(Q_CAPM), s1(Q_CAPM), H16 + 512.0, None, ALU.add))
            ch(tt(s1(Q_EV), s1(Q_INV), parmask[:, 0:1], ALU.mult))
            ch(tt(s1(Q_OD), s1(Q_INV), parmask[:, 1:2], ALU.mult))
            ch(dve.memset(s1(T2), H16 + 512.0))
            barrier(dve, "dve")
            def to_whole(c, par, half):
                dve.wait_ge(sem("q_added"), c + 1)
                b8 = bass.ds(c * 8, 8)
                for k, (_, _, QK, rows, krows) in enumerate(QKPARTS):
                    t = qt[:, par, k]
                    for dst, src, r in ((QK[rows, b8, 0:2 * NQ], t[rows, :, 0:2 * NQ], rows),
                                        (QK[krows, b8, 3 * NQ:QKW], t[krows, :, 2 * NQ + NL:QTW], krows),
                                        (t[rows, :, 2 * NQ:2 * NQ + NL], t[rows, :, 2 * NQ:2 * NQ + NL], rows)):
                        last = ts(dst, src, sc[r, Q_CAPM:Q_CAPM + 1], H16 + 512.0, ALU.min, ALU.subtract)
                last.then_inc(sem("q_rounded"), 1)

            def extremes(c, par, half):
                for i in range(4):
                    g = c * 4 + i
                    dve.wait_ge(sem("scored"), g + 1)
                    for part, (_, k, s0) in enumerate(PARTS):
                        sv = score_part(4 * (i % 2), part)
                        dve.tensor_reduce(rowmax[:, bass.ds(g, 1), s0:s0 + 2 * k].rearrange("p o (a s) -> p (o a) s", a=2), sv, X, ALU.max)
                        last = dve.tensor_reduce(gmin[:, bass.ds(g * 2 + part, 1)], sv, mybir.AxisListType.XYZ, ALU.min)
                    last.then_inc(sem("extremes"), 1)

            pipeline(dve, [(to_whole, 0), (extremes, 1)], 8)
            for n in range(8):
                dve.wait_ge(sem("v_added"), n + 1)
                ts(VQ[:, 8 * n:8 * n + 8, :], vt[:, n % 2], s1(Q_CAPM, N), H16 + 512.0, ALU.min, ALU.subtract).then_inc(sem("v_rounded"), 1)
            dve.wait_ge(sem("extremes"), 32)
            ch(dve.tensor_reduce(s1(A_MX), rowmax, XY, ALU.max))
            ch(ts(s1(A_MX), s1(A_MX), 0.0, None, ALU.max))
            ch(dve.tensor_reduce(s1(A_NMN), gmin, X, ALU.min, negate=True))
            ch(ts(s1(A_NMN), s1(A_NMN), 0.0, None, ALU.max))
            dve.drain().then_inc(sem("a_minmax"), 1)
            dve.wait_ge(sem("reduced"), 2)
            ch(tt(s1(A_K1), s1(Q_S), s1(Q_S), ALU.mult))
            ch(ts(s1(A_K1), s1(A_K1), HD ** -0.5, None, ALU.mult))
            ch(ts(sc[:, A_MX:A_MX + 2], sc[:, G0:G0 + 2], s1(A_K1), None, ALU.mult))
            scale_of(A_MX, A_NMN, A_S, A_INV, A_CAP)
            ch(ts(s1(A_CAP), s1(A_CAP), H16 + 512.0, None, ALU.add))
            ch(dve.memset(s1(A_M16), H16 + 512.0))
            ch(tt(s1(A_KK), s1(A_K1), s1(A_INV), ALU.mult))
            ch(ts(s1(A_NKK), s1(A_KK), -1.0, None, ALU.mult))
            ch(dve.reciprocal(s1(A_IS), s1(A_S)))

            def floor_(k, tmp):
                ch(ts(s1(tmp), s1(k), MAGIC, MAGIC, ALU.add, ALU.subtract))
                ch(tt(s1(T1), s1(tmp), s1(k), ALU.is_gt))
                ch(tt(s1(tmp), s1(tmp), s1(T1), ALU.subtract))
                ch(ts(s1(T1), s1(k), 4194304.0, None, ALU.is_gt))
                ch(tt(s1(T0), s1(k), s1(tmp), ALU.subtract))
                ch(tt(s1(T0), s1(T0), s1(T1), ALU.mult))
                ch(tt(s1(k), s1(tmp), s1(T0), ALU.add))

            ch(ts(s1(A_A), s1(A_IS), 0.6931, 1e6, ALU.mult, ALU.min))
            ch(ts(s1(A_B), s1(A_A), MAGIC, MAGIC, ALU.add, ALU.subtract))
            ch(tt(s1(T1), s1(A_A), s1(A_B), ALU.is_gt))
            ch(tt(s1(A_A), s1(A_B), s1(T1), ALU.add))
            ch(ts(s1(A_A), s1(A_A), 256.0, None, ALU.min))
            ch(dve.reciprocal(s1(A_IA), s1(A_A)))
            ch(ts(s1(A_NA), s1(A_A), -1.0, None, ALU.mult))
            ch(ts(s1(A_B), s1(A_IS), 0.96963238 / C0, None, ALU.mult))
            floor_(A_B, T2)
            ch(tt(s1(A_C), s1(A_IS), s1(A_IS), ALU.mult))
            ch(ts(s1(A_C), s1(A_C), 1.0 / C0, None, ALU.mult))
            floor_(A_C, T2)
            ch(ts(s1(A_BH), s1(A_A), H16, -H16, ALU.mult, ALU.add))
            ch(ts(s1(T0), s1(A_B), 0.5, None, ALU.mult))
            ch(tt(s1(A_BH), s1(A_BH), s1(T0), ALU.subtract))
            ch(tt(s1(T0), s1(T0), s1(T0), ALU.mult))
            ch(tt(s1(A_K0), s1(A_C), s1(T0), ALU.subtract))
            ch(ts(s1(A_CL), s1(A_A), 30.0, H16, ALU.mult, ALU.add))
            ch(ts(s1(A_SB), s1(A_IA), -H16, H16 - 0.5 + 2.0 ** -10, ALU.mult, ALU.add))
            ch(dve.memset(s1(A_CB), H16 + 1.5 + 2.0 ** -12))
            ch(dve.memset(s1(A_PB), 128.0 * (127.0 + 1.0 + H16) + 64.0))
            barrier(dve, "dve")
            dve.wait_ge(sem("rmq"), 1)
            ch(ts(rmq, rmq, s1(A_CAP), None, ALU.min))
            ch(ts(rmq, rmq, -512.0, None, ALU.add))

            def front(g, par, half):
                dve.wait_ge(sem("scored"), 32 + g + 1)
                D, Q = Dq[par], Qq[par]
                for part, (_, k, s0) in enumerate(PARTS):
                    m = rmq[:, bass.ds(g, 1), s0:s0 + 2 * k].rearrange("p o (a s) -> p (o a) s", a=2)
                    for a in range(2):
                        last = dve.scalar_tensor_tensor(D[:, s0 + k * a:s0 + k * (a + 1), :], score_part(0, part)[:, a],
                                                        s1(A_NKK), m[:, a, :].unsqueeze(2).to_broadcast([P, k, N]),
                                                        ALU.mult, ALU.add)
                last.then_inc(sem("dist"), 1)
                dve.wait_ge(sem("dist"), g + 1)
                ts(D, D, H16, s1(A_CL), ALU.max, ALU.min).then_inc(sem("clamped"), 1)
                dve.wait_ge(sem("clamped"), g + 1)
                ts(Q, D, s1(A_IA), s1(A_SB), ALU.mult, ALU.add).then_inc(sem("quot"), 1)
                dve.wait_ge(sem("quot"), g + 1)
                dve.scalar_tensor_tensor(sq[par], Q, s1(A_NA), D, ALU.mult, ALU.add).then_inc(sem("rem"), 1)

            def mid(g, par, half):
                dve.wait_ge(sem("sq"), g + 1)
                dve.wait_ge(sem("power"), g + 1)
                wait(dve, "top", g - 1)
                W = wv[par]
                dve.scalar_tensor_tensor(W, sq[par], s1(A_K0), PW[par].rearrange("p s k -> p (s k)").bitcast(BF16).rearrange("p (s k) -> p s k", k=N),
                                         ALU.add, ALU.mult).then_inc(sem("w"), 1)
                dve.wait_ge(sem("w"), g + 1)
                dve.tensor_reduce(S[:, par, 0, :], W, X, ALU.add).then_inc(sem("wsum"), 1)
                dve.wait_ge(sem("wsum"), g + 1)
                ts(S[:, par, 1, :], S[:, par, 0, :], 1.0 / 3.0, None, ALU.mult).then_inc(sem("third"), 1)
                ts(S[:, par, 2, :], S[:, par, 0, :], 2.0 / 3.0, None, ALU.mult)
                dve.wait_ge(sem("third"), g + 1)
                wait(dve, "exponent", g - 1)
                dve.scalar_tensor_tensor(L[par], W, 1.0 / 6.0, S[:, par, 1, :].unsqueeze(2).to_broadcast([P, 2 * SLOTS, N]),
                                         ALU.mult, ALU.add).then_inc(sem("total"), 1)

            def tail(g, par, half):
                dve.wait_ge(sem("exponent"), g + 1)
                wait(dve, "pt_psum", g - 1)
                pi = Pb[par].rearrange("p s k -> p (s k)").bitcast(I16)
                ts(pi, yb[par].rearrange("p s k -> p (s k)"), -128.0, 128.0 * (H16 + 127.0), ALU.mult, ALU.add).then_inc(sem("pbits"), 1)
                dve.wait_ge(sem("pbits"), g + 1)
                ts(Pb[par], Pb[par], 384.0, 384.0, ALU.add, ALU.subtract).then_inc(sem("masked"), 1)
                dve.wait_ge(sem("masked"), g + 1)
                dve.wait_ge(sem("top"), g + 1)
                tt(Pb[par], Pb[par], top[par], ALU.max).then_inc(sem("probs"), 1)

            pipeline(dve, [(front, 0), (mid, 1), (tail, 2)], 32)
            barrier(dve, "dve")
            minmax([(P, oT[0], X), (C1, oT[1], X)], O_MX)
            dve.drain().then_inc(sem("o_minmax"), 1)
            dve.wait_ge(sem("reduced"), 3)
            ch(ts(sc[:, O_MX:O_MX + 2], sc[:, G0:G0 + 2], s1(Q_S), None, ALU.mult))
            scale_of(O_MX, O_NMN, O_S, O_INV, O_CAPM)
            ch(ts(s1(O_CAPM), s1(O_CAPM), MAGIC, None, ALU.add))
            ch(tt(s1(O_SC), s1(Q_S), s1(O_INV), ALU.mult))
            ch(dve.memset(s1(T2), MAGIC))
            ch(ts(prow, prow, s1(O_S), None, ALU.mult))
            dve.drain().then_inc(sem("o_scalars"), 1)
            dve.wait_ge(sem("ffn_w"), 16 * 32)
            dve.tensor_reduce(s1(W_M1), w1a, X, ALU.max, apply_absolute_value=True)
            dve.tensor_reduce(s1(W_M2), w2a[:, 0:W2M, :], XY, ALU.max, apply_absolute_value=True)
            ch(dve.tensor_reduce(s1(T0, C1), w2a[0:C1, W2M, :], X, ALU.max, apply_absolute_value=True))
            ch(tt(s1(W_M2, C1), s1(W_M2, C1), s1(T0, C1), ALU.max))
            dve.drain().then_inc(sem("w_max"), 1)
            dve.wait_ge(sem("o_added"), 2)
            ts(oq[0], oT[0], s1(O_CAPM), MAGIC, ALU.min, ALU.subtract)
            ts(oq[1], oT[1], s1(O_CAPM, C1), MAGIC, ALU.min, ALU.subtract).then_inc(sem("oq"), 1)
            for i in range(TT):
                dve.wait_ge(sem("y2_psum"), i + 1)
                tt(y2[:, i, :], ps[:, i % 2, 0:C], prow, ALU.mult).then_inc(sem("y2_a"), 1)
            dve.wait_ge(sem("y2_a"), TT)
            ch(tt(y2, y2, bprow.unsqueeze(1).to_broadcast([P, TT, C]), ALU.add))
            dve.wait_ge(sem("w_reduced"), 1)
            ch(ts(sc[:, W_E1:W_E2 + 1], sc[:, G2:G3 + 1], 2.0 ** -25, None, ALU.max))
            ch(ts(sc[:, W_E1:W_E2 + 1].bitcast(I32), sc[:, W_E1:W_E2 + 1].bitcast(I32), 0x7F800000, None, ALU.bitwise_and))
            ch(dve.reciprocal(sc[:, W_S1:W_S2 + 1], sc[:, W_E1:W_E2 + 1]))
            ch(ts(sc[:, W_S1:W_S2 + 1], sc[:, W_S1:W_S2 + 1], 2.0 ** 14, None, ALU.mult))
            ch(ts(s1(W_U), s1(W_E1), s1(W_E1), 2.0 ** -14 / (X_UNIT * 2.0 ** 14 * H_UNIT) ** 2, ALU.mult, ALU.mult))
            ch(tt(s1(W_U), s1(W_U), s1(W_E2), ALU.mult))
            dve.drain().then_inc(sem("w_unit"), 1)
            minmax([(P, y2, XY)], Y_MX)
            dve.drain().then_inc(sem("y2_minmax"), 1)
            dve.wait_ge(sem("reduced"), 4)
            ch(dve.tensor_copy(sc[:, Y_MX:Y_MX + 2], sc[:, G0:G0 + 2]))
            scale_of(Y_MX, Y_NMN, Y_S, Y_INV, Y_CAPM)
            ch(ts(s1(Y_CAPM), s1(Y_CAPM), MAGIC, None, ALU.add))
            ch(ts(y2, y2, s1(Y_INV), MAGIC, ALU.mult, ALU.add))
            ch(ts(y2, y2, s1(Y_CAPM), MAGIC, ALU.min, ALU.subtract))
            dve.wait_ge(sem("hf"), 16)
            ch(dve.scalar_tensor_tensor(hf, y2, s1(Y_S), hf, ALU.mult, ALU.add))
            for i in range(TT):
                ch(dve.bn_stats(bst2[:, i % 2, :], hf[:, i, :]))
                ch(dve.bn_aggr(mv2[:, i, :], bst2[:, i % 2, :]))
            inverse_deviation(mv2[:, :, 1], rs2, "ln2")
            for i in range(TT):
                last = ts(xn2[:, i, 0:C], hf[:, i, :], mv2[:, i, 0:1], rs2[:, 2, i:i + 1], ALU.subtract, ALU.mult)
            ch(last)
            dve.drain().then_inc(sem("xn2"), 1)
            barrier(dve, "dve")
            for i in range(TT // 2):
                dve.wait_ge(sem("X_high"), i + 1)
                src = ps[:, i % 2, :].rearrange("p (k t) -> p k t", k=2)
                t = slice(2 * P * i, 2 * P * (i + 1))
                dve.scalar_tensor_tensor(XS[:, 1, t], src[:, 0], X_UNIT, XS[:, 0, t], ALU.mult, ALU.subtract)
                dve.scalar_tensor_tensor(XS[C1:P, 2, t], src[C1:P, 1], X_UNIT, XS[C1:P, 2, t], ALU.mult, ALU.subtract).then_inc(sem("X"), 1)
            dve.wait_ge(sem("sigmoid"), 1)
            dve.wait_ge(sem("ffn_w"), 16 * 32)
            dve.wait_ge(sem("ffn_c"), 32)
            scores, biased, rank, comb = scr
            ch(tt(biased, scores, bbrow.unsqueeze(1).to_broadcast([P, TT, E]), ALU.add))
            mine = biased.unsqueeze(3).to_broadcast([P, TT, E, E])
            other = biased.unsqueeze(2).to_broadcast([P, TT, E, E])
            ch(tt(cmp_a, other, mine, ALU.is_equal))
            ch(tt(cmp_a.rearrange("p i e f -> p i (e f)"), cmp_a.rearrange("p i e f -> p i (e f)"),
                  lower.unsqueeze(1).to_broadcast([P, TT, E * E]), ALU.mult))
            ch(tt(cmp_b, other, mine, ALU.is_gt))
            ch(tt(cmp_a, cmp_a, cmp_b, ALU.add))
            ch(dve.tensor_reduce(rank, cmp_a, X, ALU.add))
            ch(dve.scalar_tensor_tensor(comb, rank, 1.5, scores, ALU.is_lt, ALU.mult))
            ch(dve.tensor_reduce(csum[:, 0, :], comb, X, ALU.add))
            ch(ts(csum[:, 0, :], csum[:, 0, :], 1e-20, None, ALU.add))
            ch(dve.reciprocal(csum[:, 1, :], csum[:, 0, :]))
            ch(tt(comb, comb, csum[:, 1, :].unsqueeze(2).to_broadcast([P, TT, E]), ALU.mult))
            ch(dve.memset(C3, 0.0))
            for k in range(3):
                ch(dve.tensor_copy(C3[:, :, E * k:E * (k + 1)], comb))
                ch(tt(comb, comb, C3[:, :, E * k:E * (k + 1)], ALU.subtract))
            ch(dve.memset(C3[:, :, 24:25], 1.0))
            dve.drain().then_inc(sem("C3"), 1)
            barrier(dve, "dve")

            def weigh(g, m, par, n, half):
                rows = chunk_rows(m)
                dve.wait_ge(sem("relu"), n + 1)
                dve.wait_ge(sem("c_psum"), n + 1)
                wait(dve, "squared", n - 1)
                tt(hc[0:rows, m % 2, :], hr[0:rows, m % HB, :], ps[0:rows, 2 + m % 2, 0:256], ALU.mult).then_inc(sem("weighted"), 1)

            def low(g, m, par, n, half):
                rows = chunk_rows(m)
                dve.wait_ge(sem("high"), n + 1)
                wait(dve, "h_used", n - HB + 1)
                tt(hh[1][0:rows, m % HB, :], hs[0:rows, m % 2, :], hh[0][0:rows, m % HB, :], ALU.subtract).then_inc(sem("low"), 1)

            def add_h(g, m, par, n, half):
                if m < W2M:
                    return
                dve.wait_ge(sem("h_used"), n + 1)
                wait(dve, f"stored{par}", half * 16)
                dve.scalar_tensor_tensor(ost[:, par], ps[:, 4 + 2 * par:6 + 2 * par, 0:C], s1(W_U), hf[:, bass.ds(g * 2, 2), :],
                                         ALU.mult, ALU.add).then_inc(sem("out_ready"), 1)

            chunks([(low, 2), (weigh, 0), (add_h, 7)])(dve)

        @block.tensor
        def _(pe):
            def mm(o, a, b, start=True, stop=True):
                return pe.matmul(o, a, b, start=start, stop=stop, skip_group_check=True)

            pe.wait_ge(sem("consts"), 48)
            pe.wait_ge(sem("w_rows"), 48)
            pe.wait_ge(sem("vector_step"), wready[0])
            for n, (pieces, rows, cols, dst) in enumerate(turns):
                wait(pe, "w_turned", n - 1)
                for src, m, at in pieces:
                    if src is None:
                        last = mm(ps[:, n % 2, 0:96], ones[0:96, :], wtmp[0:96, m, 0:96])
                    else:
                        last = pe.transpose(ps[0:rows, n % 2, at:at + m], src, ident[0:m, 0:m])
                last.then_inc(sem("w_psum"), 1)
            pe.wait_ge(sem("w_turned"), len(turns))

            for q in range(4):
                pe.wait_ge(sem("by_patch_a"), q + 1)
                pe.wait_ge(sem("by_patch_b"), q + 1)
                for wp in range(GRID):
                    n = q * GRID + wp
                    wait(pe, "patT_a", n)
                    wait(pe, "patT_b", n)
                    for k in range(KC):
                        c, half = k // 2, k % 2
                        src = xp[:, q % 2, c, (2 * wp + half) * P:(2 * wp + half + 1) * P]
                        last = pe.transpose(ps[:, k // 3, (k % 3) * 96:(k % 3) * 96 + 96], src, ident[0:96, 0:96])
                    last.then_inc(sem("pat_psum"), 1)
                    pe.wait_ge(sem("patT_a"), n + 1)
                    pe.wait_ge(sem("patT_b"), n + 1)
                    wait(pe, "img_h", n - 1)
                    for k in range(KC):
                        last = mm(ps[0:96, 2 + n % 2, 0:C], patT[:, n % 2, k * 96:(k + 1) * 96], tokT[:, k, :], k == 0, k == KC - 1)
                    last.then_inc(sem("h_out"), 1)
            pe.wait_ge(sem("img_h"), 24)
            for t in range(16):
                n = 24 + t
                pe.wait_ge(sem(f"emb{t % 4}"), 16 * (t // 4 + 1))
                for k in range(KC):
                    last = pe.transpose(ps[:, k // 3, (k % 3) * P:(k % 3) * P + P], emb[:, t % 4, k * P:(k + 1) * P], ident[:, :])
                last.then_inc(sem("pat_psum"), 1)
                pe.wait_ge(sem("patT_a"), n + 1)
                pe.wait_ge(sem("patT_b"), n + 1)
                wait(pe, "zT", t)
                for m in range(2):
                    for k in range(KC):
                        last = mm(ps[0:96, 4, m * P:(m + 1) * P], w1T[:, k, m * 96:(m + 1) * 96], patT[:, n % 2, k * P:(k + 1) * P], k == 0, k == KC - 1)
                last.then_inc(sem("z_psum"), 1)
                pe.wait_ge(sem("zT"), t + 1)
                wait(pe, "txt_h", t - 1)
                for m in range(2):
                    last = mm(ps[:, 2 + n % 2, 0:C], zT[:, t % 2, m, :], w2T[:, m, :], m == 0, m == 1)
                last.then_inc(sem("h_out"), 1)
            barrier(pe, "pe")

            def turn_x(g, par, half):
                pe.wait_ge(sem("xn_twice"), g + 1)
                wait(pe, "xT", g)
                for k in range(4):
                    pe.transpose(ps[:, 0, k * N:(k + 1) * N], xn[:, par, k, 0:P], ident[0:N, 0:N])
                    last = pe.transpose(ps[:, 1, k * N:(k + 1) * N], xn[:, par, k, P:2 * P], ident[0:N, 0:N])
                last.then_inc(sem("x_psum"), 1)

            def qkv(g, par, half):
                pe.wait_ge(sem("xT"), g + 1)
                wait(pe, "qk_stored", g)
                hi, lo, both = (xT[:, par, k, :] for k in range(3))
                for j in range(3):
                    o, u = ps[:, 2 + j, 0:272], slice(j * P, (j + 1) * P)
                    mm(o, wqT0[:, u], hi, True, False)
                    mm(o, wqT0[:, u], lo, False, False)
                    last = mm(o, wqT1[:, u], both, False, True)
                last.then_inc(sem("qk_psum"), 1)
                for k in range(2):
                    wait(pe, "v_scaled", g * 2 + k - 1)
                    for b in range(2):
                        t = slice((2 * k + b) * N, (2 * k + b + 1) * N)
                        o = ps[0:N, 5 + k, b * C:(b + 1) * C]
                        mm(o, hi[:, t], wqT0[:, 2 * C:3 * C], True, False)
                        mm(o, lo[:, t], wqT0[:, 2 * C:3 * C], False, False)
                        last = mm(o, both[:, t], wqT1[:, 2 * C:3 * C], False, True)
                    last.then_inc(sem("v_psum"), 1)

            pipeline(pe, [(turn_x, 0), (qkv, 1)], 16)
            barrier(pe, "pe")

            def scores(g, base, par, at):
                for b in range(2):
                    for j in range(PAIRS):
                        st = st0 if j < 4 else st1
                        rows = slice(32 * (j % 4), 32 * (j % 4) + 32)
                        bank, k, _ = score_slot(b, j)
                        for a in range(2):
                            mm(ps[NQ * a:NQ * (a + 1), base + bank, k * N:(k + 1) * N],
                               st[rows, par, at + b, NQ * a:NQ * (a + 1)], st[rows, par, at + b, 3 * NQ:QKW])
                for b in range(2):
                    bank, k, _ = score_slot(b, PAIRS)
                    for a in range(2):
                        o = ps[NQ * a:NQ * (a + 1), base + bank, k * N:(k + 1) * N]
                        mm(o, st0[:, par, at + b, 2 * NQ:3 * NQ], st0[:, par, at + b, 3 * NQ:QKW], True, False)
                        last = mm(o, st1[:, par, at + b, 2 * NQ:3 * NQ], st1[:, par, at + b, 3 * NQ:QKW], False, True)
                last.then_inc(sem("scored"), 1)

            def first_scores(g, par, half):
                pe.wait_ge(sem(f"st_qk{par}"), (half + 1) * 48)
                for k in range(2):
                    wait(pe, "extremes", g * 2 + k - 1)
                    scores(g * 2 + k, 4 * k, par, 2 * k)

            def second_scores(g, par, half):
                pe.wait_ge(sem(f"st_qk{par}"), (8 + half + 1) * 48)
                wait(pe, "dist", g)
                scores(g, 0, par, 0)

            pipeline(pe, [(first_scores, 0)], 16)
            barrier(pe, "pe")

            def turn_p(g, par, half):
                pe.wait_ge(sem("probs"), g + 1)
                wait(pe, "PT", g)
                for s in range(2 * SLOTS):
                    last = pe.transpose(pPT[:, s // SLOTS, s % SLOTS, :], Pb[par][:, s, :], ident_b[:, :])
                last.then_inc(sem("pt_psum"), 1)

            def sum_v(g, par, half):
                pe.wait_ge(sem("PT"), g + 1)
                pe.wait_ge(sem("v_spread"), g + 1)
                wait(pe, "o_out", g - 1)
                pt = PT[par].rearrange("p b s q -> p (b s) q")
                for b in range(2):
                    left = pt[:, score_slot(b, PAIRS)[2], :]
                    for j in range(PAIRS):
                        rows = slice(32 * (j % 4), 32 * (j % 4) + 32)
                        main = pt[:, score_slot(b, j)[2], :]
                        o = pO[par][rows, b, j // 4, :]
                        for a in range(2):
                            mm(o[:, 0:NQ], stv[:, par, b, a, 32 * j:32 * j + 32], main[:, NQ * a:NQ * (a + 1)], a == 0, a == 1)
                        for a in range(2):
                            h = 2 * j + a
                            last = mm(o[:, NQ:N], stv[:, par, b, a, 32 * j:32 * j + 32], left[:, NL * h:NL * (h + 1)], a == 0, a == 1)
                last.then_inc(sem("o_summed"), 1)

            pipeline(pe, [(second_scores, 0), (turn_p, 3), (sum_v, 4)], 32)
            barrier(pe, "pe")
            pe.wait_ge(sem("oq"), 1)
            for i in range(TT):
                wait(pe, "y2_a", i - 1)
                t = slice(i * P, (i + 1) * P)
                mm(ps[:, i % 2, 0:C], oq[0][:, t], wpb0, True, False)
                mm(ps[:, i % 2, 0:C], oq[1][:, t], wpb1, False, True).then_inc(sem("y2_psum"), 1)
            barrier(pe, "pe")
            pe.wait_ge(sem("ffn_w"), 16 * 32)
            pe.transpose(ps[:, 5, 0:E], rw_rows[:, 0:P], ident[0:E, 0:E])
            pe.transpose(ps[0:C1, 5, E:2 * E], rw_rows[:, P:C], ident[0:E, 0:E]).then_inc(sem("rw_psum"), 1)
            def route(i):
                pe.wait_ge(sem("xf"), i + 1)
                for j in range(2):
                    o = ps[:, 2, (2 * i + j) * E:(2 * i + j + 1) * E]
                    mm(o, xf[:, i % 2, 0, j, :], rwT[:, 0, :], True, False)
                    last = mm(o, xf[0:C1, i % 2, 1, j, :], rwT[0:C1, 1, :], False, True)
                last.then_inc(sem("routed"), 1)

            pe.wait_ge(sem("rwT"), 1)
            for i in range(TT // 2):
                wait(pe, "X", i - 1)
                for j in range(2):
                    pe.transpose(ps[:, i % 2, j * P:(j + 1) * P], xn2[:, 2 * i + j, 0:P], ident[:, :])
                    last = pe.transpose(ps[:, i % 2, (2 + j) * P:(3 + j) * P], xn2[:, 2 * i + j, P:2 * P], ident[:, :])
                last.then_inc(sem("x2_psum"), 1)
                if i:
                    route(i - 1)
            route(TT // 2 - 1)
            pe.wait_ge(sem("C3"), 1)
            for q in range(5):
                wait(pe, "CT", q - 1)
                for k in range(min(8, TT - 8 * q)):
                    last = pe.transpose(ps[0:32, 3 + q % 2, k * 64:(k + 1) * 64].bitcast(BF16), C3[:, 8 * q + k, :], ident_b[:, :])
                last.then_inc(sem("ct_psum"), 1)
            barrier(pe, "pe")

            def up(g, m, par, n, half):
                rows = chunk_rows(m)
                if m == 0:
                    pe.wait_ge(sem(f"xs{par}"), (half + 1) * 32)
                wait(pe, "relu", n - 1)
                u, v = slice(m * P, m * P + rows), slice(U + m * P, U + m * P + rows)
                o = ps[0:rows, m % 2, 0:256]
                mm(o, w1s[0][:, u], xs[:, par, 0], True, False)
                mm(o, w1s[0][:, u], xs[:, par, 1], False, False)
                mm(o, w1s[1][:, u], xs[:, par, 0], False, False)
                mm(o, w1s[0][:, v], xs[:, par, 2], False, False)
                mm(o, w1s[1][:, v], xs[:, par, 2], False, True).then_inc(sem("h_psum"), 1)
                wait(pe, "weighted", n - 1)
                mm(ps[0:rows, 2 + m % 2, 0:256], sel_b[:, u], cts[:, par]).then_inc(sem("c_psum"), 1)

            def down(g, m, par, n, half):
                rows = chunk_rows(m)
                if m == 0:
                    wait(pe, "out_ready", g - 1)
                for i in range(2):
                    o = ps[:, 4 + 2 * par + i, 0:C]
                    t = slice(i * P, (i + 1) * P)
                    if i == 0:
                        pe.wait_ge(sem("high"), n + 1)
                    mm(o, hh[0][0:rows, m % HB, t], w2s[0][0:rows, m, :], m == 0, False)
                    mm(o, hh[0][0:rows, m % HB, t], w2s[1][0:rows, m, :], False, False)
                    if i == 0:
                        pe.wait_ge(sem("low"), n + 1)
                    last = mm(o, hh[1][0:rows, m % HB, t], w2s[0][0:rows, m, :], False, m == W2M)
                last.then_inc(sem("h_used"), 1)

            chunks([(up, 0), (down, 4)])(pe)


_INS = ['x', 'x_txt', 'L0_tok_W', 'L0_tok_b', 'L0_tok_pos', 'L0_txt_tok_embed', 'L0_txt_W1', 'L0_txt_b1', 'L0_txt_W2',
        'L0_txt_b2', 'L0_attn_w_qkv', 'L0_attn_b_qkv', 'L0_attn_w_proj', 'L0_attn_b_proj', 'L0_ffn_w_fc_sh',
        'L0_ffn_w_proj_sh', 'L0_ffn_w1', 'L0_ffn_w2', 'L0_ffn_router_w', 'L0_ffn_balance_bias']


def constants():
    import numpy as np

    p = np.arange(P)
    h = np.arange(16)
    masks = np.zeros((P, 34), np.float32)
    masks[:, 0:16] = (p[:, None] // HD == h) & (h < 8)
    masks[:, 16:32] = (p[:, None] // HD + 8 == h) & (h < H)
    masks[:, 32] = p // HD % 2 == 0
    masks[:, 33] = p // HD % 2 == 1
    u = np.arange(UC * P)
    rows = np.arange(32)
    expert = np.where(rows < 3 * E, rows % E, np.where(rows == 3 * E, E, -1))
    select = (u // C == expert[:, None]).astype(np.float32)
    e = np.arange(E)
    lower = (e[None, :] < e[:, None]).astype(np.float32).reshape(-1)
    return {"ident": np.eye(P, dtype=np.float32), "masks": masks, "select": select, "lower": lower}


def kernel(**inputs):
    import numpy as _np
    import concourse.bacc as _bacc
    from concourse import mybir as _mybir
    from concourse.bass_utils import run_bass_kernel_spmd as _run

    nc = _bacc.Bacc("TRN2", target_bir_lowering=False, num_devices=1)
    arrays, args = {}, []
    for name, a in [(n, inputs[n]) for n in _INS] + list(constants().items()):
        a = _np.ascontiguousarray(a)
        arrays[f"in_{name}_dram"] = a
        args.append(nc.dram_tensor(f"in_{name}_dram", a.shape, _mybir.dt.from_np(a.dtype), kind="ExternalInput").ap())
    args.append(nc.dram_tensor("out_0_dram", (B, N, C), _mybir.dt.float32, kind="ExternalOutput").ap())
    program(nc, *args)
    r = _run(nc, [arrays], core_ids=[0])
    return r.results[0]["out_0_dram"]
```

```python
from contextlib import ExitStack

import concourse.bass as bass
from concourse import mybir

F32 = mybir.dt.float32
F16 = mybir.dt.float16
BF16 = mybir.dt.bfloat16
I16 = mybir.dt.int16
I32 = mybir.dt.int32
ALU = mybir.AluOpType
ACT = mybir.ActivationFunctionType
X = mybir.AxisListType.X
XY = mybir.AxisListType.XY
RMAX = bass.bass_isa.ReduceOp.max

P = 128
B = 64
C = 192
C1 = C - P
GRID = 6
PATCH = 16
NI = GRID * GRID
NT = 32
N = NI + NT
T = B * N
TT = T // P
H = 12
HD = C // H
MW = 6356
PAIRS = H // 2
NQ = 64
NL = N - NQ
FRONT = 768
KC = FRONT // P
SLOTS = PAIRS + 1
QKW = 3 * NQ + N
E = 8
U = (E + 1) * C
UC = (U + P - 1) // P
HB = 7
WEIGHED = E * C // P
W2M = UC - 1
X_UNIT = 1024.0
H_UNIT = 2.0 ** -25
EPS_LN = 1e-5
EPS_Q = 1.1920928955078125e-07
MAGIC = 12582912.0
H16 = 1024.0
C0 = 0.35815147


def pipeline(eng, stages, groups):
    last = max(lag for _, lag in stages)
    lead = last + 2 + (groups - last) % 2

    def step(s):
        for fn, lag in stages:
            if 0 <= s - lag < groups:
                fn(s - lag, (s - lag) % 2, (s - lag) // 2)

    for s in range(lead):
        step(s)
    with eng.Fori(0, (groups - lead) // 2) as i:
        for p in (0, 1):
            for fn, lag in stages:
                g = lead + p - lag
                fn(i * 2 + g, g % 2, i + g // 2)
    for s in range(groups, groups + last):
        step(s)


def program(nc, x, x_txt, tok_W, tok_b, tok_pos, embed, W1, b1, W2, b2, w_qkv, b_qkv, w_proj, b_proj,
            w_fc_sh, w_proj_sh, w1, w2, router_w, balance_bias, ident_c, headmask_c, select_c, lower_c, out):
    ctx = ExitStack()
    with ctx:
        def sb(name, shape, dt=F32):
            return ctx.enter_context(nc.sbuf_tensor(name, shape, dt))

        sems = {}

        def sem(name):
            if name not in sems:
                sems[name] = ctx.enter_context(nc.semaphore(name))
            return sems[name]

        def wait(eng, name, value):
            if isinstance(value, int) and value <= 0:
                return
            eng.wait_ge(sem(name), value)

        counts = {}

        def chain(eng, name, ins):
            counts[name] = counts.get(name, 0) + 1
            ins.then_inc(sem(name), 1)
            eng.wait_ge(sem(name), counts[name])

        barriers = {}

        def barrier(eng, name):
            n = barriers.get(name, 0) + 1
            barriers[name] = n
            eng.drain().then_inc(sem("all_engines_done"), 1)
            eng.wait_ge(sem("all_engines_done"), 5 * n)

        h_dram = nc.dram_tensor("h_rows", [T, C], F32, kind="Internal").ap()

        R0 = sb("R0", [P, 4 * T])
        R1 = sb("R1", [P, B * C])
        R2 = sb("R2", [P, 16640])
        M = sb("M", [P, MW])
        ps = ctx.enter_context(nc.psum_tensor("ps", [P, 8, 512], F32))
        used = [0]

        def misc(words, dt=F32, rows=P):
            a = used[0]
            used[0] += words
            assert used[0] <= MW, used[0]
            v = M[0:rows, a:a + words]
            return v if dt == F32 else v.bitcast(dt)

        ident = sb("ident", [P, P])
        ident_b = sb("ident_b", [P, P], BF16)
        headmask = sb("headmask", [P, 2, 16])
        parmask = sb("parmask", [P, 2])
        sc = sb("sc", [P, 64])
        biases = sb("biases", [P, 16])
        ones = sb("ones", [P, P])

        ximg = R0[0:96, 0:2 * 4608].rearrange("p (a c f) -> p a c f", a=2, c=3)
        emb = R0[:, 9216:9216 + 2 * FRONT].rearrange("p (a f) -> p a f", a=2)
        patT = R0[:, 12288:12288 + 2 * 768].rearrange("p (a f) -> p a f", a=2)
        hstage = R1[0:96, 0:2 * 1152].rearrange("p (a w c) -> p a w c", a=2, w=GRID)
        tstage = R1[:, 2304:2304 + 2 * C].rearrange("p (a c) -> p a c", a=2)
        zT = R1[0:96, 2688:2688 + 4 * P].rearrange("p (a m t) -> p a m t", a=2, m=2)
        posb = R1[0:96, 3200:3200 + GRID * C].rearrange("p (w c) -> p w c", w=GRID)
        brow = R1[:, 4352:4352 + 3 * C].rearrange("p (k c) -> p k c", k=3)
        idx = R1[:, 4928:4944].bitcast(I32)
        w_rows = R1[0:96, 5000:5000 + 2 * 2 * FRONT].rearrange("p (a j f) -> p a j f", a=2, j=2)
        w2_rows = R1[0:96, 8072:8072 + 2 * C].rearrange("p (j f) -> p j f", j=2)
        tokT = R2[:, 0:KC * C].rearrange("p (k c) -> p k c", k=KC)
        w1T = R2[:, 1152:1152 + KC * C].rearrange("p (k c) -> p k c", k=KC)
        xp = R2[0:96, 6300:6300 + 2 * 4608].rearrange("p (a c f) -> p a c f", a=2, c=3)
        w2T = R2[0:96, 2304:2304 + 2 * C].rearrange("p (m c) -> p m c", m=2)

        WROWS = [([(0, P, 0)], 0), ([(C, P, 0)], P), ([(P, C1, 0), (C + P, C1, C1)], 2 * P),
                 ([(2 * C, 96, 0)], 2 * C), ([(2 * C + 96, 96, 0)], 2 * C + 96),
                 ([(3 * C, 96, 0)], 0), ([(3 * C + 96, 96, 0)], 96)]
        WJ = [(parts[-1][1] + parts[-1][2], at) for parts, at in WROWS]
        wq_rows = R2[:, 2700:2700 + 7 * 2 * P].rearrange("p (j c) -> p j c", j=7)
        wqT0 = misc(3 * C // 2, F16)
        wqT1 = misc(3 * C // 2, F16)
        wpb0 = misc(C // 2, BF16)
        wpb1 = misc(C // 2, BF16, rows=C1)
        wscale = misc(8)
        wtmp = R2[:, 4500:4500 + 7 * C].rearrange("p (j c) -> p j c", j=7)
        vrow = misc(C)
        prow = misc(C)
        bprow = misc(C)
        bvrow = misc(C)

        yqk = R0[:, 0:3 * T].rearrange("p (k t) -> p k t", k=3)
        yv = R1[0:N, :].rearrange("p (b c) -> p b c", b=B)
        hb = R2[0:N, 0:B * C].rearrange("p (b c) -> p b c", b=B)
        xn = R2[0:N, B * C:B * C + 2 * 4 * 2 * P].rearrange("p (a b c) -> p a b c", a=2, b=4)
        xT = R2[:, 14336:14336 + 3 * 272].bitcast(F16).rearrange("p (a k t) -> p a k t", a=2, k=3)
        mv = R2[0:N, 15152:15152 + 2 * B].rearrange("p (b s) -> p b s", s=2)
        rs = R2[0:N, 15280:15280 + 3 * B].rearrange("p (k b) -> p k b", k=3)
        bst = R2[0:N, 15472:15472 + 6 * B].rearrange("p (b s) -> p b s", s=6)
        extr = misc(4 * 16).rearrange("p (m k g) -> p m k g", m=2, k=2)

        QK0 = R2[:, 0:B * QKW // 2].bitcast(BF16).rearrange("p (b w) -> p b w", b=B)
        QK1 = R2[:, B * QKW // 2:B * QKW].bitcast(BF16).rearrange("p (b w) -> p b w", b=B)
        VQ = R0[0:N, 0:B * C // 2].bitcast(BF16).rearrange("p (b c) -> p b c", b=B)
        QTW = 2 * NQ + NL + N
        qt = R0[:, 3 * T:3 * T + 4 * 8 * QTW // 2].bitcast(F16).rearrange("p (a k b w) -> p a k b w", a=2, k=2, b=8)
        vt = R0[0:N, B * C // 2:B * C].bitcast(F16).rearrange("p (b c) -> p b c", b=B)

        CW = 2 * SLOTS * N
        st0 = misc(4 * QKW, BF16).rearrange("p (a b w) -> p a b w", a=2, b=4)
        st1 = misc(4 * QKW, BF16, rows=C1).rearrange("p (a b w) -> p a b w", a=2, b=4)
        stv = misc(2 * 2 * C, BF16, rows=N).rearrange("p (a b h c) -> p a b h c", a=2, b=2, h=2)
        rowmax = misc(32 * 2 * SLOTS).rearrange("p (g s) -> p g s", g=32)
        gmin = misc(64)
        rmq = misc(32 * SLOTS, F16).rearrange("p (g s) -> p g s", g=32)
        oT = [R1[:, 0:T], R1[0:C1, T:2 * T]]
        w0 = [B * C // 2]

        def r0(words, dt=F32):
            a = w0[0]
            w0[0] += words
            assert w0[0] <= 4 * T
            v = R0[:, a:a + words]
            return v if dt == F32 else v.bitcast(dt)

        w1_ = [2 * T]

        def r1(words, dt=F32):
            a = w1_[0]
            w1_[0] += words
            assert w1_[0] <= B * C
            v = R1[:, a:a + words]
            return v if dt == F32 else v.bitcast(dt)

        def slots(v):
            return v.rearrange("p (s k) -> p s k", k=N)

        Dq = [slots(r0(CW // 2, F16)) for _ in range(2)]
        Qq = [slots(r0(CW // 2, F16)) for _ in range(2)]
        PW = [slots(r0(CW // 2, I16)) for _ in range(2)]
        sq = [slots(r0(CW)) for _ in range(2)]
        wv = [slots(r1(CW)) for _ in range(2)]
        L = [slots(r0(CW)) for _ in range(2)]
        yb = [slots(r1(CW // 2, F16)) for _ in range(2)]
        Pb = [slots(r0(CW // 2, BF16)) for _ in range(2)]
        PT = [r0(SLOTS * P, BF16)[0:N].rearrange("p (b s q) -> p b s q", b=2, s=SLOTS) for _ in range(2)]
        S = misc(3 * 4 * SLOTS).rearrange("p (a k s) -> p a k s", a=2, k=3)
        top = [slots(r0(CW // 2, BF16)) for _ in range(2)]

        def score_slot(b, j):
            if j == PAIRS:
                return 2 + b, 2, 8 + 3 * b + 2
            r = j % 4
            if r < 2:
                k = 2 * b + j // 4
                return r, k, 4 * r + k
            return r, b, 8 + 3 * (r - 2) + b

        PARTS = [(0, 4, 0), (2, 3, 8)]

        def score_part(base, part):
            bank, k, _ = PARTS[part]
            return ps[:, base + bank:base + bank + 2, 0:k * N].rearrange("p a (s k) -> p a s k", k=N)

        pPT = ps[0:N, 4:6, 0:SLOTS * P // 2].bitcast(BF16).rearrange("p b (s q) -> p b s q", s=SLOTS)
        pO = [ps[:, 6, 0:4 * N].rearrange("p (b c t) -> p b c t", b=2, c=2),
              ps[:, 7, 0:4 * N].rearrange("p (b c t) -> p b c t", b=2, c=2)]

        oq = [R0[:, 0:T // 2].bitcast(BF16), R0[0:C1, T // 2:T].bitcast(BF16)]
        y2 = R0[:, T:T + TT * C].rearrange("p (i c) -> p i c", i=TT)
        hf = R0[:, T + TT * C:T + 2 * TT * C].rearrange("p (i c) -> p i c", i=TT)
        xn2 = R1[:, 0:TT * 2 * P].rearrange("p (i c) -> p i c", i=TT)
        CT = R1[0:32, 8704:8704 + T // 2].bitcast(BF16)
        hr = R1[:, 0:7 * 256].rearrange("p (a t) -> p a t", a=HB)
        hc = R1[:, 1792:1792 + 7 * 256].rearrange("p (a t) -> p a t", a=HB)
        hs = R1[:, 3584:3584 + 7 * 256].rearrange("p (a t) -> p a t", a=HB)
        hh = [R1[:, 5376 + 896 * k:5376 + 896 * (k + 1)].bitcast(F16).rearrange("p (a t) -> p a t", a=HB) for k in range(2)]
        ost = R1[:, 7168:7168 + 2 * 2 * C].rearrange("p (a i c) -> p a i c", a=2, i=2)
        sel_b = R1[0:32, 11008:11008 + UC * P // 2].bitcast(BF16)
        w1a = R2[:, 8704:8704 + 2 * U]
        w2a = R2[:, 12160:12160 + UC * C].rearrange("p (m c) -> p m c", m=UC)
        w1s = [R2[:, U * k:U * (k + 1)].bitcast(F16) for k in range(2)]
        w2s = [R2[:, 2 * U + 1344 * k:2 * U + 1344 * (k + 1)].bitcast(F16).rearrange("p (m c) -> p m c", m=UC) for k in range(2)]
        XS = R2[:, 6144:6144 + 3 * T // 2].bitcast(F16).rearrange("p (k t) -> p k t", k=3)
        mv2 = R2[:, 14848:14848 + 2 * TT].rearrange("p (i s) -> p i s", s=2)
        rs2 = R2[:, 14920:14920 + 3 * TT].rearrange("p (k i) -> p k i", k=3)
        bst2 = R2[:, 15330:15330 + 6 * TT].rearrange("p (i s) -> p i s", i=TT)
        rwT = R2[:, 15040:15056].rearrange("p (k e) -> p k e", k=2)
        rws = [R2[:, 15056 + 8 * k:15064 + 8 * k].bitcast(F16).rearrange("p (k e) -> p k e", k=2) for k in range(2)]
        rw_rows = R2[0:E, 15072:15072 + C + C1]
        bbrow = R2[:, 16574:16582]
        scr = [R2[:, 15330 + 272 * k:15330 + 272 * (k + 1)].rearrange("p (i e) -> p i e", e=E) for k in range(4)]
        cmp_a = R0[:, T:T + TT * E * E].rearrange("p (i e f) -> p i e f", e=E, f=E)
        cmp_b = R0[:, T + TT * E * E:T + 2 * TT * E * E].rearrange("p (i e f) -> p i e f", e=E, f=E)
        lower = R0[:, T + 2 * TT * E * E:T + 2 * TT * E * E + E * E]
        sel_w = R0[0:32, T + 2 * TT * E * E + 64:T + 2 * TT * E * E + 64 + UC * P]
        xs = R0[:, 0:768].bitcast(F16).rearrange("p (a k t) -> p a k t", a=2, k=3)
        cts = R0[0:32, 1024:1280].bitcast(BF16).rearrange("p (a t) -> p a t", a=2)
        C3 = misc(TT * 16, BF16).rearrange("p (i e) -> p i e", i=TT)
        csum = misc(2 * TT).rearrange("p (k i) -> p k i", k=2)

        turns = []

        def turn(pieces, rows, cols, dst):
            turns.append((pieces, rows, cols, dst))

        for a, dst in ((1, w1T), (0, tokT)):
            for k in range(KC):
                turn([(w_rows[:, a, j, k * P:(k + 1) * P], 96, j * 96) for j in range(2)], P, C, dst[:, k, :])
        for m in range(2):
            turn([(w2_rows[:, j, m * 96:(m + 1) * 96], 96, j * 96) for j in range(2)], 96, C, w2T[:, m, :])
        EMBED_TURNS = len(turns)
        for j, (m, at) in enumerate(WJ):
            d0, d1, end = (wqT0, wqT1, 2 * P) if j < 5 else (wpb0, wpb1, C)
            turn([(wq_rows[0:m, j, 0:P], m, 0)], P, m, d0[:, at:at + m])
            turn([(wq_rows[0:m, j, P:end], m, 0)], end - P, m, d1[:, at:at + m])
        for j, row in ((3, vrow), (4, vrow), (5, prow), (6, prow)):
            turn([(None, j, 0)], P, 96, row[:, (1 - j % 2) * 96:(2 - j % 2) * 96])
        wready = []

        def chunk_rows(m):
            return P if m < W2M else C1

        def chunks(steps):
            most = max(lag for _, lag in steps)

            def group(g, par, half):
                for m in range(UC):
                    for fn, lag in steps:
                        if m >= lag:
                            fn(g, m - lag, par, g * UC + m - lag, half)
                        elif not (isinstance(g, int) and g == 0):
                            fn(g - 1, m - lag + UC, 1 - par, g * UC + m - lag, half - 1 + par)

            def run(eng):
                pipeline(eng, [(group, 0)], TT // 2)
                for m in range(most):
                    for fn, lag in steps:
                        if m < lag:
                            g = TT // 2
                            fn(g - 1, m - lag + UC, 1 - g % 2, g * UC + m - lag, (g - 1) // 2)

            return run

        block = ctx.enter_context(nc.Block())

        (Q_MX, Q_NMN, Q_R, Q_INV, Q_CAPM, Q_EV, Q_OD, Q_S, A_MX, A_NMN, A_S, A_INV, A_KK, A_NKK, A_CAP, A_IS,
         A_A, A_IA, A_BH, A_K0, A_CL, A_CB, A_NA, A_SB, O_MX, O_NMN, O_S, O_INV, O_CAPM, O_SC, Y_MX, Y_NMN, Y_S,
         Y_INV, Y_CAPM, T0, T1, T2, G0, G1, A_M16, A_B, A_C, A_K1, A_PB, W_M1, W_M2, W_M3, W_E1, W_E2,
         W_E3, W_S1, W_S2, W_S3, W_U, G2, G3, G4, W_RU) = range(59)

        QKPARTS = [(yqk[:, 0].rearrange("p (b n) -> p b n", n=N), yqk[:, 1].rearrange("p (b n) -> p b n", n=N),
                    QK0, slice(0, P), slice(0, P)),
                   (yqk[:, 2].rearrange("p (b n) -> p b n", n=N), yqk[:, 2].rearrange("p (b n) -> p b n", n=N),
                    QK1, slice(0, C1), slice(C1, P))]

        def s1(k, rows=P):
            return sc[0:rows, k:k + 1]

        @block.sync
        def _(sp):
            sp.dma_start(ident[:, :], ident_c).then_inc(sem("consts"), 16)
            sp.dma_start(headmask[:, :, :], headmask_c[:, 0:32].rearrange("p (k h) -> p k h", k=2)).then_inc(sem("consts"), 16)
            sp.dma_start(parmask[:, :], headmask_c[:, 32:34]).then_inc(sem("consts"), 16)
            sp.dma_start(w_rows[:, 0], tok_W.rearrange("(j p) f -> p j f", p=96)).then_inc(sem("w_rows"), 16)
            sp.dma_start(w_rows[:, 1], W1.rearrange("(j p) f -> p j f", p=96)).then_inc(sem("w_rows"), 16)
            sp.dma_start(w2_rows[:, :, :], W2.rearrange("(j p) f -> p j f", p=96)).then_inc(sem("w_rows"), 16)
            for j, (parts, _) in enumerate(WROWS):
                for o, m, p0 in parts:
                    src = w_qkv[o:o + m, :] if o < 3 * C else w_proj[o - 3 * C:o - 3 * C + m, :]
                    sp.dma_start(wq_rows[p0:p0 + m, j, 0:C], src).then_inc(sem("wq_rows"), 16)
                    sp.dma_start(wq_rows[p0:p0 + m, j, C:2 * P], src[:, P:C]).then_inc(sem("wq_rows"), 16)
            sp.dma_start(biases[0:96, 0:2], b1.rearrange("(j p) -> p j", p=96), allow_slow_non_contiguous=True).then_inc(sem("bias_b1"), 16)
            sp.dma_start(brow[:, 0, :], tok_b.partition_broadcast(P)).then_inc(sem("bias_rows"), 16)
            sp.dma_start(brow[:, 1, :], b2.partition_broadcast(P)).then_inc(sem("bias_rows"), 16)
            for b in range(16):
                sp.dma_start(posb[GRID * b:GRID * (b + 1), :, :],
                             tok_pos.rearrange("o (h w) c -> (o h) w c", w=GRID)).then_inc(sem("bias_rows"), 16)
            xv = x.rearrange("b c (h r) w -> c b h (r w)", h=GRID)

            def load_images(q):
                for c in range(3):
                    sp.dma_start(ximg[:, q % 2, c, :], xv[c, 16 * q:16 * q + 16]).then_inc(sem(f"ximg{q % 2}"), 16)

            load_images(0)
            load_images(1)
            sp.dma_start(bprow, b_proj.partition_broadcast(P)).then_inc(sem("bias_later"), 16)
            sp.dma_start(bvrow, b_qkv[2 * C:3 * C].partition_broadcast(P)).then_inc(sem("bias_later"), 16)
            for j in range(3):
                for o, m, p0 in WROWS[j][0]:
                    sp.dma_start(biases[p0:p0 + m, 2 + j:3 + j], b_qkv[o:o + m].rearrange("(p a) -> p a", a=1),
                                 allow_slow_non_contiguous=True).then_inc(sem("bias_later"), 16)
            hv = h_dram.rearrange("(b n) c -> b n c", n=N)

            def store_text(t, par, half):
                sp.wait_ge(sem("h_added"), t + 1)
                sp.dma_start(hv[bass.ds(t * 4, 4), NI:N, :], tstage[:, par, :]).then_inc(sem(f"t_stored{par}"), 16)

            pipeline(sp, [(store_text, 0)], 16)
            for q in (2, 3):
                sp.wait_ge(sem("by_patch_a"), q - 1)
                sp.wait_ge(sem("by_patch_b"), q - 1)
                load_images(q)
            for q in range(4):
                sp.wait_ge(sem("h_added"), 16 + GRID * (q + 1))
                sp.dma_start(hv[16 * q:16 * q + 16, 0:NI, :].rearrange("b (h w) c -> b h (w c)", w=GRID),
                             hstage[:, q % 2].rearrange("p w c -> p (w c)")).then_inc(sem(f"h_stored{q % 2}"), 16)
            sp.wait_ge(sem("bias_later"), 16 * 6)
            for a in range(2):
                sp.wait_ge(sem(f"h_stored{a}"), 32)
                sp.wait_ge(sem(f"t_stored{a}"), 128)
            barrier(sp, "sp")
            for q in range(4):
                sp.dma_start(hb[:, 16 * q:16 * q + 16, :],
                             hv[16 * q:16 * q + 16].rearrange("b n c -> n b c")).then_inc(sem(f"hb{q}"), 16)
            barrier(sp, "sp")
            def load_seqs(par, b, n):
                sp.dma_start(st0[:, par, 0:n], QK0[:, b, :]).then_inc(sem(f"st_qk{par}"), 16)
                sp.dma_start(st1[:, par, 0:n, 0:3 * NQ], QK1[0:C1, b, 0:3 * NQ]).then_inc(sem(f"st_qk{par}"), 16)
                sp.dma_start(st1[:, par, 0:n, 3 * NQ:QKW], QK1[C1:P, b, 3 * NQ:QKW]).then_inc(sem(f"st_qk{par}"), 16)

            def load_four(g, par, half):
                if par == 0:
                    sp.wait_ge(sem("qk_chunk"), half + 1)
                else:
                    wait(sp, "scored", (g - 1) * 2)
                load_seqs(par, bass.ds(g * 4, 4), 4)

            def load_two(g, par, half):
                wait(sp, "scored", 32 + g - 1)
                load_seqs(par, bass.ds(g * 2, 2), 2)

            pipeline(sp, [(load_four, 0)], 16)
            barrier(sp, "sp")
            pipeline(sp, [(load_two, 0)], 32)
            barrier(sp, "sp")
            sp.dma_start(hf, h_dram.rearrange("(i p) c -> p i c", p=P)).then_inc(sem("hf"), 16)
            for e in range(E + 1):
                src = w1[e] if e < E else w_fc_sh
                sp.dma_start(w1a[:, e * C:(e + 1) * C], src[0:P, :]).then_inc(sem("ffn_w"), 16)
                for k in range(2):
                    sp.dma_start(w1a[C1 * k:C1 * (k + 1), U + e * C:U + (e + 1) * C], src[P:C, :]).then_inc(sem("ffn_w"), 16)
            sp.dma_start(w2a[:, 0:UC - 2, :], w2.rearrange("e h c -> (e h) c").rearrange("(m p) c -> p m c", p=P)).then_inc(sem("ffn_w"), 16)
            sp.dma_start(w2a[:, UC - 2, :], w_proj_sh[0:P, :]).then_inc(sem("ffn_w"), 16)
            sp.dma_start(w2a[0:C1, UC - 1, :], w_proj_sh[P:C, :]).then_inc(sem("ffn_w"), 16)
            sp.dma_start(rw_rows[:, 0:C], router_w).then_inc(sem("ffn_w"), 16)
            sp.dma_start(rw_rows[:, C:2 * P], router_w[:, P:C]).then_inc(sem("ffn_w"), 16)
            sp.dma_start(bbrow, balance_bias.partition_broadcast(P)).then_inc(sem("ffn_w"), 16)
            barrier(sp, "sp")
            sp.dma_start(lower, lower_c.partition_broadcast(P)).then_inc(sem("ffn_c"), 16)
            sp.dma_start(sel_w, select_c).then_inc(sem("ffn_c"), 16)
            barrier(sp, "sp")
            ov = out.rearrange("b n c -> (b n) c").rearrange("(i p) c -> p i c", p=P)

            def store(g, par, half):
                sp.wait_ge(sem("out_ready"), g + 1)
                sp.dma_start(ov[:, bass.ds(g * 2, 2), :], ost[:, par]).then_inc(sem(f"stored{par}"), 16)

            def load_x(g, par, half):
                wait(sp, "h_used", (g - 1) * UC)
                t = bass.ds(g * 256, 256)
                sp.dma_start(xs[:, par], XS[:, :, t]).then_inc(sem(f"xs{par}"), 16)
                sp.dma_start(cts[:, par], CT[:, t]).then_inc(sem(f"xs{par}"), 16)

            pipeline(sp, [(load_x, 0), (store, 2)], TT // 2)
            sp.wait_ge(sem("stored0"), 16 * 9)
            sp.wait_ge(sem("stored1"), 16 * 8)

        @block.gpsimd
        def _(pool):
            pool.dma_start(idx, x_txt.rearrange("b s -> (b s)").rearrange("(t p) -> p t", p=P),
                           allow_slow_non_contiguous=True).then_inc(sem("idx"), 16)
            pool.wait_ge(sem("idx"), 16)
            for t in range(16):
                if t >= 2:
                    pool.wait_ge(sem("pat_psum"), t - 1)
                pool.indirect_dma_start(emb[:, t % 2, :], None, embed,
                                        bass.IndirectOffsetOnAxis(ap=idx[:, t:t + 1], axis=0)).then_inc(sem(f"emb{t % 2}"), 16)
            barrier(pool, "pool")

            def reduce_pair(k, name):
                pool.wait_ge(sem(name), 1)
                pool.partition_all_reduce(sc[:, G0:G0 + 2], sc[:, k:k + 2], P, RMAX).then_inc(sem("reduced"), 1)

            def normalise(g, par, half):
                pool.wait_ge(sem("ln_done"), 1 if isinstance(g, int) and g < 4 else 2)
                wait(pool, "x_psum", g - 1)
                b4 = bass.ds(g * 4, 4)
                v = xn[:, par, :, 0:C]
                pool.tensor_tensor(v, hb[:, b4, :], mv[:, b4, 0:1].to_broadcast([N, 4, C]), ALU.subtract).then_inc(sem("centred"), 1)
                pool.wait_ge(sem("centred"), g + 1)
                pool.tensor_tensor(v, v, rs[:, 2, b4].unsqueeze(2).to_broadcast([N, 4, C]), ALU.mult).then_inc(sem("xn"), 1)

            def v_bias(g, par, half):
                pool.wait_ge(sem("v_scaled"), g * 2 + 2)
                v = yv[:, bass.ds(g * 4, 4), :]
                pool.tensor_tensor(v, v, bvrow[0:N, :].unsqueeze(1).to_broadcast([N, 4, C]), ALU.add).then_inc(sem("v_stored"), 1)

            pipeline(pool, [(normalise, 0), (v_bias, 2)], 16)
            reduce_pair(Q_MX, "q_minmax")
            barrier(pool, "pool")

            def leftovers(c, par, half):
                pool.wait_ge(sem("q_rounded"), c + 1)
                for k, (_, _, QK, rows, _) in enumerate(QKPARTS):
                    if k == 1:
                        wait(pool, "scored", 4 * c - 2)
                    last = pool.tensor_tensor(QK[rows, bass.ds(c * 8, 8), 2 * NQ:3 * NQ].rearrange("p b (h i) -> p b h i", i=NL),
                                              qt[rows, par, k, :, 2 * NQ:2 * NQ + NL].unsqueeze(2).to_broadcast([rows.stop, 8, 16, NL]),
                                              headmask[rows, k, :].unsqueeze(1).unsqueeze(3).to_broadcast([rows.stop, 8, 16, NL]),
                                              ALU.mult)
                last.then_inc(sem("qk_chunk"), 1)

            pipeline(pool, [(leftovers, 0)], 8)
            reduce_pair(A_MX, "a_minmax")
            barrier(pool, "pool")

            def quotient_bits(g, par, half):
                pool.wait_ge(sem("total"), g + 1)
                pool.tensor_tensor(L[par].bitcast(I32), L[par].bitcast(I32), wv[par].bitcast(I32), ALU.subtract).then_inc(sem("log2"), 1)
                wait(pool, "probs", g - 1)
                pool.tensor_tensor(top[par], wv[par], S[:, par, 2, :].unsqueeze(2).to_broadcast([P, 2 * SLOTS, N]),
                                   ALU.subtract).then_inc(sem("excess"), 1)

            def spread_v(g, par, half):
                wait(pool, "o_summed", g - 1)
                for a in range(2):
                    last = pool.tensor_copy(stv[:, par, :, a].rearrange("p b (j h d) -> p b j h d", h=2, d=HD)[:, :, :, a, :],
                                            VQ[:, bass.ds(g * 2, 2), :].rearrange("p b (j h d) -> p b j h d", h=2, d=HD)[:, :, :, a, :])
                last.then_inc(sem("v_spread"), 1)

            pool.memset(stv, 0.0).then_inc(sem("v_cleared"), 1)
            pool.wait_ge(sem("v_cleared"), 1)
            pipeline(pool, [(quotient_bits, 0), (spread_v, 2)], 32)
            barrier(pool, "pool")
            reduce_pair(O_MX, "o_minmax")
            pool.wait_ge(sem("w_max"), 1)
            pool.partition_all_reduce(sc[:, G2:G4 + 1], sc[:, W_M1:W_M3 + 1], P, RMAX).then_inc(sem("w_reduced"), 1)
            for i in range(TT // 2):
                pool.wait_ge(sem("y2_a"), i + 1)
                y = y2[:, 2 * i:2 * i + 2, :]
                pool.tensor_tensor(y, y, bprow.unsqueeze(1).to_broadcast([P, 2, C]), ALU.add).then_inc(sem("y2"), 1)
            pool.wait_ge(sem("y2_minmax"), 1)
            pool.partition_all_reduce(sc[:, G0:G0 + 2], sc[:, Y_MX:Y_MX + 2], P, RMAX).then_inc(sem("reduced"), 1)
            def low_part(dst, ws, high, n):
                pool.wait_ge(sem("w_high"), n)
                pool.tensor_tensor(dst, ws, high, ALU.subtract).then_inc(sem("w_low"), 1)

            low_part(w1s[1], w1a, w1s[0], 1)
            low_part(w2s[1][:, 0:W2M, :], w2a[:, 0:W2M, :], w2s[0][:, 0:W2M, :], 2)
            low_part(w2s[1][0:C1, W2M, :], w2a[0:C1, W2M, :], w2s[0][0:C1, W2M, :], 3)
            barrier(pool, "pool")
            barrier(pool, "pool")

            def square(g, m, par, n, half):
                rows = chunk_rows(m)
                if m < WEIGHED:
                    pool.wait_ge(sem("weighted"), g * WEIGHED + m + 1)
                else:
                    pool.wait_ge(sem("relu"), n + 1)
                wait(pool, "low", n - HB + 1)
                other = hc[0:rows, m % HB, :] if m < WEIGHED else hr[0:rows, m % HB, :]
                pool.tensor_tensor(hs[0:rows, m % HB, :], hr[0:rows, m % HB, :], other, ALU.mult).then_inc(sem("squared"), 1)

            chunks([(square, 0)])(pool)

        @block.scalar
        def _(act):
            def copy(out_, in_):
                return act.activation(out_, in_, ACT.Copy)

            def ident_(out_, in_, scale=1.0, bias=0.0):
                return act.activation(out_, in_, ACT.Identity, scale=scale, bias=bias)

            act.wait_ge(sem("consts"), 48)
            copy(ident_b[:, :], ident[:, :]).then_inc(sem("ident_b"), 1)
            for n in range(EMBED_TURNS):
                _, rows, cols, dst = turns[n]
                act.wait_ge(sem("w_psum"), n + 1)
                copy(dst, ps[0:rows, n % 2, 0:cols]).then_inc(sem("w_turned"), 1)

            def turned_text(t, par, half):
                act.wait_ge(sem("pat_psum"), t + 1)
                wait(act, "z_psum", t - 1)
                copy(patT[:, par, 0:384], ps[:, 2 * par, 0:384]).then_inc(sem("patT_a"), 1)

            def gelu(t, par, half):
                act.wait_ge(sem("z_psum"), t + 1)
                wait(act, "h_out", t - 1)
                for m in range(2):
                    last = act.activation(zT[:, par, m, :], ps[0:96, 6 + par, m * P:(m + 1) * P], ACT.Gelu, bias=biases[0:96, m:m + 1])
                last.then_inc(sem("zT"), 1)

            act.wait_ge(sem("bias_b1"), 16)
            pipeline(act, [(turned_text, 0), (gelu, 1)], 16)

            def by_patch(q, c):
                act.wait_ge(sem(f"ximg{q % 2}"), 48 * (q // 2 + 1))
                if q >= 2:
                    act.wait_ge(sem("pat_psum"), 16 + (q - 1) * GRID)
                copy(xp[:, q % 2, c].rearrange("p (w r v) -> p w r v", w=GRID, v=PATCH),
                     ximg[:, q % 2, c].rearrange("p (r w v) -> p w r v", w=GRID, v=PATCH)).then_inc(sem("by_patch_a"), 1)

            by_patch(0, 0)
            for q in range(4):
                if q < 3:
                    by_patch(q + 1, 0)
                for wp in range(GRID):
                    n = 16 + q * GRID + wp
                    act.wait_ge(sem("pat_psum"), n + 1)
                    act.wait_ge(sem("h_out"), n - 1)
                    copy(patT[:, n % 2, 0:288], ps[:, 2 * (n % 2), 0:288]).then_inc(sem("patT_a"), 1)
            barrier(act, "act")
            act.wait_ge(sem("ln_var"), 1)
            act.activation(rs[:, 1, 0:16], rs[:, 0, 0:16], ACT.Sqrt).then_inc(sem("ln_sqrt"), 1)

            def twice(g, par, half):
                act.wait_ge(sem("xn"), g + 1)
                copy(xn[:, par, :, C:2 * P], xn[:, par, :, P:C]).then_inc(sem("xn_twice"), 1)

            def x_high(g, par, half):
                act.wait_ge(sem("x_psum"), g + 1)
                wait(act, "v_psum", (g - 1) * 2)
                act.activation(xT[:, par, 0:3:2, :], ps[:, 0:2, 0:272], ACT.Copy, scale=X_UNIT).then_inc(sem("x_high"), 1)

            def evac_qk(g, par, half):
                act.wait_ge(sem("qk_psum"), g + 1)
                cols = bass.ds(g * 272, 272)
                for j in range(3):
                    last = ident_(yqk[:, j, cols], ps[:, 2 + j, 0:272], scale=wscale[:, j:j + 1], bias=biases[:, 2 + j:3 + j])
                last.then_inc(sem("qk_stored"), 1)

            def more_roots(g, par, half):
                if isinstance(g, int) and g == 3:
                    act.wait_ge(sem("ln_var"), 2)
                    act.activation(rs[:, 1, 16:B], rs[:, 0, 16:B], ACT.Sqrt).then_inc(sem("ln_sqrt"), 1)

            pipeline(act, [(twice, 0), (x_high, 0), (evac_qk, 1), (more_roots, 0)], 16)
            barrier(act, "act")
            def to_halves(c, par, half):
                wait(act, "qk_chunk", c - 1)
                b8 = bass.ds(c * 8, 8)
                for k, (q, kk, _, rows, krows) in enumerate(QKPARTS):
                    t = qt[:, par, k]
                    for dst, src, r, scale in ((t[rows, :, 0:NQ], q[rows, b8, 0:NQ], rows, Q_EV),
                                               (t[rows, :, NQ:2 * NQ], q[rows, b8, 0:NQ], rows, Q_OD),
                                               (t[rows, :, 2 * NQ:2 * NQ + NL], q[rows, b8, NQ:N], rows, Q_INV),
                                               (t[krows, :, 2 * NQ + NL:QTW], kk[krows, b8, :], krows, Q_INV)):
                        last = ident_(dst, src, scale=sc[r, scale:scale + 1], bias=sc[r, T2:T2 + 1])
                last.then_inc(sem("q_added"), 1)

            pipeline(act, [(to_halves, 0)], 8)
            act.wait_ge(sem("qk_chunk"), 8)
            for n in range(2):
                bs = slice(32 * n, 32 * n + 32)
                ident_(vt[:, bs, :], yv[:, bs, :], scale=s1(Q_INV, N), bias=s1(T2, N)).then_inc(sem("v_added"), 1)
            barrier(act, "act")
            ident_(rmq[:, :, :], rowmax[:, :, :], scale=s1(A_KK), bias=s1(A_M16)).then_inc(sem("rmq"), 1)

            def squares(g, par, half):
                act.wait_ge(sem("rem"), g + 1)
                act.activation(sq[par], sq[par], ACT.Square, bias=s1(A_BH)).then_inc(sem("sq"), 1)

            def signs(g, par, half):
                act.wait_ge(sem("excess"), g + 1)
                act.activation(top[par], top[par], ACT.Sign).then_inc(sem("top"), 1)

            def powers(g, par, half):
                act.wait_ge(sem("quot"), g + 1)
                wait(act, "w", g - 1)
                ident_(PW[par], Qq[par], scale=-128.0, bias=s1(A_PB)).then_inc(sem("power"), 1)

            def exponent(g, par, half):
                act.wait_ge(sem("log2"), g + 1)
                wait(act, "pbits", g - 1)
                ident_(yb[par], L[par].bitcast(I32), scale=2.0 ** -23, bias=s1(A_CB)).then_inc(sem("exponent"), 1)

            def evac_pt(g, par, half):
                act.wait_ge(sem("pt_psum"), g + 1)
                wait(act, "o_summed", g - 1)
                copy(PT[par], pPT).then_inc(sem("PT"), 1)

            def evac_o(g, par, half):
                act.wait_ge(sem("o_summed"), g + 1)
                b = bass.ds(g * 2, 2)
                copy(oT[0].rearrange("p (b n) -> p b n", n=N)[:, b, :], pO[par][:, :, 0, :])
                copy(oT[1].rearrange("p (b n) -> p b n", n=N)[:, b, :], pO[par][0:C1, :, 1, :]).then_inc(sem("o_out"), 1)

            pipeline(act, [(powers, 0), (squares, 0), (evac_pt, 3), (exponent, 1), (signs, 1), (evac_o, 4)], 32)
            barrier(act, "act")
            act.wait_ge(sem("o_scalars"), 1)
            ident_(oT[0], oT[0], scale=s1(O_SC), bias=s1(T2)).then_inc(sem("o_added"), 1)
            ident_(oT[1], oT[1], scale=s1(O_SC, C1), bias=s1(T2, C1)).then_inc(sem("o_added"), 1)
            act.wait_ge(sem("w_unit"), 1)
            act.wait_ge(sem("ffn_w"), 16 * 33)
            for ws, high, s_ in ((w1a, w1s[0], W_S1), (w2a[:, 0:W2M, :], w2s[0][:, 0:W2M, :], W_S2),
                                 (w2a[0:C1, W2M, :], w2s[0][0:C1, W2M, :], W_S2)):
                chain(act, "scalar_step", ident_(ws, ws, scale=s1(s_, ws.shape[0])))
                copy(high, ws).then_inc(sem("w_high"), 1)
            act.wait_ge(sem("ln2_var"), 1)
            act.activation(rs2[:, 1, :], rs2[:, 0, :], ACT.Sqrt).then_inc(sem("ln2_sqrt"), 1)
            act.wait_ge(sem("xn2"), 1)
            copy(xn2[:, :, C:2 * P], xn2[:, :, P:C])
            barrier(act, "act")
            act.wait_ge(sem("rw_psum"), 1)
            chain(act, "scalar_step", ident_(rwT, ps[:, 5, 0:2 * E].rearrange("p (k e) -> p k e", k=2), scale=s1(W_S3)))
            copy(rws[0], rwT).then_inc(sem("rw_high"), 1)
            for i in range(TT // 2):
                act.wait_ge(sem("x2_psum"), i + 1)
                src = ps[:, i % 2, :].rearrange("p (k i t) -> p k i t", k=2, i=2)
                act.activation(XS[:, 0:3:2, 2 * P * i:2 * P * (i + 1)].rearrange("p k (i t) -> p k i t", i=2), src,
                               ACT.Copy, scale=X_UNIT).then_inc(sem("X_high"), 1)
            act.wait_ge(sem("routed"), TT // 2)
            act.activation(scr[0], ps[:, 2, 0:TT * E].rearrange("p (i e) -> p i e", e=E), ACT.Sigmoid, scale=s1(W_RU)).then_inc(sem("sigmoid"), 1)
            act.wait_ge(sem("ffn_c"), 32)
            copy(sel_b, sel_w).then_inc(sem("sel_b"), 1)
            for q in range(5):
                act.wait_ge(sem("ct_psum"), q + 1)
                n = min(8, TT - 8 * q) * P
                copy(CT[:, 1024 * q:1024 * q + n], ps[0:32, 3 + q % 2, 0:n // 2].bitcast(BF16)).then_inc(sem("CT"), 1)
            barrier(act, "act")

            def relu(g, m, par, n, half):
                rows = chunk_rows(m)
                act.wait_ge(sem("h_psum"), n + 1)
                wait(act, "squared", n - HB + 1)
                act.activation(hr[0:rows, m % HB, :], ps[0:rows, m % 2, 0:256], ACT.Relu, scale=H_UNIT).then_inc(sem("relu"), 1)

            def high(g, m, par, n, half):
                rows = chunk_rows(m)
                act.wait_ge(sem("squared"), n + 1)
                wait(act, "h_used", n - HB + 1)
                copy(hh[0][0:rows, m % HB, :], hs[0:rows, m % HB, :]).then_inc(sem("high"), 1)

            chunks([(relu, 0), (high, 3)])(act)

        @block.vector
        def _(dve):
            def ch(ins):
                chain(dve, "vector_step", ins)

            ts = dve.tensor_scalar
            tt = dve.tensor_tensor
            dve.wait_ge(sem("wq_rows"), 16 * 16)
            mxw, mnw, nzw, inw = (wtmp[:, k, 0:8] for k in range(4))
            ch(dve.memset(wtmp[:, 0:6, :], 0.0))
            ch(dve.memset(wscale, 1.0))
            for j, (m, _) in enumerate(WJ):
                dve.tensor_reduce(mxw[0:m, j:j + 1], wq_rows[0:m, j, :], X, ALU.max)
                last = dve.tensor_reduce(mnw[0:m, j:j + 1], wq_rows[0:m, j, :], X, ALU.min)
            ch(last)
            ch(ts(mxw, mxw, 0.0, None, ALU.max))
            ch(ts(mnw, mnw, 0.0, None, ALU.min))
            ch(tt(wscale, mxw, mnw, ALU.subtract))
            ch(ts(wscale, wscale, 1.0 / 255.0, EPS_Q, ALU.mult, ALU.max))
            ch(dve.reciprocal(inw, wscale))
            ch(tt(nzw, mnw, inw, ALU.mult))
            ch(ts(nzw, nzw, MAGIC, MAGIC, ALU.add, ALU.subtract))
            ch(ts(nzw, nzw, 255.0, MAGIC, ALU.add, ALU.add))
            for j, (m, _) in enumerate(WJ):
                w = wq_rows[0:m, j, :]
                ch(ts(w, w, inw[0:m, j:j + 1], MAGIC, ALU.mult, ALU.add))
                ch(ts(w, w, nzw[0:m, j:j + 1], MAGIC, ALU.min, ALU.subtract))
            ch(ts(wscale[:, 0:5], wscale[:, 0:5], 1.0 / X_UNIT, None, ALU.mult))
            for j in (3, 4, 5, 6):
                ch(ts(wtmp[0:96, j, 0:96], ident[0:96, 0:96], wscale[0:96, j:j + 1], None, ALU.mult))
            ch(dve.memset(ones[:, :], 1.0))
            wready.append(counts["vector_step"])
            dve.wait_ge(sem("bias_rows"), 16 * 18)
            for wp in range(GRID):
                last = tt(posb[:, wp, :], posb[:, wp, :], brow[0:96, 0, :], ALU.add)
            ch(last)

            def turned_text(t, par, half):
                dve.wait_ge(sem("pat_psum"), t + 1)
                wait(dve, "z_psum", t - 1)
                dve.tensor_copy(patT[:, par, 384:768], ps[:, 2 * par + 1, 0:384]).then_inc(sem("patT_b"), 1)

            def text_h(t, par, half):
                dve.wait_ge(sem("h_out"), t + 1)
                wait(dve, f"t_stored{par}", half * 16)
                tt(tstage[:, par, :], ps[:, 4 + par, 0:C], brow[:, 1, :], ALU.add).then_inc(sem("h_added"), 1)

            pipeline(dve, [(turned_text, 0), (text_h, 2)], 16)

            def by_patch(q):
                dve.wait_ge(sem(f"ximg{q % 2}"), 48 * (q // 2 + 1))
                if q >= 2:
                    dve.wait_ge(sem("pat_psum"), 16 + (q - 1) * GRID)
                for c in (1, 2):
                    last = dve.tensor_copy(xp[:, q % 2, c].rearrange("p (w r v) -> p w r v", w=GRID, v=PATCH),
                                           ximg[:, q % 2, c].rearrange("p (r w v) -> p w r v", w=GRID, v=PATCH))
                last.then_inc(sem("by_patch_b"), 1)

            for n in range(EMBED_TURNS, len(turns)):
                _, rows, cols, dst = turns[n]
                dve.wait_ge(sem("w_psum"), n + 1)
                dve.tensor_copy(dst, ps[0:rows, n % 2, 0:cols]).then_inc(sem("w_turned"), 1)
            by_patch(0)

            def image_h(n):
                q, wp = divmod(n - 16, GRID)
                dve.wait_ge(sem("h_out"), n + 1)
                if q >= 2 and wp == 0:
                    dve.wait_ge(sem(f"h_stored{q % 2}"), 16 * (q // 2))
                tt(hstage[:, q % 2, wp, :], ps[0:96, 4 + n % 2, 0:C], posb[:, wp, :], ALU.add).then_inc(sem("h_added"), 1)

            for q in range(4):
                if q < 3:
                    by_patch(q + 1)
                for wp in range(GRID):
                    n = 16 + q * GRID + wp
                    dve.wait_ge(sem("pat_psum"), n + 1)
                    dve.wait_ge(sem("h_out"), n - 1)
                    dve.tensor_copy(patT[:, n % 2, 288:576], ps[:, 2 * (n % 2) + 1, 0:288]).then_inc(sem("patT_b"), 1)
                    if n > 16:
                        image_h(n - 1)
            image_h(16 + 23)
            barrier(dve, "dve")

            def statistics(first, end):
                for b in range(first, end):
                    if b % 16 == 0:
                        dve.wait_ge(sem(f"hb{b // 16}"), 16)
                    last = dve.bn_stats(bst[:, b, :], hb[:, b, :])
                ch(last)
                for b in range(first, end):
                    last = dve.bn_aggr(mv[:, b, :], bst[:, b, :])
                ch(last)

            def inverse_deviation(var, r, name, times=1):
                ch(ts(r[:, 0, :], var, EPS_LN, None, ALU.add))
                ch(ts(r[:, 2, :], r[:, 0, :], 1.0, None, ALU.mult))
                dve.drain().then_inc(sem(f"{name}_var"), 1)
                dve.wait_ge(sem(f"{name}_sqrt"), times)
                ch(dve.reciprocal(r[:, 2, :], r[:, 1, :]))
                ch(tt(r[:, 2, :], r[:, 2, :], r[:, 0, :], ALU.mult))
                ch(tt(r[:, 1, :], r[:, 1, :], r[:, 2, :], ALU.add))
                ch(ts(r[:, 1, :], r[:, 1, :], 0.5, None, ALU.mult))
                ch(dve.reciprocal(r[:, 2, :], r[:, 1, :]))

            statistics(0, 16)
            inverse_deviation(mv[:, 0:16, 1], rs[:, :, 0:16], "ln")
            dve.drain().then_inc(sem("ln_done"), 1)
            ch(dve.memset(extr, 0.0))

            def more_statistics(g, par, half):
                if isinstance(g, int) and g < 4:
                    statistics(16 + 12 * g, 28 + 12 * g)
                    if g == 3:
                        inverse_deviation(mv[:, 16:B, 1], rs[:, :, 16:B], "ln", 2)
                        dve.drain().then_inc(sem("ln_done"), 1)

            def x_low(g, par, half):
                dve.wait_ge(sem("x_high"), g + 1)
                dve.scalar_tensor_tensor(xT[:, par, 1, :], ps[:, 0, 0:272], X_UNIT, xT[:, par, 0, :], ALU.mult, ALU.subtract)
                dve.scalar_tensor_tensor(xT[C1:P, par, 2, :], ps[C1:P, 1, 0:272], X_UNIT, xT[C1:P, par, 2, :],
                                         ALU.mult, ALU.subtract).then_inc(sem("xT"), 1)

            def scale_v(g, par, half):
                for k in range(2):
                    dve.wait_ge(sem("v_psum"), g * 2 + k + 1)
                    tt(yv[:, bass.ds(g * 4 + 2 * k, 2), :], ps[0:N, 5 + k, 0:2 * C].rearrange("p (b c) -> p b c", b=2),
                       vrow[0:N, :].unsqueeze(1).to_broadcast([N, 2, C]), ALU.mult).then_inc(sem("v_scaled"), 1)

            def extremes_qkv(g, par, half):
                dve.wait_ge(sem("qk_stored"), g + 1)
                dve.wait_ge(sem("v_stored"), g + 1)
                qk, v = yqk[:, :, bass.ds(g * 272, 272)], yv[:, bass.ds(g * 4, 4), :]
                at = bass.ds(g, 1)
                dve.tensor_reduce(extr[:, 0, 0, at], qk, XY, ALU.max)
                dve.tensor_reduce(extr[:, 1, 0, at], qk, XY, ALU.min)
                dve.tensor_reduce(extr[0:N, 0, 1, at], v, XY, ALU.max)
                dve.tensor_reduce(extr[0:N, 1, 1, at], v, XY, ALU.min).then_inc(sem("qkv_extremes"), 1)

            pipeline(dve, [(more_statistics, 0), (x_low, 0), (scale_v, 1), (extremes_qkv, 3)], 16)
            dve.wait_ge(sem("qkv_extremes"), 16)

            def minmax(parts, k):
                ch(dve.memset(sc[:, T0:T1 + 1], 0.0))
                ch(dve.memset(sc[:, k:k + 2], 0.0))
                for rows, part, axis in parts:
                    ch(dve.tensor_reduce(sc[0:rows, T0:T0 + 1], part, axis, ALU.max))
                    ch(dve.tensor_reduce(sc[0:rows, T1:T1 + 1], part, axis, ALU.min, negate=True))
                    ch(tt(sc[0:rows, k:k + 2], sc[0:rows, k:k + 2], sc[0:rows, T0:T0 + 2], ALU.max))

            def scale_of(mx, nmn, s, inv, capm):
                ch(tt(s1(T0), s1(mx), s1(nmn), ALU.add))
                ch(ts(s1(s), s1(T0), 1.0 / 255.0, EPS_Q, ALU.mult, ALU.max))
                ch(dve.reciprocal(s1(inv), s1(s)))
                ch(tt(s1(T0), s1(nmn), s1(inv), ALU.mult))
                ch(ts(s1(T0), s1(T0), MAGIC, MAGIC, ALU.add, ALU.subtract))
                ch(ts(s1(capm), s1(T0), -1.0, 255.0, ALU.mult, ALU.add))

            dve.tensor_reduce(s1(Q_MX), extr[:, 0], XY, ALU.max)
            ch(dve.tensor_reduce(s1(Q_NMN), extr[:, 1], XY, ALU.min, negate=True))
            dve.drain().then_inc(sem("q_minmax"), 1)
            dve.wait_ge(sem("reduced"), 1)
            ch(dve.tensor_copy(sc[:, Q_MX:Q_MX + 2], sc[:, G0:G0 + 2]))
            scale_of(Q_MX, Q_NMN, Q_S, Q_INV, Q_CAPM)
            ch(ts(s1(Q_CAPM), s1(Q_CAPM), H16 + 512.0, None, ALU.add))
            ch(tt(s1(Q_EV), s1(Q_INV), parmask[:, 0:1], ALU.mult))
            ch(tt(s1(Q_OD), s1(Q_INV), parmask[:, 1:2], ALU.mult))
            ch(dve.memset(s1(T2), H16 + 512.0))
            barrier(dve, "dve")
            def to_whole(c, par, half):
                dve.wait_ge(sem("q_added"), c + 1)
                b8 = bass.ds(c * 8, 8)
                for k, (_, _, QK, rows, krows) in enumerate(QKPARTS):
                    t = qt[:, par, k]
                    for dst, src, r in ((QK[rows, b8, 0:2 * NQ], t[rows, :, 0:2 * NQ], rows),
                                        (QK[krows, b8, 3 * NQ:QKW], t[krows, :, 2 * NQ + NL:QTW], krows),
                                        (t[rows, :, 2 * NQ:2 * NQ + NL], t[rows, :, 2 * NQ:2 * NQ + NL], rows)):
                        last = ts(dst, src, sc[r, Q_CAPM:Q_CAPM + 1], H16 + 512.0, ALU.min, ALU.subtract)
                last.then_inc(sem("q_rounded"), 1)

            def extremes(c, par, half):
                for i in range(4):
                    g = c * 4 + i
                    dve.wait_ge(sem("scored"), g + 1)
                    for part, (_, k, s0) in enumerate(PARTS):
                        sv = score_part(4 * (i % 2), part)
                        dve.tensor_reduce(rowmax[:, bass.ds(g, 1), s0:s0 + 2 * k].rearrange("p o (a s) -> p (o a) s", a=2), sv, X, ALU.max)
                        last = dve.tensor_reduce(gmin[:, bass.ds(g * 2 + part, 1)], sv, mybir.AxisListType.XYZ, ALU.min)
                    last.then_inc(sem("extremes"), 1)

            pipeline(dve, [(to_whole, 0), (extremes, 1)], 8)
            dve.wait_ge(sem("v_added"), 2)
            ts(VQ, vt, s1(Q_CAPM, N), H16 + 512.0, ALU.min, ALU.subtract)
            dve.wait_ge(sem("extremes"), 32)
            ch(dve.tensor_reduce(s1(A_MX), rowmax, XY, ALU.max))
            ch(ts(s1(A_MX), s1(A_MX), 0.0, None, ALU.max))
            ch(dve.tensor_reduce(s1(A_NMN), gmin, X, ALU.min, negate=True))
            ch(ts(s1(A_NMN), s1(A_NMN), 0.0, None, ALU.max))
            dve.drain().then_inc(sem("a_minmax"), 1)
            dve.wait_ge(sem("reduced"), 2)
            ch(tt(s1(A_K1), s1(Q_S), s1(Q_S), ALU.mult))
            ch(ts(s1(A_K1), s1(A_K1), HD ** -0.5, None, ALU.mult))
            ch(ts(sc[:, A_MX:A_MX + 2], sc[:, G0:G0 + 2], s1(A_K1), None, ALU.mult))
            scale_of(A_MX, A_NMN, A_S, A_INV, A_CAP)
            ch(ts(s1(A_CAP), s1(A_CAP), H16 + 512.0, None, ALU.add))
            ch(dve.memset(s1(A_M16), H16 + 512.0))
            ch(tt(s1(A_KK), s1(A_K1), s1(A_INV), ALU.mult))
            ch(ts(s1(A_NKK), s1(A_KK), -1.0, None, ALU.mult))
            ch(dve.reciprocal(s1(A_IS), s1(A_S)))

            def floor_(k, tmp):
                ch(ts(s1(tmp), s1(k), MAGIC, MAGIC, ALU.add, ALU.subtract))
                ch(tt(s1(T1), s1(tmp), s1(k), ALU.is_gt))
                ch(tt(s1(tmp), s1(tmp), s1(T1), ALU.subtract))
                ch(ts(s1(T1), s1(k), 4194304.0, None, ALU.is_gt))
                ch(tt(s1(T0), s1(k), s1(tmp), ALU.subtract))
                ch(tt(s1(T0), s1(T0), s1(T1), ALU.mult))
                ch(tt(s1(k), s1(tmp), s1(T0), ALU.add))

            ch(ts(s1(A_A), s1(A_IS), 0.6931, 1e6, ALU.mult, ALU.min))
            ch(ts(s1(A_B), s1(A_A), MAGIC, MAGIC, ALU.add, ALU.subtract))
            ch(tt(s1(T1), s1(A_A), s1(A_B), ALU.is_gt))
            ch(tt(s1(A_A), s1(A_B), s1(T1), ALU.add))
            ch(ts(s1(A_A), s1(A_A), 256.0, None, ALU.min))
            ch(dve.reciprocal(s1(A_IA), s1(A_A)))
            ch(ts(s1(A_NA), s1(A_A), -1.0, None, ALU.mult))
            ch(ts(s1(A_B), s1(A_IS), 0.96963238 / C0, None, ALU.mult))
            floor_(A_B, T2)
            ch(tt(s1(A_C), s1(A_IS), s1(A_IS), ALU.mult))
            ch(ts(s1(A_C), s1(A_C), 1.0 / C0, None, ALU.mult))
            floor_(A_C, T2)
            ch(ts(s1(A_BH), s1(A_A), H16, -H16, ALU.mult, ALU.add))
            ch(ts(s1(T0), s1(A_B), 0.5, None, ALU.mult))
            ch(tt(s1(A_BH), s1(A_BH), s1(T0), ALU.subtract))
            ch(tt(s1(T0), s1(T0), s1(T0), ALU.mult))
            ch(tt(s1(A_K0), s1(A_C), s1(T0), ALU.subtract))
            ch(ts(s1(A_CL), s1(A_A), 30.0, H16, ALU.mult, ALU.add))
            ch(ts(s1(A_SB), s1(A_IA), -H16, H16 - 0.5 + 2.0 ** -10, ALU.mult, ALU.add))
            ch(dve.memset(s1(A_CB), H16 + 1.5 + 2.0 ** -12))
            ch(dve.memset(s1(A_PB), 128.0 * (127.0 + 1.0 + H16) + 64.0))
            barrier(dve, "dve")
            dve.wait_ge(sem("rmq"), 1)
            ch(ts(rmq, rmq, s1(A_CAP), None, ALU.min))
            ch(ts(rmq, rmq, -512.0, None, ALU.add))

            def distances(g, par, half):
                dve.wait_ge(sem("scored"), 32 + g + 1)
                D = Dq[par]
                for part, (_, k, s0) in enumerate(PARTS):
                    m = rmq[:, bass.ds(g, 1), s0:s0 + 2 * k].rearrange("p o (a s) -> p (o a) s", a=2)
                    for a in range(2):
                        last = dve.scalar_tensor_tensor(D[:, s0 + k * a:s0 + k * (a + 1), :], score_part(0, part)[:, a],
                                                        s1(A_NKK), m[:, a, :].unsqueeze(2).to_broadcast([P, k, N]),
                                                        ALU.mult, ALU.add)
                last.then_inc(sem("dist"), 1)

            def clamp(g, par, half):
                dve.wait_ge(sem("dist"), g + 1)
                D = Dq[par]
                ts(D, D, H16, s1(A_CL), ALU.max, ALU.min).then_inc(sem("clamped"), 1)

            def quotients(g, par, half):
                dve.wait_ge(sem("clamped"), g + 1)
                ts(Qq[par], Dq[par], s1(A_IA), s1(A_SB), ALU.mult, ALU.add).then_inc(sem("quot"), 1)

            def remainders(g, par, half):
                dve.wait_ge(sem("quot"), g + 1)
                dve.scalar_tensor_tensor(sq[par], Qq[par], s1(A_NA), Dq[par], ALU.mult, ALU.add).then_inc(sem("rem"), 1)

            def weights(g, par, half):
                dve.wait_ge(sem("sq"), g + 1)
                dve.wait_ge(sem("power"), g + 1)
                wait(dve, "top", g - 1)
                W = wv[par]
                dve.scalar_tensor_tensor(W, sq[par], s1(A_K0), PW[par].rearrange("p s k -> p (s k)").bitcast(BF16).rearrange("p (s k) -> p s k", k=N),
                                         ALU.add, ALU.mult).then_inc(sem("w"), 1)

            def weight_sums(g, par, half):
                dve.wait_ge(sem("w"), g + 1)
                dve.tensor_reduce(S[:, par, 0, :], wv[par], X, ALU.add).then_inc(sem("wsum"), 1)

            def totals(g, par, half):
                dve.wait_ge(sem("wsum"), g + 1)
                ts(S[:, par, 1, :], S[:, par, 0, :], 1.0 / 3.0, None, ALU.mult).then_inc(sem("third"), 1)
                ts(S[:, par, 2, :], S[:, par, 0, :], 2.0 / 3.0, None, ALU.mult)
                dve.wait_ge(sem("third"), g + 1)
                wait(dve, "exponent", g - 1)
                dve.scalar_tensor_tensor(L[par], wv[par], 1.0 / 6.0, S[:, par, 1, :].unsqueeze(2).to_broadcast([P, 2 * SLOTS, N]),
                                         ALU.mult, ALU.add).then_inc(sem("total"), 1)

            def prob_bits(g, par, half):
                dve.wait_ge(sem("exponent"), g + 1)
                wait(dve, "pt_psum", g - 1)
                pi = Pb[par].rearrange("p s k -> p (s k)").bitcast(I16)
                ts(pi, yb[par].rearrange("p s k -> p (s k)"), -128.0, 128.0 * (H16 + 127.0), ALU.mult, ALU.add).then_inc(sem("pbits"), 1)

            def mask(g, par, half):
                dve.wait_ge(sem("pbits"), g + 1)
                ts(Pb[par], Pb[par], 384.0, 384.0, ALU.add, ALU.subtract).then_inc(sem("masked"), 1)

            def probabilities(g, par, half):
                dve.wait_ge(sem("masked"), g + 1)
                dve.wait_ge(sem("top"), g + 1)
                tt(Pb[par], Pb[par], top[par], ALU.max).then_inc(sem("probs"), 1)

            pipeline(dve, [(distances, 0), (clamp, 0), (quotients, 0), (remainders, 0), (weights, 1), (prob_bits, 2),
                           (weight_sums, 1), (mask, 2), (totals, 1), (probabilities, 2)], 32)
            barrier(dve, "dve")
            minmax([(P, oT[0], X), (C1, oT[1], X)], O_MX)
            dve.drain().then_inc(sem("o_minmax"), 1)
            dve.wait_ge(sem("reduced"), 3)
            ch(ts(sc[:, O_MX:O_MX + 2], sc[:, G0:G0 + 2], s1(Q_S), None, ALU.mult))
            scale_of(O_MX, O_NMN, O_S, O_INV, O_CAPM)
            ch(ts(s1(O_CAPM), s1(O_CAPM), MAGIC, None, ALU.add))
            ch(tt(s1(O_SC), s1(Q_S), s1(O_INV), ALU.mult))
            ch(dve.memset(s1(T2), MAGIC))
            ch(ts(prow, prow, s1(O_S), None, ALU.mult))
            dve.drain().then_inc(sem("o_scalars"), 1)
            dve.wait_ge(sem("ffn_w"), 16 * 33)
            ch(dve.memset(s1(W_M3), 0.0))
            dve.tensor_reduce(s1(W_M3, E), rw_rows, X, ALU.max, apply_absolute_value=True)
            dve.tensor_reduce(s1(W_M1), w1a, X, ALU.max, apply_absolute_value=True)
            dve.tensor_reduce(s1(W_M2), w2a[:, 0:W2M, :], XY, ALU.max, apply_absolute_value=True)
            ch(dve.tensor_reduce(s1(T0, C1), w2a[0:C1, W2M, :], X, ALU.max, apply_absolute_value=True))
            ch(tt(s1(W_M2, C1), s1(W_M2, C1), s1(T0, C1), ALU.max))
            dve.drain().then_inc(sem("w_max"), 1)
            dve.wait_ge(sem("o_added"), 2)
            ts(oq[0], oT[0], s1(O_CAPM), MAGIC, ALU.min, ALU.subtract)
            ts(oq[1], oT[1], s1(O_CAPM, C1), MAGIC, ALU.min, ALU.subtract).then_inc(sem("oq"), 1)
            for i in range(TT // 2):
                dve.wait_ge(sem("y2_psum"), i + 1)
                tt(y2[:, 2 * i:2 * i + 2, :], ps[:, i % 4, 0:2 * C].rearrange("p (j c) -> p j c", j=2),
                   prow.unsqueeze(1).to_broadcast([P, 2, C]), ALU.mult).then_inc(sem("y2_a"), 1)
            dve.wait_ge(sem("w_reduced"), 1)
            ch(ts(sc[:, W_E1:W_E3 + 1], sc[:, G2:G4 + 1], 2.0 ** -25, None, ALU.max))
            ch(ts(sc[:, W_E1:W_E3 + 1].bitcast(I32), sc[:, W_E1:W_E3 + 1].bitcast(I32), 0x7F800000, None, ALU.bitwise_and))
            ch(dve.reciprocal(sc[:, W_S1:W_S3 + 1], sc[:, W_E1:W_E3 + 1]))
            ch(ts(sc[:, W_S1:W_S3 + 1], sc[:, W_S1:W_S3 + 1], 2.0 ** 14, None, ALU.mult))
            ch(ts(s1(W_U), s1(W_E1), s1(W_E1), 2.0 ** -14 / (X_UNIT * 2.0 ** 14 * H_UNIT) ** 2, ALU.mult, ALU.mult))
            ch(tt(s1(W_U), s1(W_U), s1(W_E2), ALU.mult))
            ch(ts(s1(W_RU), s1(W_E3), 2.0 ** -14 / X_UNIT, None, ALU.mult))
            dve.drain().then_inc(sem("w_unit"), 1)
            dve.wait_ge(sem("y2"), TT // 2)
            minmax([(P, y2, XY)], Y_MX)
            dve.drain().then_inc(sem("y2_minmax"), 1)
            dve.wait_ge(sem("reduced"), 4)
            ch(dve.tensor_copy(sc[:, Y_MX:Y_MX + 2], sc[:, G0:G0 + 2]))
            scale_of(Y_MX, Y_NMN, Y_S, Y_INV, Y_CAPM)
            ch(ts(s1(Y_CAPM), s1(Y_CAPM), MAGIC, None, ALU.add))
            ch(ts(y2, y2, s1(Y_INV), MAGIC, ALU.mult, ALU.add))
            ch(ts(y2, y2, s1(Y_CAPM), MAGIC, ALU.min, ALU.subtract))
            dve.wait_ge(sem("hf"), 16)
            ch(dve.scalar_tensor_tensor(hf, y2, s1(Y_S), hf, ALU.mult, ALU.add))
            for i in range(TT):
                last = dve.bn_stats(bst2[:, i, :], hf[:, i, :])
            ch(last)
            for i in range(TT):
                last = dve.bn_aggr(mv2[:, i, :], bst2[:, i, :])
            ch(last)
            inverse_deviation(mv2[:, :, 1], rs2, "ln2")
            for i in range(TT):
                last = ts(xn2[:, i, 0:C], hf[:, i, :], mv2[:, i, 0:1], rs2[:, 2, i:i + 1], ALU.subtract, ALU.mult)
            ch(last)
            dve.drain().then_inc(sem("xn2"), 1)
            barrier(dve, "dve")
            dve.wait_ge(sem("rw_high"), 1)
            tt(rws[1], rwT, rws[0], ALU.subtract).then_inc(sem("rw_low"), 1)
            for i in range(TT // 2):
                dve.wait_ge(sem("X_high"), i + 1)
                src = ps[:, i % 2, :].rearrange("p (k t) -> p k t", k=2)
                t = slice(2 * P * i, 2 * P * (i + 1))
                dve.scalar_tensor_tensor(XS[:, 1, t], src[:, 0], X_UNIT, XS[:, 0, t], ALU.mult, ALU.subtract)
                dve.scalar_tensor_tensor(XS[C1:P, 2, t], src[C1:P, 1], X_UNIT, XS[C1:P, 2, t], ALU.mult, ALU.subtract).then_inc(sem("X"), 1)
            dve.wait_ge(sem("sigmoid"), 1)
            dve.wait_ge(sem("ffn_w"), 16 * 33)
            dve.wait_ge(sem("ffn_c"), 32)
            scores, biased, rank, comb = scr
            ch(tt(biased, scores, bbrow.unsqueeze(1).to_broadcast([P, TT, E]), ALU.add))
            mine = biased.unsqueeze(3).to_broadcast([P, TT, E, E])
            other = biased.unsqueeze(2).to_broadcast([P, TT, E, E])
            ch(tt(cmp_a, other, mine, ALU.is_equal))
            ch(tt(cmp_a.rearrange("p i e f -> p i (e f)"), cmp_a.rearrange("p i e f -> p i (e f)"),
                  lower.unsqueeze(1).to_broadcast([P, TT, E * E]), ALU.mult))
            ch(tt(cmp_b, other, mine, ALU.is_gt))
            ch(tt(cmp_a, cmp_a, cmp_b, ALU.add))
            ch(dve.tensor_reduce(rank, cmp_a, X, ALU.add))
            ch(dve.scalar_tensor_tensor(comb, rank, 1.5, scores, ALU.is_lt, ALU.mult))
            ch(dve.tensor_reduce(csum[:, 0, :], comb, X, ALU.add))
            ch(ts(csum[:, 0, :], csum[:, 0, :], 1e-20, None, ALU.add))
            ch(dve.reciprocal(csum[:, 1, :], csum[:, 0, :]))
            ch(tt(comb, comb, csum[:, 1, :].unsqueeze(2).to_broadcast([P, TT, E]), ALU.mult))
            ch(dve.memset(C3, 0.0))
            for k in range(3):
                ch(dve.tensor_copy(C3[:, :, E * k:E * (k + 1)], comb))
                ch(tt(comb, comb, C3[:, :, E * k:E * (k + 1)], ALU.subtract))
            ch(dve.memset(C3[:, :, 24:25], 1.0))
            dve.drain().then_inc(sem("C3"), 1)
            barrier(dve, "dve")

            def weigh(g, m, par, n, half):
                if m >= WEIGHED:
                    return
                first, last_e = m * P // C, (m * P + P - 1) // C
                dve.wait_ge(sem("relu"), n + 1)
                dve.wait_ge(sem("c_psum"), g * E + last_e + 1)
                wait(dve, "squared", n - HB + 1)
                for e in range(first, last_e + 1):
                    rows = slice(max(e * C - m * P, 0), min((e + 1) * C - m * P, P))
                    last = tt(hc[rows, m % HB, :], hr[rows, m % HB, :], ps[rows, 2 + e % 2, 0:256], ALU.mult)
                last.then_inc(sem("weighted"), 1)

            def low(g, m, par, n, half):
                rows = chunk_rows(m)
                dve.wait_ge(sem("high"), n + 1)
                wait(dve, "h_used", n - HB + 1)
                tt(hh[1][0:rows, m % HB, :], hs[0:rows, m % HB, :], hh[0][0:rows, m % HB, :], ALU.subtract).then_inc(sem("low"), 1)

            def add_h(g, m, par, n, half):
                if m < W2M:
                    return
                dve.wait_ge(sem("h_used"), n + 1)
                wait(dve, f"stored{par}", half * 16)
                dve.scalar_tensor_tensor(ost[:, par], ps[:, 4 + 2 * par:6 + 2 * par, 0:C], s1(W_U), hf[:, bass.ds(g * 2, 2), :],
                                         ALU.mult, ALU.add).then_inc(sem("out_ready"), 1)

            chunks([(weigh, 0), (low, 3), (add_h, 8)])(dve)

        @block.tensor
        def _(pe):
            def mm(o, a, b, start=True, stop=True):
                return pe.matmul(o, a, b, start=start, stop=stop, skip_group_check=True)

            pe.wait_ge(sem("consts"), 48)
            pe.wait_ge(sem("w_rows"), 48)

            def turn_weights(first, end):
                for n in range(first, end):
                    pieces, rows, cols, dst = turns[n]
                    wait(pe, "w_turned", n - 1)
                    for src, m, at in pieces:
                        if src is None:
                            last = mm(ps[:, n % 2, 0:96], ones[0:96, :], wtmp[0:96, m, 0:96])
                        else:
                            last = pe.transpose(ps[0:rows, n % 2, at:at + m], src, ident[0:m, 0:m])
                    last.then_inc(sem("w_psum"), 1)
                pe.wait_ge(sem("w_turned"), end)

            turn_weights(0, EMBED_TURNS)

            def turn_text(t, par, half):
                pe.wait_ge(sem(f"emb{par}"), half * 16 + 16)
                wait(pe, "patT_a", t - 1)
                wait(pe, "patT_b", t - 1)
                for k in range(KC):
                    last = pe.transpose(ps[:, 2 * par + k // 3, (k % 3) * P:(k % 3) * P + P], emb[:, par, k * P:(k + 1) * P], ident[:, :])
                last.then_inc(sem("pat_psum"), 1)

            def times_w1(t, par, half):
                pe.wait_ge(sem("patT_a"), t + 1)
                pe.wait_ge(sem("patT_b"), t + 1)
                wait(pe, "zT", t - 1)
                for m in range(2):
                    for k in range(KC):
                        last = mm(ps[0:96, 6 + par, m * P:(m + 1) * P], w1T[:, k, m * 96:(m + 1) * 96], patT[:, par, k * P:(k + 1) * P], k == 0, k == KC - 1)
                last.then_inc(sem("z_psum"), 1)

            def times_w2(t, par, half):
                pe.wait_ge(sem("zT"), t + 1)
                wait(pe, "h_added", t - 1)
                for m in range(2):
                    last = mm(ps[:, 4 + par, 0:C], zT[:, par, m, :], w2T[:, m, :], m == 0, m == 1)
                last.then_inc(sem("h_out"), 1)

            pipeline(pe, [(turn_text, 0), (times_w1, 1), (times_w2, 2)], 16)

            pe.wait_ge(sem("patT_a"), 16)
            pe.wait_ge(sem("patT_b"), 16)
            pe.wait_ge(sem("vector_step"), wready[0])
            turn_weights(EMBED_TURNS, len(turns))

            def times_w(n):
                pe.wait_ge(sem("patT_a"), n + 1)
                pe.wait_ge(sem("patT_b"), n + 1)
                pe.wait_ge(sem("h_added"), n - 1)
                for k in range(KC):
                    last = mm(ps[0:96, 4 + n % 2, 0:C], patT[:, n % 2, k * 96:(k + 1) * 96], tokT[:, k, :], k == 0, k == KC - 1)
                last.then_inc(sem("h_out"), 1)

            for q in range(4):
                pe.wait_ge(sem("by_patch_a"), q + 1)
                pe.wait_ge(sem("by_patch_b"), q + 1)
                for wp in range(GRID):
                    n = 16 + q * GRID + wp
                    pe.wait_ge(sem("patT_a"), n - 1)
                    pe.wait_ge(sem("patT_b"), n - 1)
                    for k in range(KC):
                        c, half = k // 2, k % 2
                        src = xp[:, q % 2, c, (2 * wp + half) * P:(2 * wp + half + 1) * P]
                        last = pe.transpose(ps[:, 2 * (n % 2) + k // 3, (k % 3) * 96:(k % 3) * 96 + 96], src, ident[0:96, 0:96])
                    last.then_inc(sem("pat_psum"), 1)
                    if n > 16:
                        times_w(n - 1)
            times_w(16 + 23)
            barrier(pe, "pe")

            def turn_x(g, par, half):
                pe.wait_ge(sem("xn_twice"), g + 1)
                wait(pe, "xT", g)
                for k in range(4):
                    pe.transpose(ps[:, 0, k * N:(k + 1) * N], xn[:, par, k, 0:P], ident[0:N, 0:N])
                    last = pe.transpose(ps[:, 1, k * N:(k + 1) * N], xn[:, par, k, P:2 * P], ident[0:N, 0:N])
                last.then_inc(sem("x_psum"), 1)

            def qkv(g, par, half):
                pe.wait_ge(sem("xT"), g + 1)
                wait(pe, "qk_stored", g)
                hi, lo, both = (xT[:, par, k, :] for k in range(3))
                for j in range(3):
                    o, u = ps[:, 2 + j, 0:272], slice(j * P, (j + 1) * P)
                    mm(o, wqT0[:, u], hi, True, False)
                    mm(o, wqT0[:, u], lo, False, False)
                    last = mm(o, wqT1[:, u], both, False, True)
                last.then_inc(sem("qk_psum"), 1)
                for k in range(2):
                    wait(pe, "v_scaled", g * 2 + k - 1)
                    for b in range(2):
                        t = slice((2 * k + b) * N, (2 * k + b + 1) * N)
                        o = ps[0:N, 5 + k, b * C:(b + 1) * C]
                        mm(o, hi[:, t], wqT0[:, 2 * C:3 * C], True, False)
                        mm(o, lo[:, t], wqT0[:, 2 * C:3 * C], False, False)
                        last = mm(o, both[:, t], wqT1[:, 2 * C:3 * C], False, True)
                    last.then_inc(sem("v_psum"), 1)

            pipeline(pe, [(turn_x, 0), (qkv, 1)], 16)
            barrier(pe, "pe")

            def scores(g, base, par, at):
                for b in range(2):
                    for j in range(PAIRS):
                        st = st0 if j < 4 else st1
                        rows = slice(32 * (j % 4), 32 * (j % 4) + 32)
                        bank, k, _ = score_slot(b, j)
                        for a in range(2):
                            mm(ps[NQ * a:NQ * (a + 1), base + bank, k * N:(k + 1) * N],
                               st[rows, par, at + b, NQ * a:NQ * (a + 1)], st[rows, par, at + b, 3 * NQ:QKW])
                for b in range(2):
                    bank, k, _ = score_slot(b, PAIRS)
                    for a in range(2):
                        o = ps[NQ * a:NQ * (a + 1), base + bank, k * N:(k + 1) * N]
                        mm(o, st0[:, par, at + b, 2 * NQ:3 * NQ], st0[:, par, at + b, 3 * NQ:QKW], True, False)
                        last = mm(o, st1[:, par, at + b, 2 * NQ:3 * NQ], st1[:, par, at + b, 3 * NQ:QKW], False, True)
                last.then_inc(sem("scored"), 1)

            def first_scores(g, par, half):
                pe.wait_ge(sem(f"st_qk{par}"), (half + 1) * 48)
                for k in range(2):
                    wait(pe, "extremes", g * 2 + k - 1)
                    scores(g * 2 + k, 4 * k, par, 2 * k)

            def second_scores(g, par, half):
                pe.wait_ge(sem(f"st_qk{par}"), (8 + half + 1) * 48)
                wait(pe, "dist", g)
                scores(g, 0, par, 0)

            pipeline(pe, [(first_scores, 0)], 16)
            barrier(pe, "pe")

            def turn_p(g, par, half):
                pe.wait_ge(sem("probs"), g + 1)
                wait(pe, "PT", g)
                for s in range(2 * SLOTS):
                    last = pe.transpose(pPT[:, s // SLOTS, s % SLOTS, :], Pb[par][:, s, :], ident_b[:, :])
                last.then_inc(sem("pt_psum"), 1)

            def sum_v(g, par, half):
                pe.wait_ge(sem("PT"), g + 1)
                pe.wait_ge(sem("v_spread"), g + 1)
                wait(pe, "o_out", g - 1)
                pt = PT[par].rearrange("p b s q -> p (b s) q")
                for b in range(2):
                    left = pt[:, score_slot(b, PAIRS)[2], :]
                    for j in range(PAIRS):
                        rows = slice(32 * (j % 4), 32 * (j % 4) + 32)
                        main = pt[:, score_slot(b, j)[2], :]
                        o = pO[par][rows, b, j // 4, :]
                        for a in range(2):
                            mm(o[:, 0:NQ], stv[:, par, b, a, 32 * j:32 * j + 32], main[:, NQ * a:NQ * (a + 1)], a == 0, a == 1)
                        for a in range(2):
                            h = 2 * j + a
                            last = mm(o[:, NQ:N], stv[:, par, b, a, 32 * j:32 * j + 32], left[:, NL * h:NL * (h + 1)], a == 0, a == 1)
                last.then_inc(sem("o_summed"), 1)

            pipeline(pe, [(second_scores, 0), (turn_p, 3), (sum_v, 4)], 32)
            barrier(pe, "pe")
            pe.wait_ge(sem("oq"), 1)
            for i in range(TT // 2):
                wait(pe, "y2_a", i - 3)
                for j in range(2):
                    t = slice((2 * i + j) * P, (2 * i + j + 1) * P)
                    o = ps[:, i % 4, j * C:(j + 1) * C]
                    mm(o, oq[0][:, t], wpb0, True, False)
                    last = mm(o, oq[1][:, t], wpb1, False, True)
                last.then_inc(sem("y2_psum"), 1)
            barrier(pe, "pe")
            pe.wait_ge(sem("ffn_w"), 16 * 33)
            pe.transpose(ps[:, 5, 0:E], rw_rows[:, 0:P], ident[0:E, 0:E])
            pe.transpose(ps[:, 5, E:2 * E], rw_rows[:, P:2 * P], ident[0:E, 0:E]).then_inc(sem("rw_psum"), 1)
            def route(i):
                pe.wait_ge(sem("X"), i + 1)
                for j in range(2):
                    o = ps[:, 2, (2 * i + j) * E:(2 * i + j + 1) * E]
                    hi, lo, both = (XS[:, k, (2 * i + j) * P:(2 * i + j + 1) * P] for k in range(3))
                    mm(o, hi, rws[0][:, 0, :], True, False)
                    mm(o, hi, rws[1][:, 0, :], False, False)
                    mm(o, lo, rws[0][:, 0, :], False, False)
                    mm(o, both, rws[0][:, 1, :], False, False)
                    last = mm(o, both, rws[1][:, 1, :], False, True)
                last.then_inc(sem("routed"), 1)

            pe.wait_ge(sem("rw_low"), 1)
            for i in range(TT // 2):
                wait(pe, "X", i - 1)
                for j in range(2):
                    pe.transpose(ps[:, i % 2, j * P:(j + 1) * P], xn2[:, 2 * i + j, 0:P], ident[:, :])
                    last = pe.transpose(ps[:, i % 2, (2 + j) * P:(3 + j) * P], xn2[:, 2 * i + j, P:2 * P], ident[:, :])
                last.then_inc(sem("x2_psum"), 1)
                if i >= 2:
                    route(i - 2)
            route(TT // 2 - 2)
            route(TT // 2 - 1)
            pe.wait_ge(sem("C3"), 1)
            for q in range(5):
                wait(pe, "CT", q - 1)
                for k in range(min(8, TT - 8 * q)):
                    last = pe.transpose(ps[0:32, 3 + q % 2, k * 64:(k + 1) * 64].bitcast(BF16), C3[:, 8 * q + k, :], ident_b[:, :])
                last.then_inc(sem("ct_psum"), 1)
            barrier(pe, "pe")

            def up(g, m, par, n, half):
                rows = chunk_rows(m)
                if m == 0:
                    pe.wait_ge(sem(f"xs{par}"), (half + 1) * 32)
                wait(pe, "relu", n - 1)
                u, v = slice(m * P, m * P + rows), slice(U + m * P, U + m * P + rows)
                o = ps[0:rows, m % 2, 0:256]
                mm(o, w1s[0][:, u], xs[:, par, 0], True, False)
                mm(o, w1s[0][:, u], xs[:, par, 1], False, False)
                mm(o, w1s[1][:, u], xs[:, par, 0], False, False)
                mm(o, w1s[0][:, v], xs[:, par, 2], False, False)
                mm(o, w1s[1][:, v], xs[:, par, 2], False, True).then_inc(sem("h_psum"), 1)

            def weights(g, m, par, n, half):
                for e in range(E):
                    if e * C // P != m:
                        continue
                    if e >= 2:
                        pe.wait_ge(sem("weighted"), g * WEIGHED + ((e - 1) * C - 1) // P + 1)
                    else:
                        wait(pe, "weighted", (g - 1) * WEIGHED + ((e + E - 1) * C - 1) // P + 1)
                    mm(ps[:, 2 + e % 2, 0:256], sel_b[:, e * C:e * C + P], cts[:, par]).then_inc(sem("c_psum"), 1)

            def down(g, m, par, n, half):
                rows = chunk_rows(m)
                if m == 0:
                    wait(pe, "out_ready", g - 1)
                for i in range(2):
                    o = ps[:, 4 + 2 * par + i, 0:C]
                    t = slice(i * P, (i + 1) * P)
                    if i == 0:
                        pe.wait_ge(sem("high"), n + 1)
                    mm(o, hh[0][0:rows, m % HB, t], w2s[0][0:rows, m, :], m == 0, False)
                    mm(o, hh[0][0:rows, m % HB, t], w2s[1][0:rows, m, :], False, False)
                    if i == 0:
                        pe.wait_ge(sem("low"), n + 1)
                    last = mm(o, hh[1][0:rows, m % HB, t], w2s[0][0:rows, m, :], False, m == W2M)
                last.then_inc(sem("h_used"), 1)

            chunks([(up, 0), (weights, 0), (down, 5)])(pe)


_INS = ['x', 'x_txt', 'L0_tok_W', 'L0_tok_b', 'L0_tok_pos', 'L0_txt_tok_embed', 'L0_txt_W1', 'L0_txt_b1', 'L0_txt_W2',
        'L0_txt_b2', 'L0_attn_w_qkv', 'L0_attn_b_qkv', 'L0_attn_w_proj', 'L0_attn_b_proj', 'L0_ffn_w_fc_sh',
        'L0_ffn_w_proj_sh', 'L0_ffn_w1', 'L0_ffn_w2', 'L0_ffn_router_w', 'L0_ffn_balance_bias']


def constants():
    import numpy as np

    p = np.arange(P)
    h = np.arange(16)
    masks = np.zeros((P, 34), np.float32)
    masks[:, 0:16] = (p[:, None] // HD == h) & (h < 8)
    masks[:, 16:32] = (p[:, None] // HD + 8 == h) & (h < H)
    masks[:, 32] = p // HD % 2 == 0
    masks[:, 33] = p // HD % 2 == 1
    u = np.arange(UC * P)
    rows = np.arange(32)
    expert = np.where(rows < 3 * E, rows % E, np.where(rows == 3 * E, E, -1))
    select = (u // C == expert[:, None]).astype(np.float32)
    e = np.arange(E)
    lower = (e[None, :] < e[:, None]).astype(np.float32).reshape(-1)
    return {"ident": np.eye(P, dtype=np.float32), "masks": masks, "select": select, "lower": lower}


def kernel(**inputs):
    import numpy as _np
    import concourse.bacc as _bacc
    from concourse import mybir as _mybir
    from concourse.bass_utils import run_bass_kernel_spmd as _run

    nc = _bacc.Bacc("TRN2", target_bir_lowering=False, num_devices=1)
    arrays, args = {}, []
    for name, a in [(n, inputs[n]) for n in _INS] + list(constants().items()):
        a = _np.ascontiguousarray(a)
        arrays[f"in_{name}_dram"] = a
        args.append(nc.dram_tensor(f"in_{name}_dram", a.shape, _mybir.dt.from_np(a.dtype), kind="ExternalInput").ap())
    args.append(nc.dram_tensor("out_0_dram", (B, N, C), _mybir.dt.float32, kind="ExternalOutput").ap())
    program(nc, *args)
    r = _run(nc, [arrays], core_ids=[0])
    return r.results[0]["out_0_dram"]
```
